# Optimizing a Trainium2 kernel written in Bass

```python
import numpy as np
import jax
import jax.numpy as jnp

def _softmax(x, axis=-1):
    return jax.nn.softmax(x, axis=axis)

def _gelu(x):
    return jax.nn.gelu(x, approximate=True)

def _silu(x):
    return jax.nn.silu(x)

def _sigmoid(x):
    return jax.nn.sigmoid(x)

def _layernorm(x, axis=-1, eps=1e-05):
    m = jnp.mean(x, axis=axis, keepdims=True)
    v = jnp.var(x, axis=axis, keepdims=True)
    return (x - m) / jnp.sqrt(v + eps)

def _scatter_add(tgt, idx, src, axis=0):
    return tgt.at[idx].add(src)

def _segment_sum(src, seg, n):
    return jax.ops.segment_sum(src, seg, n)
kernel_name = 'mk_sandwich_d2_jaxref_r8_50a198'

def setup_inputs(seed: int=0):
    np.random.seed(seed)
    _w = jnp.asarray

    def _L0_attn_setup():
        import jax, jax.numpy as jnp
        import numpy as np
        N_HEADS = 16

        def _rope(t, sin, cos):
            t_rot = jnp.stack([-t[..., 1::2], t[..., ::2]], axis=-1).reshape(t.shape)
            return t * cos + t_rot * sin
        key = jax.random.key(seed)
        ks = jax.random.split(key, 5)
        B, S, D = (2, 256, 128)
        scale = 1.0 / np.sqrt(D)
        return {'x': jax.random.normal(ks[0], (B, S, D), dtype=jnp.float32), 'Wq': jax.random.normal(ks[1], (D, D), dtype=jnp.float32) * scale, 'Wk': jax.random.normal(ks[2], (D, D), dtype=jnp.float32) * scale, 'Wv': jax.random.normal(ks[3], (D, D), dtype=jnp.float32) * scale, 'Wo': jax.random.normal(ks[4], (D, D), dtype=jnp.float32) * scale}
    _L0_attn_in = _L0_attn_setup()

    def _L0_ffn_setup():
        import jax, jax.numpy as jnp
        import numpy as np
        DIM = 128
        DEPTH = 2
        HEADS = 8
        DIM_HEAD = 64
        WINDOW = 64
        INNER = HEADS * DIM_HEAD
        HID = int(DIM * 4 * 2 / 3)
        B, N = (2, 1024)
        QK_SCALE = 8.0

        def shift_token(t):
            t1, t2 = jnp.split(t, 2, axis=-1)
            t2 = jnp.pad(t2, ((0, 0), (1, 0), (0, 0)))[:, :-1]
            return jnp.concatenate([t1, t2], axis=-1)

        def l2norm(t):
            return t / jnp.clip(jnp.linalg.norm(t, axis=-1, keepdims=True), 1e-12)

        def rotate_half(x):
            x1, x2 = jnp.split(x, 2, axis=-1)
            return jnp.concatenate([-x2, x1], axis=-1)

        def rotary_xpos(q, k):
            n = q.shape[-2]
            half_idx = jnp.arange(0, DIM_HEAD, 2, dtype=jnp.float32)
            inv_freq = 1.0 / 10000.0 ** (half_idx / DIM_HEAD)
            t = jnp.arange(n, dtype=jnp.float32)
            freqs = t[:, None] * inv_freq[None, :]
            freqs = jnp.concatenate([freqs, freqs], axis=-1)
            base = (half_idx + 0.4 * DIM_HEAD) / (1.4 * DIM_HEAD)
            power = (t - n // 2) / float(WINDOW // 2)
            scale = base[None, :] ** power[:, None]
            scale = jnp.concatenate([scale, scale], axis=-1)
            cos, sin = (jnp.cos(freqs), jnp.sin(freqs))
            q = q * cos * scale + rotate_half(q) * sin * scale
            k = k * cos / scale + rotate_half(k) * sin / scale
            return (q, k)

        def local_attention(q, k, v):
            b, h, n, d = q.shape
            w = n // WINDOW
            bq = q.reshape(b, h, w, WINDOW, d) * QK_SCALE
            bk = k.reshape(b, h, w, WINDOW, d)
            bv = v.reshape(b, h, w, WINDOW, d)

            def look_around(t):
                p = jnp.pad(t, ((0, 0), (0, 0), (1, 0), (0, 0), (0, 0)))
                return jnp.concatenate([p[:, :, :w], p[:, :, 1:]], axis=3)
            bk, bv = (look_around(bk), look_around(bv))
            bt = jnp.arange(n).reshape(w, WINDOW)
            btp = jnp.pad(bt, ((1, 0), (0, 0)), constant_values=-1)
            btk = jnp.concatenate([btp[:w], btp[1:]], axis=1)
            sim = jnp.einsum('bhwid,bhwjd->bhwij', bq, bk)
            i = bt[:, :, None]
            j = btk[:, None, :]
            mask = (i < j) | (i > j + WINDOW) | (j == -1)
            sim = jnp.where(mask, -jnp.finfo(sim.dtype).max, sim)
            attn = jax.nn.softmax(sim, axis=-1)
            out = jnp.einsum('bhwij,bhwjd->bhwid', attn, bv)
            return out.reshape(b, h, n, d)

        def _layer(x, wqkv, qs, ksc, wo, lg, lb, w1, b1, w2, b2):
            b, n, _ = x.shape
            h = shift_token(x)
            qkv = h @ wqkv
            q, k, v = jnp.split(qkv, 3, axis=-1)
            to_heads = lambda t: t.reshape(b, n, HEADS, DIM_HEAD).transpose(0, 2, 1, 3)
            q, k, v = (to_heads(q), to_heads(k), to_heads(v))
            q = l2norm(q) * qs
            k = l2norm(k) * ksc
            q, k = rotary_xpos(q, k)
            o = local_attention(q, k, v)
            o = o.transpose(0, 2, 1, 3).reshape(b, n, INNER)
            x = x + o @ wo
            h = shift_token(x)
            mu = h.mean(-1, keepdims=True)
            var = h.var(-1, keepdims=True)
            h = (h - mu) / jnp.sqrt(var + 1e-05) * lg + lb
            h = h @ w1 + b1
            a, g = jnp.split(h, 2, axis=-1)
            h = a * jax.nn.gelu(g, approximate=False)
            x = x + h @ w2 + b2
            return x
        key = jax.random.key(seed)
        ks = jax.random.split(key, 6)
        return {'x': jax.random.normal(ks[0], (B, N, DIM), jnp.float32), 'wqkv': jax.random.normal(ks[1], (DEPTH, DIM, 3 * INNER), jnp.float32) * 0.02, 'q_scale': jnp.ones((DEPTH, DIM_HEAD), jnp.float32), 'k_scale': jnp.ones((DEPTH, DIM_HEAD), jnp.float32), 'wo': jax.random.normal(ks[2], (DEPTH, INNER, DIM), jnp.float32) * 0.02, 'ln_g': jnp.ones((DEPTH, DIM), jnp.float32), 'ln_b': jnp.zeros((DEPTH, DIM), jnp.float32), 'w1': jax.random.normal(ks[3], (DEPTH, DIM, 2 * HID), jnp.float32) * 0.02, 'b1': jnp.zeros((DEPTH, 2 * HID), jnp.float32), 'w2': jax.random.normal(ks[4], (DEPTH, HID, DIM), jnp.float32) * 0.02, 'b2': jnp.zeros((DEPTH, DIM), jnp.float32)}
    _L0_ffn_in = _L0_ffn_setup()

    def _L1_attn_setup():
        import jax, jax.numpy as jnp
        import numpy as np
        D_CONV = 4
        DT_RANK = 64
        D_STATE = 16

        def silu(v):
            return v * jax.nn.sigmoid(v)
        key = jax.random.key(seed)
        ks = jax.random.split(key, 10)
        B, L, d_model, d_inner = (2, 256, 128, 256)

        def nrm(k, shape, scale):
            return jax.random.normal(k, shape, dtype=jnp.float32) * scale
        A = jnp.tile(jnp.arange(1, D_STATE + 1, dtype=jnp.float32), (d_inner, 1))
        return {'x': nrm(ks[0], (B, L, d_model), 1.0), 'W_in': nrm(ks[1], (d_model, 2 * d_inner), d_model ** (-0.5)), 'conv_w': nrm(ks[2], (d_inner, D_CONV), D_CONV ** (-0.5)), 'conv_b': nrm(ks[3], (d_inner,), 0.02), 'W_x': nrm(ks[4], (d_inner, DT_RANK + 2 * D_STATE), d_inner ** (-0.5)), 'W_dt': nrm(ks[5], (DT_RANK, d_inner), DT_RANK ** (-0.5)), 'b_dt': nrm(ks[6], (d_inner,), 0.02), 'A_log': jnp.log(A), 'D': jnp.ones((d_inner,), dtype=jnp.float32), 'W_out': nrm(ks[7], (d_inner, d_model), d_inner ** (-0.5))}
    _L1_attn_in = _L1_attn_setup()

    def _L1_ffn_setup():
        import jax, jax.numpy as jnp
        import numpy as np
        DIM = 128
        HIDDEN = 384
        SCALE = 1.0 / 127.0

        def _dequant(w_int, dtype):
            return w_int.astype(dtype) * jnp.asarray(SCALE, dtype)
        key = jax.random.key(seed)
        k_x, k_g, k_u, k_d = jax.random.split(key, 4)
        x = jax.random.normal(k_x, (4, 256, DIM), dtype=jnp.float32)
        w_gate = jax.random.randint(k_g, (HIDDEN, DIM), -127, 128, dtype=jnp.int32)
        w_up = jax.random.randint(k_u, (HIDDEN, DIM), -127, 128, dtype=jnp.int32)
        w_down = jax.random.randint(k_d, (DIM, HIDDEN), -127, 128, dtype=jnp.int32)
        return {'x': x, 'w_gate': w_gate, 'w_up': w_up, 'w_down': w_down}
    _L1_ffn_in = _L1_ffn_setup()
    _d = {'L0_attn_x': _L0_attn_in['x'], 'L0_attn_Wq': _L0_attn_in['Wq'], 'L0_attn_Wk': _L0_attn_in['Wk'], 'L0_attn_Wv': _L0_attn_in['Wv'], 'L0_attn_Wo': _L0_attn_in['Wo'], 'L0_ffn_wqkv': _L0_ffn_in['wqkv'], 'L0_ffn_q_scale': _L0_ffn_in['q_scale'], 'L0_ffn_k_scale': _L0_ffn_in['k_scale'], 'L0_ffn_wo': _L0_ffn_in['wo'], 'L0_ffn_ln_g': _L0_ffn_in['ln_g'], 'L0_ffn_ln_b': _L0_ffn_in['ln_b'], 'L0_ffn_w1': _L0_ffn_in['w1'], 'L0_ffn_b1': _L0_ffn_in['b1'], 'L0_ffn_w2': _L0_ffn_in['w2'], 'L0_ffn_b2': _L0_ffn_in['b2'], 'L1_attn_W_in': _L1_attn_in['W_in'], 'L1_attn_conv_w': _L1_attn_in['conv_w'], 'L1_attn_conv_b': _L1_attn_in['conv_b'], 'L1_attn_W_x': _L1_attn_in['W_x'], 'L1_attn_W_dt': _L1_attn_in['W_dt'], 'L1_attn_b_dt': _L1_attn_in['b_dt'], 'L1_attn_A_log': _L1_attn_in['A_log'], 'L1_attn_D': _L1_attn_in['D'], 'L1_attn_W_out': _L1_attn_in['W_out'], 'L1_ffn_w_gate': _L1_ffn_in['w_gate'], 'L1_ffn_w_up': _L1_ffn_in['w_up'], 'L1_ffn_w_down': _L1_ffn_in['w_down']}
    _x0 = _d['L0_attn_x']
    _d['L0_attn_x'] = jax.random.normal(jax.random.fold_in(jax.random.key(seed), 1), (16, 256, 128), dtype=_x0.dtype)
    del _x0
    return _d

def reference(L0_attn_x, L0_attn_Wq, L0_attn_Wk, L0_attn_Wv, L0_attn_Wo, L0_ffn_wqkv, L0_ffn_q_scale, L0_ffn_k_scale, L0_ffn_wo, L0_ffn_ln_g, L0_ffn_ln_b, L0_ffn_w1, L0_ffn_b1, L0_ffn_w2, L0_ffn_b2, L1_attn_W_in, L1_attn_conv_w, L1_attn_conv_b, L1_attn_W_x, L1_attn_W_dt, L1_attn_b_dt, L1_attn_A_log, L1_attn_D, L1_attn_W_out, L1_ffn_w_gate, L1_ffn_w_up, L1_ffn_w_down):

    def _L0_attn_ref(x, Wq, Wk, Wv, Wo):
        import jax, jax.numpy as jnp
        import numpy as np
        N_HEADS = 16

        def _rope(t, sin, cos):
            t_rot = jnp.stack([-t[..., 1::2], t[..., ::2]], axis=-1).reshape(t.shape)
            return t * cos + t_rot * sin
        B, S, D = x.shape
        H = N_HEADS
        dk = D // H
        q = (x @ Wq.T).reshape(B, S, H, dk).transpose(0, 2, 1, 3)
        k = (x @ Wk.T).reshape(B, S, H, dk).transpose(0, 2, 1, 3)
        v = (x @ Wv.T).reshape(B, S, H, dk).transpose(0, 2, 1, 3)
        inv_freq = 1.0 / 10000.0 ** (jnp.arange(0, dk, 2, dtype=jnp.float32) / dk)
        pos = jnp.arange(S, dtype=jnp.float32)
        freqs = pos[:, None] * inv_freq[None, :]
        sin = jnp.repeat(jnp.sin(freqs), 2, axis=-1)
        cos = jnp.repeat(jnp.cos(freqs), 2, axis=-1)
        q = _rope(q, sin, cos)
        k = _rope(k, sin, cos)
        scores = jnp.einsum('bhqd,bhkd->bhqk', q, k) / jnp.sqrt(jnp.float32(dk))
        slopes = 2.0 ** (-8.0 * jnp.arange(H, dtype=jnp.float32) / H)
        rel = -jnp.abs(pos[:, None] - pos[None, :])
        scores = scores + slopes[None, :, None, None] * rel[None, None]
        attn = jax.nn.softmax(scores, axis=-1)
        out = jnp.einsum('bhqk,bhkd->bhqd', attn, v)
        out = out.transpose(0, 2, 1, 3).reshape(B, S, D)
        return out @ Wo.T

    def _L0_ffn_ref(x, wqkv, q_scale, k_scale, wo, ln_g, ln_b, w1, b1, w2, b2):
        import jax, jax.numpy as jnp
        import numpy as np
        DIM = 128
        DEPTH = 2
        HEADS = 8
        DIM_HEAD = 64
        WINDOW = 64
        INNER = HEADS * DIM_HEAD
        HID = int(DIM * 4 * 2 / 3)
        B, N = (2, 1024)
        QK_SCALE = 8.0

        def shift_token(t):
            t1, t2 = jnp.split(t, 2, axis=-1)
            t2 = jnp.pad(t2, ((0, 0), (1, 0), (0, 0)))[:, :-1]
            return jnp.concatenate([t1, t2], axis=-1)

        def l2norm(t):
            return t / jnp.clip(jnp.linalg.norm(t, axis=-1, keepdims=True), 1e-12)

        def rotate_half(x):
            x1, x2 = jnp.split(x, 2, axis=-1)
            return jnp.concatenate([-x2, x1], axis=-1)

        def rotary_xpos(q, k):
            n = q.shape[-2]
            half_idx = jnp.arange(0, DIM_HEAD, 2, dtype=jnp.float32)
            inv_freq = 1.0 / 10000.0 ** (half_idx / DIM_HEAD)
            t = jnp.arange(n, dtype=jnp.float32)
            freqs = t[:, None] * inv_freq[None, :]
            freqs = jnp.concatenate([freqs, freqs], axis=-1)
            base = (half_idx + 0.4 * DIM_HEAD) / (1.4 * DIM_HEAD)
            power = (t - n // 2) / float(WINDOW // 2)
            scale = base[None, :] ** power[:, None]
            scale = jnp.concatenate([scale, scale], axis=-1)
            cos, sin = (jnp.cos(freqs), jnp.sin(freqs))
            q = q * cos * scale + rotate_half(q) * sin * scale
            k = k * cos / scale + rotate_half(k) * sin / scale
            return (q, k)

        def local_attention(q, k, v):
            b, h, n, d = q.shape
            w = n // WINDOW
            bq = q.reshape(b, h, w, WINDOW, d) * QK_SCALE
            bk = k.reshape(b, h, w, WINDOW, d)
            bv = v.reshape(b, h, w, WINDOW, d)

            def look_around(t):
                p = jnp.pad(t, ((0, 0), (0, 0), (1, 0), (0, 0), (0, 0)))
                return jnp.concatenate([p[:, :, :w], p[:, :, 1:]], axis=3)
            bk, bv = (look_around(bk), look_around(bv))
            bt = jnp.arange(n).reshape(w, WINDOW)
            btp = jnp.pad(bt, ((1, 0), (0, 0)), constant_values=-1)
            btk = jnp.concatenate([btp[:w], btp[1:]], axis=1)
            sim = jnp.einsum('bhwid,bhwjd->bhwij', bq, bk)
            i = bt[:, :, None]
            j = btk[:, None, :]
            mask = (i < j) | (i > j + WINDOW) | (j == -1)
            sim = jnp.where(mask, -jnp.finfo(sim.dtype).max, sim)
            attn = jax.nn.softmax(sim, axis=-1)
            out = jnp.einsum('bhwij,bhwjd->bhwid', attn, bv)
            return out.reshape(b, h, n, d)

        def _layer(x, wqkv, qs, ksc, wo, lg, lb, w1, b1, w2, b2):
            b, n, _ = x.shape
            h = shift_token(x)
            qkv = h @ wqkv
            q, k, v = jnp.split(qkv, 3, axis=-1)
            to_heads = lambda t: t.reshape(b, n, HEADS, DIM_HEAD).transpose(0, 2, 1, 3)
            q, k, v = (to_heads(q), to_heads(k), to_heads(v))
            q = l2norm(q) * qs
            k = l2norm(k) * ksc
            q, k = rotary_xpos(q, k)
            o = local_attention(q, k, v)
            o = o.transpose(0, 2, 1, 3).reshape(b, n, INNER)
            x = x + o @ wo
            h = shift_token(x)
            mu = h.mean(-1, keepdims=True)
            var = h.var(-1, keepdims=True)
            h = (h - mu) / jnp.sqrt(var + 1e-05) * lg + lb
            h = h @ w1 + b1
            a, g = jnp.split(h, 2, axis=-1)
            h = a * jax.nn.gelu(g, approximate=False)
            x = x + h @ w2 + b2
            return x
        for l in range(DEPTH):
            x = _layer(x, wqkv[l], q_scale[l], k_scale[l], wo[l], ln_g[l], ln_b[l], w1[l], b1[l], w2[l], b2[l])
        return x

    def _L1_attn_ref(x, W_in, conv_w, conv_b, W_x, W_dt, b_dt, A_log, D, W_out):
        import jax, jax.numpy as jnp
        import numpy as np
        D_CONV = 4
        DT_RANK = 64
        D_STATE = 16

        def silu(v):
            return v * jax.nn.sigmoid(v)
        B, L, _ = x.shape
        d_inner = W_dt.shape[1]
        xz = x @ W_in
        xb, z = jnp.split(xz, 2, axis=-1)
        xp = jnp.pad(xb, ((0, 0), (D_CONV - 1, 0), (0, 0)))
        xc = sum((xp[:, k:k + L, :] * conv_w[:, k] for k in range(D_CONV))) + conv_b
        xb = silu(xc)
        x_dbl = xb @ W_x
        dt_low, Bm, Cm = jnp.split(x_dbl, [DT_RANK, DT_RANK + D_STATE], axis=-1)
        dt = jax.nn.softplus(dt_low @ W_dt + b_dt)
        A = -jnp.exp(A_log)

        def step(h, inp):
            dt_t, B_t, C_t, x_t = inp
            dA = jnp.exp(A * dt_t[..., None])
            h = h * dA + (x_t * dt_t)[..., None] * B_t[:, None, :]
            y = jnp.einsum('bdn,bn->bd', h, C_t)
            return (h, y)
        xs = (dt.swapaxes(0, 1), Bm.swapaxes(0, 1), Cm.swapaxes(0, 1), xb.swapaxes(0, 1))
        h0 = jnp.zeros((B, d_inner, D_STATE), dtype=x.dtype)
        _, ys = jax.lax.scan(step, h0, xs)
        y = ys.swapaxes(0, 1) + xb * D
        out = y * silu(z)
        return out @ W_out

    def _L1_ffn_ref(x, w_gate, w_up, w_down):
        import jax, jax.numpy as jnp
        import numpy as np
        DIM = 128
        HIDDEN = 384
        SCALE = 1.0 / 127.0

        def _dequant(w_int, dtype):
            return w_int.astype(dtype) * jnp.asarray(SCALE, dtype)
        wg = _dequant(w_gate, x.dtype)
        wu = _dequant(w_up, x.dtype)
        wd = _dequant(w_down, x.dtype)
        gate = jnp.einsum('bsd,hd->bsh', x, wg)
        up = jnp.einsum('bsd,hd->bsh', x, wu)
        h = jax.nn.silu(gate) * up
        return jnp.einsum('bsh,dh->bsd', h, wd)
    x = L0_attn_x
    x = x + _layernorm(_L0_attn_ref(_layernorm(x, axis=-1), L0_attn_Wq, L0_attn_Wk, L0_attn_Wv, L0_attn_Wo), axis=-1)
    x = x + _layernorm(_L0_ffn_ref(_layernorm(x, axis=-1), L0_ffn_wqkv, L0_ffn_q_scale, L0_ffn_k_scale, L0_ffn_wo, L0_ffn_ln_g, L0_ffn_ln_b, L0_ffn_w1, L0_ffn_b1, L0_ffn_w2, L0_ffn_b2), axis=-1)
    x = x + _layernorm(_L1_attn_ref(_layernorm(x, axis=-1), L1_attn_W_in, L1_attn_conv_w, L1_attn_conv_b, L1_attn_W_x, L1_attn_W_dt, L1_attn_b_dt, L1_attn_A_log, L1_attn_D, L1_attn_W_out), axis=-1)
    x = x + _layernorm(_L1_ffn_ref(_layernorm(x, axis=-1), L1_ffn_w_gate, L1_ffn_w_up, L1_ffn_w_down), axis=-1)
    return x

_drawn_inputs = setup_inputs


def setup_inputs(seed=0):
    import zlib

    import numpy as np

    out = dict(_drawn_inputs(seed))
    spreads = {'L0_ffn_q_scale': (1.0, 0.6),
     'L0_ffn_k_scale': (1.0, 0.6),
     'L0_ffn_ln_g': (1.0, 0.6),
     'L0_ffn_ln_b': (0.0, 0.8),
     'L0_ffn_b1': (0.0, 0.8),
     'L0_ffn_b2': (0.0, 0.513),
     'L1_attn_D': (1.0, 0.2)}
    factors = {'L0_ffn_w1': 5.764, 'L0_ffn_w2': 5.652, 'L1_attn_conv_b': 3.707, 'L1_attn_b_dt': 8.0}
    for name, (base, spread) in spreads.items():
        noise = np.random.default_rng([zlib.crc32(name.encode()), seed]).standard_normal(out[name].shape)
        drawn = base * np.exp(spread * noise) if base else spread * noise
        out[name] = jnp.asarray(drawn.astype(out[name].dtype))
    for name, factor in factors.items():
        out[name] = (out[name] * factor).astype(out[name].dtype)
    return out
```

```python
import numpy as np
from contextlib import ExitStack, contextmanager

import concourse.bass as bass
from concourse import mybir

F32 = mybir.dt.float32
I32 = mybir.dt.int32
ALU = mybir.AluOpType
ACT = mybir.ActivationFunctionType
AX = mybir.AxisListType

P = 128
BATCH, SEQ, DIM = 16, 256, 128
TPB = SEQ // P
NT = BATCH * TPB
LN_EPS = 1e-5
LEN_SCALE = 2.0 ** 8

AH, ADK = 16, 8
AG = 4
DEPTH, FH, FD, WIN = 2, 8, 64, 64
INNER = FH * FD
HID = DIM * 4 * 2 // 3
HCH = [(0, 114), (114, 114), (228, 113)]
MASKED = 1e30
DIN, NST, DTR, NCONV = 256, 16, 64, 4
CH = DIN // P
HID1 = 384


def shape_constants():
    f = np.float32
    pos = np.arange(SEQ, dtype=f)
    inv = (1.0 / 10000.0 ** (np.arange(0, ADK, 2, dtype=f) / ADK)).astype(f)
    fr = (pos[:, None] * inv[None, :]).astype(f)
    sin = np.repeat(np.sin(fr), 2, axis=-1).T
    cos = np.repeat(np.cos(fr), 2, axis=-1).T
    sign = np.where(np.arange(ADK) % 2 == 0, -1.0, 1.0)[:, None]
    slopes = 2.0 ** (-8.0 * np.arange(AH, dtype=np.float64) / AH)
    qs = np.repeat(-1.0 / (np.sqrt(ADK) * slopes), ADK)[:, None]
    cosr, sinr = np.tile(cos, (AH, 1)), np.tile(sin * sign, (AH, 1))
    rope = np.stack([cosr * qs, sinr * qs, cosr, sinr], 1).astype(f)
    dist = np.abs(pos[:, None] - pos[None, :]).reshape(TPB, P, SEQ).transpose(1, 0, 2).astype(f)
    headmask = (np.arange(P)[:, None] // ADK % AG == np.arange(AG)[None, :]).astype(f)
    ones = np.zeros((P, AG, 32), f)
    for j in range(AG):
        ones[:, j, j * ADK:(j + 1) * ADK] = 1.0

    half = np.arange(0, FD, 2, dtype=f)
    finv = (1.0 / 10000.0 ** (half / FD)).astype(f)
    ff = (pos[:, None] * finv[None, :]).astype(f)
    ff = np.concatenate([ff, ff], -1)
    base = (half + f(0.4 * FD)) / f(1.4 * FD)
    power = (pos - SEQ // 2) / f(WIN // 2)
    sc = (base[None, :] ** power[:, None]).astype(f)
    sc = np.concatenate([sc, sc], -1).astype(np.float64)
    s2 = np.where(np.arange(FD) < FD // 2, -1.0, 1.0)
    c64, s64 = np.cos(ff).astype(np.float64), np.sin(ff).astype(np.float64)
    xpos = np.stack([c64 * sc * -8.0, s64 * sc * s2 * -8.0, c64 / sc, s64 / sc * s2], 1) * LEN_SCALE
    xpos = xpos.reshape(TPB, P, 4, FD).transpose(1, 0, 2, 3).astype(f)
    wmask = np.full((P, TPB, 192), MASKED, f)
    for t in range(TPB):
        first = 0 if t == 0 else t * P - WIN
        i = np.arange(P)[:, None] + t * P
        j = np.arange(192)[None, :] + first
        wmask[:, t] = np.where((j <= i) & (j >= i - WIN), 0.0, MASKED)
    center = (np.eye(P) - 1.0 / P).astype(f)
    select = np.zeros((2 * NST, 2 * NST, P), f)
    select[np.arange(2 * NST), np.arange(2 * NST)] = 1.0
    return {"center": center, "select": select, "rope": rope, "dist": dist, "headmask": headmask, "onesmask": ones, "xpos": xpos, "wmask": wmask}


def flat(ap):
    return ap.rearrange("p a c -> p (a c)")


def build(nc, d, out, stop=99):
    ctx = ExitStack()
    names = {}

    def sb(name, shape, dt=F32):
        return ctx.enter_context(nc.sbuf_tensor(name, shape, dt))

    stage_semaphores = []

    def sem(name):
        stage_semaphores[-1].append(nc.alloc_semaphore(name=name))
        return stage_semaphores[-1][-1]

    @contextmanager
    def stage():
        stage_semaphores.append([])
        yield
        nc.clear_and_free_semaphores(stage_semaphores.pop())
        nc.all_engine_barrier()

    with ctx:
        X = sb("X", [P, NT, DIM])
        Z = sb("Z", [P, NT, DIM])
        Y = sb("Y", [P, NT, DIM])
        STAT = sb("STAT", [P, NT, 6])
        RSTD = sb("RSTD", [P, NT])
        NMR = sb("NMR", [P, NT])
        EPS = sb("EPS", [P, 2])
        ident = sb("ident", [P, P])
        ps = ctx.enter_context(nc.psum_tensor("ps", [P, 8, 512], F32))

        xv = d["x"].rearrange("b (t p) d -> p (b t) d", p=P)
        ov = out.rearrange("b (t p) d -> p (b t) d", p=P)

        x_in = nc.alloc_semaphore(name="x_in")

        passed = {}

        def wait_alone(e, semaphore, value):
            if e.engine not in passed:
                passed[e.engine] = nc.alloc_semaphore(name=f"passed_{len(passed)}")
            e.wait_ge(semaphore, value)
            e.sem_inc(passed[e.engine], 1)

        with stage(), nc.Block() as block:
            ident_zero, ident_made = sem("ident_zero"), sem("ident_made")

            @block.sync
            def _(e):
                e.dma_start(X[:, :, :], xv).then_inc(x_in, 16)
                e.wait_ge(x_in, 16)

            @block.gpsimd
            def _(e):
                e.memset(ident[:, :], 0.0).then_inc(ident_zero, 1)
                e.memset(EPS[:, 0:1], LN_EPS)
                e.memset(EPS[:, 1:2], 1e-24)
                e.wait_ge(ident_zero, 1)
                e.affine_select(out=ident[:, :], in_=ident[:, :], compare_op=ALU.not_equal, fill=1.0,
                                base=0, pattern=[[-1, P]], channel_multiplier=1).then_inc(ident_made, 1)

        def norm_stats(tag, src, count):
            sq, tmp = names["small"][:, 0:NT], names["small"][:, NT:2 * NT]
            s_sum, s_rstd = sem(tag + "_moments"), sem(tag + "_rstd")
            s_link = sem(tag + "_link")
            with nc.Block() as block:
                @block.vector
                def _(e):
                    if count:
                        with e.Fori(0, NT // 4) as i:
                            for t in range(4):
                                e.bn_stats(STAT[:, bass.ds(i * 4 + t, 1), :].rearrange("p a c -> p (a c)"),
                                           src[:, bass.ds(i * 4 + t, 1), :].rearrange("p a c -> p (a c)")).then_inc(s_link, 1)
                        e.wait_ge(s_link, NT)
                    base = NT if count else 0
                    e.tensor_tensor(tmp, STAT[:, :, 1], STAT[:, :, 4], ALU.subtract).then_inc(s_link, 1)
                    e.tensor_tensor(sq, STAT[:, :, 2], STAT[:, :, 5], ALU.add).then_inc(s_link, 1)
                    e.tensor_tensor(NMR[:, :], STAT[:, :, 1], STAT[:, :, 4], ALU.add).then_inc(s_link, 1)
                    e.wait_ge(s_link, base + 3)
                    e.tensor_tensor(tmp, tmp, tmp, ALU.mult).then_inc(s_link, 1)
                    e.wait_ge(s_link, base + 4)
                    e.scalar_tensor_tensor(tmp, tmp, DIM / 4.0, sq, ALU.mult, ALU.add).then_inc(s_sum, 1)
                    e.wait_ge(s_rstd, 2)
                    e.scalar_tensor_tensor(NMR[:, :], NMR[:, :], -0.5, RSTD[:, :], ALU.mult, ALU.mult)

                @block.scalar
                def _(e):
                    e.preload_act_table_set("natural_log_exp_and_others")
                    e.wait_ge(s_sum, 1)
                    e.activation(sq, tmp, ACT.Ln, scale=1.0 / DIM, bias=EPS[:, 0:1]).then_inc(s_rstd, 1)
                    e.wait_ge(s_rstd, 1)
                    e.activation(RSTD[:, :], sq, ACT.Exp, scale=-0.5).then_inc(s_rstd, 1)

        small = sb("small", [P, 2 * NT])
        names["small"] = small

        def add_normed(tag, Z):
            s_t, s_x = sem(tag + "_normed"), sem(tag + "_added")
            with nc.Block() as block:
                @block.scalar
                def _(e):
                    with e.Fori(0, NT // 4) as i:
                        for t in range(4):
                            k = bass.ds(i * 4 + t, 1)
                            e.activation(Z[:, k, :].rearrange("p a c -> p (a c)"), Z[:, k, :].rearrange("p a c -> p (a c)"),
                                         ACT.Identity, scale=RSTD[:, k], bias=NMR[:, k]).then_inc(s_t, 1)

                @block.vector
                def _(e):
                    with e.Fori(0, NT // 4) as i:
                        e.wait_ge(s_t, i * 4 + 4)
                        k = bass.ds(i * 4, 4)
                        e.tensor_tensor(X[:, k, :], X[:, k, :], Z[:, k, :], ALU.add).then_inc(s_x, 1)

        def store():
            s_out = sem("stored")
            with nc.Block() as block:
                @block.sync
                def _(e):
                    e.dma_start(ov, X[:, :, :]).then_inc(s_out, 16)
                    e.wait_ge(s_out, 16)

        def attention():
            c = ExitStack()
            with c:
                def tb(name, shape, dt=F32):
                    return c.enter_context(nc.sbuf_tensor(name, shape, dt))
                G, TG = 2, 2 * TPB
                W = tb("a_w", [P, 6, P])
                rope = tb("a_rope", [P, 4, SEQ])
                dist = tb("a_dist", [P, TPB, SEQ])
                hmask = tb("a_hmask", [P, AG])
                onesm = tb("a_ones", [P, AG, 32])
                xn = tb("a_xn", [P, TG, P])
                xT = tb("a_xT", [P, TG * P])
                rot = tb("a_rot", [P, 4, TG * P])
                Q = tb("a_Q", [P, G, SEQ])
                K = tb("a_K", [P, G, SEQ])
                QM = tb("a_QM", [P, AG, G * SEQ])
                VM = tb("a_VM", [P, TG, AG, AG, 32])
                NSB, NPT = 3, 8
                SBS = tb("a_scores", [P, NSB, 2, SEQ])
                PR = tb("a_probs", [P, NSB, 2, SEQ])
                PT = tb("a_probsT", [P, NPT, 2, TPB, P])
                MN = tb("a_min", [P, 64])
                RS = tb("a_rsum", [P, G * SEQ])
                OT = tb("a_oT", [P, G * SEQ])
                w_in = sem("a_w_in")
                vm_zero = sem("a_vm_zero")
                xn_ready, xT_psum, xT_ready = sem("a_xn_ready"), sem("a_xT_psum"), sem("a_xT_ready")
                proj_psum, v_psum, rot_ready = sem("a_proj_psum"), sem("a_v_psum"), sem("a_rot_ready")
                qk_ready, qm_ready, vm_ready = sem("a_qk_ready"), sem("a_qm_ready"), sem("a_vm_ready")
                s_psum, s_moved, p_ready = sem("a_s_psum"), sem("a_s_moved"), sem("a_p_ready")
                pT_psum, pv_done = sem("a_pT_psum"), sem("a_pv_done")
                pT_even, pT_odd = sem("a_pT_even"), sem("a_pT_odd")
                rs_ready, oT_ready, z_psum, z_ready = sem("a_rs_ready"), sem("a_oT_ready"), sem("a_z_psum"), sem("a_z_ready")
                stat_done = sem("a_stat_done")
                NG = BATCH // G
                NPAIR = G * TPB * 2 * AG
                pairs = [(b, qt, jp, g) for b in range(G) for qt in range(TPB) for jp in range(2) for g in range(AG)]
                SBANK, TBANK, OBANK, DBANK = 0, 3, 6, 7

                with nc.Block() as block:
                    @block.sync
                    def _(e):
                        for n, name in enumerate(["wq", "wqr", "wk", "wkr", "wv", "wo0"]):
                            e.dma_start(W[:, n, :], d[name]).then_inc(w_in, 16)
                        e.dma_start(rope[:, :, :], d["rope"]).then_inc(w_in, 16)
                        e.dma_start(dist[:, :, :], d["dist"]).then_inc(w_in, 16)
                        e.dma_start(hmask[:, :], d["headmask"]).then_inc(w_in, 16)
                        e.dma_start(onesm[:, :, :], d["onesmask"]).then_inc(w_in, 16)
                        e.wait_ge(w_in, 160)

                    @block.gpsimd
                    def _(e):
                        e.memset(VM[:, :, :, :, :], 0.0).then_inc(vm_zero, 1)
                        e.wait_ge(w_in, 160)
                        with e.Fori(0, NG) as i:
                            e.wait_ge(rot_ready, i * 2 + 1)
                            e.wait_ge(z_psum, i)
                            e.tensor_tensor(Q[:, :, :].rearrange("p b t -> p (b t)"), rot[:, 0, :], rot[:, 1, :], ALU.add).then_inc(qk_ready, 1)
                            e.wait_ge(rot_ready, i * 2 + 2)
                            e.tensor_tensor(K[:, :, :].rearrange("p b t -> p (b t)"), rot[:, 2, :], rot[:, 3, :], ALU.add).then_inc(qk_ready, 1)
                            wait_alone(e, qk_ready, i * 2 + 2)
                            for j in range(AG):
                                e.tensor_scalar(QM[:, j, :], Q[:, :, :].rearrange("p b t -> p (b t)"), hmask[:, j:j + 1], 0.0,
                                                ALU.mult, ALU.add).then_inc(qm_ready, 1)

                    @block.scalar
                    def _(e):
                        e.wait_ge(vm_zero, 1)
                        with e.Fori(0, NG) as i:
                            wait_alone(e, z_psum, i)
                            for t in range(TG):
                                k = bass.ds(i * TG + t, 1)
                                e.activation(xn[:, t, :], X[:, k, :].rearrange("p a c -> p (a c)"), ACT.Identity,
                                             scale=RSTD[:, k], bias=NMR[:, k]).then_inc(xn_ready, 1)
                            e.wait_ge(v_psum, i + 1)
                            for j in range(AG):
                                e.activation(VM[:, :, :, j, j * ADK:(j + 1) * ADK].rearrange("p t g c -> p (t g) c"),
                                             ps[:, 5, :].rearrange("p (tg j c) -> p tg j c", j=AG, c=ADK)[:, :, j, :],
                                             ACT.Copy).then_inc(vm_ready, 1)
                            def evac(p):
                                if p % 2 == 1:
                                    e.wait_ge(pT_psum, i * NPAIR + p + 1)
                                    if p >= NPT:
                                        e.wait_ge(pv_done, i * (NPAIR // 4) + (p - NPT) // 4 + 1)
                                    e.activation(PT[:, p % NPT, :, :, :].rearrange("p a b c -> p (a b c)"), ps[:, TBANK + p % 3, :],
                                                 ACT.Copy).then_inc(pT_odd, 1)
                            for p, (b, qt, jp, g) in enumerate(pairs):
                                if p >= NSB:
                                    e.wait_ge(pT_psum, i * NPAIR + p - NSB + 1)
                                for a in range(2):
                                    h = 4 * g + 2 * jp + a
                                    e.wait_ge(s_moved, i * 2 * NPAIR + 2 * p + a + 1)
                                    e.activation(PR[:, p % NSB, a, :], SBS[:, p % NSB, a, :], ACT.Exp, scale=-1.0,
                                                 bias=MN[:, 2 * p + a:2 * p + a + 1]).then_inc(p_ready, 1)
                                if p >= 2:
                                    evac(p - 2)
                            evac(NPAIR - 2)
                            evac(NPAIR - 1)
                            wait_alone(e, z_psum, i + 1)
                            e.activation(Z[:, bass.ds(i * TG, TG), :].rearrange("p a c -> p (a c)"), ps[:, 3, :], ACT.Copy).then_inc(z_ready, 1)

                    @block.vector
                    def _(e):
                        e.wait_ge(w_in, 160)
                        with e.Fori(0, NG) as i:
                            e.wait_ge(xT_psum, i + 1)
                            e.tensor_copy(xT[:, :], ps[:, 0, :]).then_inc(xT_ready, 1)
                            for n in range(4):
                                e.wait_ge(proj_psum, i * 4 + n + 1)
                                ins = e.tensor_tensor(rot[:, n, :].rearrange("p (b t) -> p b t", b=G),
                                                      ps[:, 1 + n, :].rearrange("p (b t) -> p b t", b=G),
                                                      rope[:, n, :].unsqueeze(1).to_broadcast([P, G, SEQ]), ALU.mult)
                                if n % 2:
                                    ins.then_inc(rot_ready, 1)
                            def evac(p):
                                if p % 2 == 0:
                                    e.wait_ge(pT_psum, i * NPAIR + p + 1)
                                    if p >= NPT:
                                        e.wait_ge(pv_done, i * (NPAIR // 4) + (p - NPT) // 4 + 1)
                                    e.tensor_copy(PT[:, p % NPT, :, :, :].rearrange("p a b c -> p (a b c)"), ps[:, TBANK + p % 3, :])\
                                     .then_inc(pT_even, 1)
                            for p, (b, qt, jp, g) in enumerate(pairs):
                                wait_alone(e, s_psum, i * NPAIR + p + 1)
                                if p >= NSB:
                                    wait_alone(e, p_ready, i * 2 * NPAIR + 2 * (p - NSB) + 2)
                                for a in range(2):
                                    h = 4 * g + 2 * jp + a
                                    e.tensor_tensor_reduce(SBS[:, p % NSB, a, :], ps[:, SBANK + p % 3, a * SEQ:(a + 1) * SEQ], dist[:, qt, :],
                                                           2.0 ** (-8.0 * h / AH), 3.0e38, ALU.add, ALU.min,
                                                           accum_out=MN[:, 2 * p + a:2 * p + a + 1]).then_inc(s_moved, 1)
                                if p >= 2:
                                    evac(p - 2)
                            evac(NPAIR - 2)
                            evac(NPAIR - 1)
                            e.wait_ge(pv_done, (i + 1) * (NPAIR // 4))
                            e.reciprocal(RS[:, :], ps[:, DBANK, :]).then_inc(rs_ready, 1)
                            e.wait_ge(rs_ready, i + 1)
                            e.tensor_tensor(OT[:, :], ps[:, OBANK, :], RS[:, :], ALU.mult).then_inc(oT_ready, 1)
                            wait_alone(e, z_ready, i + 1)
                            for t in range(TG):
                                k = bass.ds(i * TG + t, 1)
                                e.bn_stats(STAT[:, k, :].rearrange("p a c -> p (a c)"), Z[:, k, :].rearrange("p a c -> p (a c)")).then_inc(stat_done, 1)

                    @block.tensor
                    def _(e):
                        e.wait_ge(w_in, 160)
                        with e.Fori(0, NG) as i:
                            for t in range(TG):
                                e.wait_ge(xn_ready, i * TG + t + 1)
                                ins = e.transpose(ps[:, 0, t * P:(t + 1) * P], xn[:, t, :], ident[:, :])
                            ins.then_inc(xT_psum, 1)
                            e.wait_ge(xT_ready, i + 1)
                            e.wait_ge(z_ready, i)
                            for n in range(4):
                                e.matmul(ps[:, 1 + n, :], W[:, n, :], xT[:, :], start=True, stop=True).then_inc(proj_psum, 1)
                            for t in range(TG):
                                ins = e.matmul(ps[:, 5, t * P:(t + 1) * P], xT[:, t * P:(t + 1) * P], W[:, 4, :], start=True, stop=True)
                            ins.then_inc(v_psum, 1)
                            e.wait_ge(rot_ready, i * 2 + 2)
                            e.wait_ge(qm_ready, i * AG + AG)
                            e.wait_ge(vm_ready, i * AG + AG)

                            def scores(p):
                                b, qt, jp, g = pairs[p]
                                if p >= 3:
                                    e.wait_ge(s_moved, i * 2 * NPAIR + 2 * (p - 3) + 2)
                                r = slice(32 * g, 32 * g + 32)
                                for a in range(2):
                                    at = b * SEQ + qt * P
                                    ins = e.matmul(ps[:, SBANK + p % 3, a * SEQ:(a + 1) * SEQ], QM[r, 2 * jp + a, at:at + P],
                                                   K[r, b, :], start=True, stop=True)
                                ins.then_inc(s_psum, 1)

                            def taken(p):
                                e.wait_ge(pT_odd if p % 2 else pT_even, i * (NPAIR // 2) + p // 2 + 1)

                            def turn(p):
                                if p >= 3:
                                    taken(p - 3)
                                for a in range(2):
                                    e.wait_ge(p_ready, i * 2 * NPAIR + 2 * p + a + 1)
                                    for kb in range(TPB):
                                        at = (a * TPB + kb) * P
                                        ins = e.transpose(ps[:, TBANK + p % 3, at:at + P], PR[:, p % NSB, a, kb * P:(kb + 1) * P], ident[:, :])
                                ins.then_inc(pT_psum, 1)

                            def weigh(q):
                                b, qt, jp, _ = pairs[4 * q]
                                taken(4 * q + 2)
                                taken(4 * q + 3)
                                for a in range(2):
                                    for kb in range(TPB):
                                        for g in range(AG):
                                            first, last = jp == 0 and a == 0 and kb == 0, jp == 1 and a == 1 and kb == TPB - 1
                                            o = slice(32 * g, 32 * g + 32)
                                            at = b * SEQ + qt * P
                                            pt = PT[:, (4 * q + g) % NPT, a, kb, :]
                                            e.matmul(ps[o, OBANK, at:at + P], VM[:, b * TPB + kb, g, 2 * jp + a, :], pt,
                                                     start=first, stop=last)
                                        for g in range(AG):
                                            o = slice(32 * g, 32 * g + 32)
                                            pt = PT[:, (4 * q + g) % NPT, a, kb, :]
                                            ins = e.matmul(ps[o, DBANK, at:at + P], onesm[:, 2 * jp + a, :], pt, start=first, stop=last)
                                ins.then_inc(pv_done, 1)

                            for p in range(NPAIR + 4):
                                if p < NPAIR:
                                    scores(p)
                                if 2 <= p < NPAIR + 2:
                                    turn(p - 2)
                                if p >= 7 and p % 4 == 3:
                                    weigh((p - 7) // 4)
                            e.wait_ge(oT_ready, i + 1)
                            for t in range(TG):
                                ins = e.matmul(ps[:, 3, t * P:(t + 1) * P], OT[:, t * P:(t + 1) * P], W[:, 5, :], start=True, stop=True)
                            ins.then_inc(z_psum, 1)


        def make_y():
            y_made = sem("y_made")
            with nc.Block() as block:
                @block.scalar
                def _(e):
                    with e.Fori(0, NT // 4) as i:
                        for t in range(4):
                            k = bass.ds(i * 4 + t, 1)
                            e.activation(flat(Y[:, k, :]), flat(X[:, k, :]), ACT.Identity, scale=RSTD[:, k],
                                         bias=NMR[:, k]).then_inc(y_made, 1)

        def window_attention(l):
            c = ExitStack()
            with c:
                def tb(name, shape, dt=F32):
                    return c.enter_context(nc.sbuf_tensor(name + str(l), shape, dt))

                G, TG = 2, 2 * TPB
                wqkv, wo = tb("w_qkv", [P, 3 * INNER]), tb("w_wo", [P, INNER // P, DIM])
                xpos, wmask = tb("w_xpos", [P, TPB, 4, FD]), tb("w_mask", [P, TPB, 192])
                scl = tb("w_scl", [P, 4, FD])
                yg, hT = tb("w_yg", [P, TG, DIM]), tb("w_hT", [P, G, SEQ])
                SQ = tb("w_sq", [P, 2, 2 * INNER])
                SS, RN = tb("w_ss", [P, TG, 2 * FH]), tb("w_rn", [P, TG, 2 * FH])
                QK = tb("w_qk", [P, 2, 2 * INNER])
                RC, RSN = tb("w_rc", [P, 2, 2 * INNER]), tb("w_rs", [P, 2, 2 * INNER])
                V = tb("w_v", [P, TG, INNER])
                QKT = tb("w_qkT", [P, 2, INNER // P, G * SEQ])
                NSB, NPT = 3, 4
                SBS, PR = tb("w_scores", [P, NSB, 2, 192]), tb("w_probs", [P, NSB, 2, SEQ])
                PT = tb("w_probsT", [P, NPT, 2, TPB, P])
                MN, SM = tb("w_min", [P, 32]), tb("w_sum", [P, TG, FH])
                RI, ON, OT = tb("w_ri", [P, TG, FH]), tb("w_on", [P, INNER]), tb("w_oT", [P, INNER // P, P])
                names = ("w_in zeroed tables yg_ready yT_psum hT_ready qkv_psum sq_ready ss_ready rn_ready ln_ready v_ready qk_ready "
                         "rs_ready rc_ready r_ready rT_psum rT_ready s_psum s_moved p_ready pT_psum pT_even pT_odd pv_done "
                         "ri_ready on_ready oT_psum oT_ready o_psum y_ready").split()
                S = {n: sem(f"w{l}_{n}") for n in names}
                NG = BATCH // G
                pairs = [(b, t, bp, a) for b in range(G) for t in range(TPB) for bp in range(2) for a in range(2)]
                NPAIR = len(pairs)
                KEYS = [P, 192]

                def heads(p):
                    return [2 * (2 * pairs[p][2] + x) + pairs[p][3] for x in range(2)]

                with nc.Block() as block:
                    @block.sync
                    def _(e):
                        e.dma_start(wqkv[:, :], d["wqkv"][l]).then_inc(S["w_in"], 16)
                        e.dma_start(wo[:, :, :], d["wo"][l].rearrange("(c p) n -> p c n", p=P)).then_inc(S["w_in"], 16)
                        e.dma_start(xpos[:, :, :, :], d["xpos"]).then_inc(S["w_in"], 16)
                        e.dma_start(wmask[:, :, :], d["wmask"]).then_inc(S["w_in"], 16)
                        for n, name in enumerate(("qs", "ks")):
                            row = d[name][l:l + 1, :]
                            e.dma_start(scl[:, 2 * n, :], row.to_broadcast([P, FD])).then_inc(S["w_in"], 16)
                            for x in range(2):
                                o = (1 - x) * FD // 2
                                e.dma_start(scl[:, 2 * n + 1, x * FD // 2:(x + 1) * FD // 2],
                                            row[:, o:o + FD // 2].to_broadcast([P, FD // 2])).then_inc(S["w_in"], 16)
                        e.wait_ge(S["w_in"], 160)

                    @block.gpsimd
                    def _(e):
                        e.memset(hT[:, :, 0:1], 0.0).then_inc(S["zeroed"], 1)
                        e.memset(PR[:, :, :, :], 0.0).then_inc(S["zeroed"], 1)
                        e.wait_ge(S["w_in"], 160)
                        for t in range(TPB):
                            e.tensor_tensor(xpos[:, t, :, :], xpos[:, t, :, :], scl[:, :, :], ALU.mult).then_inc(S["tables"], 1)
                        e.wait_ge(S["tables"], TPB)
                        with e.Fori(0, NG) as i:
                            for t in range(TG):
                                u = t % 2
                                for n in range(2):
                                    e.wait_ge(S["qk_ready"], i * 2 * TG + 2 * t + n + 1)
                                    if t >= 2:
                                        e.wait_ge(S["r_ready"], i * TG + t - 1)
                                    src = QK[:, u, n * INNER:(n + 1) * INNER].rearrange("p (h x c) -> p h x c", h=FH, x=2)
                                    dst = RSN[:, u, n * INNER:(n + 1) * INNER].rearrange("p (h x c) -> p h x c", h=FH, x=2)
                                    tab = xpos[:, t % TPB, 2 * n + 1, :].rearrange("p (x c) -> p x c", x=2)
                                    for x in range(2):
                                        e.tensor_tensor(dst[:, :, x, :], src[:, :, 1 - x, :],
                                                        tab[:, x, :].unsqueeze(1).to_broadcast([P, FH, FD // 2]), ALU.mult)\
                                         .then_inc(S["rs_ready"], 1)

                    @block.scalar
                    def _(e):
                        e.preload_act_table_set("natural_log_exp_and_others")
                        e.wait_ge(S["zeroed"], 2)
                        with e.Fori(0, NG) as i:
                            wait_alone(e, S["y_ready"], i * TG)
                            e.activation(yg[:, :, :], Y[:, bass.ds(i * TG, TG), :], ACT.Copy).then_inc(S["yg_ready"], 1)

                            def squares(t):
                                u = t % 2
                                for n in range(2):
                                    e.wait_ge(S["qkv_psum"], i * 3 * TG + 3 * t + n + 1)
                                    if t >= 2:
                                        e.wait_ge(S["ss_ready"], i * TG + t - 1)
                                    e.activation(SQ[:, u, n * INNER:(n + 1) * INNER], ps[:, 1 + 3 * u + n, :], ACT.Square)\
                                     .then_inc(S["sq_ready"], 1)
                                e.wait_ge(S["qkv_psum"], i * 3 * TG + 3 * t + 3)
                                e.activation(V[:, t, :], ps[:, 3 + 3 * u, :], ACT.Copy).then_inc(S["v_ready"], 1)
                                e.wait_ge(S["ss_ready"], i * TG + t + 1)
                                e.activation(RN[:, t, :], SS[:, t, :], ACT.Ln, scale=LEN_SCALE ** 2).then_inc(S["ln_ready"], 1)
                                e.wait_ge(S["ln_ready"], i * TG + t + 1)
                                e.activation(RN[:, t, :], RN[:, t, :], ACT.Exp, scale=-0.5).then_inc(S["rn_ready"], 1)

                            def rotated(t):
                                for n in range(2):
                                    e.wait_ge(S["rT_psum"], i * 2 * TG + 2 * t + n + 1)
                                    e.activation(QKT[:, n, :, t * P:(t + 1) * P], ps[:, 7 * n, :].rearrange("p (c q) -> p c q", q=P),
                                                 ACT.Copy).then_inc(S["rT_ready"], 1)
                            for t in range(TG + 1):
                                if t < TG:
                                    squares(t)
                                if t >= 1:
                                    rotated(t - 1)

                            def evac(p):
                                if p % 2 == 1:
                                    b, t, bp, a = pairs[p]
                                    e.wait_ge(S["pT_psum"], i * NPAIR + p + 1)
                                    if p >= NPT:
                                        e.wait_ge(S["pv_done"], i * NPAIR + p - NPT + 1)
                                    e.activation(PT[:, p % NPT, :, 0:t + 1, :], ps[:, 3 + p % 3, 0:2 * (t + 1) * P]
                                                 .rearrange("p (a k q) -> p a k q", a=2, q=P), ACT.Copy).then_inc(S["pT_odd"], 1)

                            def out_copy(k):
                                e.wait_ge(S["oT_psum"], i * TG + k + 1)
                                e.activation(OT[:, :, :], ps[:, 7, :].rearrange("p (c q) -> p c q", q=P), ACT.Copy)\
                                 .then_inc(S["oT_ready"], 1)

                            for p in range(NPAIR + 2):
                                if p < NPAIR:
                                    b, t, bp, a = pairs[p]
                                    if p >= NSB:
                                        e.wait_ge(S["pT_psum"], i * NPAIR + p - NSB + 1)
                                    for x, h in enumerate(heads(p)):
                                        e.wait_ge(S["s_moved"], i * 2 * NPAIR + 2 * p + x + 1)
                                        n, to = KEYS[t], 0 if t == 0 else WIN
                                        e.activation(PR[:, p % NSB, x, to:to + n], SBS[:, p % NSB, x, 0:n], ACT.Exp, scale=-1.0,
                                                     bias=MN[:, 2 * p + x:2 * p + x + 1],
                                                     accum_out=SM[:, b * TPB + t, h:h + 1]).then_inc(S["p_ready"], 1)
                                if p >= 2:
                                    evac(p - 2)
                                if p >= 6 and p % 4 == 2:
                                    out_copy((p - 6) // 4)
                            out_copy(TG - 1)

                    @block.vector
                    def _(e):
                        e.wait_ge(S["tables"], TPB)
                        e.wait_ge(S["zeroed"], 2)
                        with e.Fori(0, NG) as i:
                            e.wait_ge(S["yT_psum"], i + 1)
                            yT = ps[:, 0, :].rearrange("p (b t) -> p b t", b=G)
                            e.tensor_copy(hT[0:64, :, :], yT[0:64, :, :]).then_inc(S["hT_ready"], 1)
                            e.tensor_copy(hT[64:128, :, 1:SEQ], yT[64:128, :, 0:SEQ - 1]).then_inc(S["hT_ready"], 1)

                            def lengths(t):
                                u = t % 2
                                e.wait_ge(S["sq_ready"], i * 2 * TG + 2 * t + 2)
                                e.tensor_reduce(SS[:, t, :], SQ[:, u, :].rearrange("p (h c) -> p h c", c=FD), AX.X, ALU.add)\
                                 .then_inc(S["ri_ready"], 1)
                                e.wait_ge(S["ri_ready"], i * (2 * TG) + t + 1)
                                e.tensor_scalar(SS[:, t, :], SS[:, t, :], 1e-24, None, ALU.max).then_inc(S["ss_ready"], 1)

                            def rotate(t):
                                u = t % 2
                                e.wait_ge(S["rn_ready"], i * TG + t + 1)
                                if t >= 2:
                                    e.wait_ge(S["rs_ready"], i * 4 * TG + 4 * (t - 1))
                                for n in range(2):
                                    e.tensor_tensor(QK[:, u, n * INNER:(n + 1) * INNER].rearrange("p (h c) -> p h c", c=FD),
                                                    ps[:, 1 + 3 * u + n, :].rearrange("p (h c) -> p h c", c=FD),
                                                    RN[:, t, n * FH:(n + 1) * FH].unsqueeze(2).to_broadcast([P, FH, FD]), ALU.mult)\
                                     .then_inc(S["qk_ready"], 1)
                                e.wait_ge(S["qk_ready"], i * 2 * TG + 2 * t + 2)
                                for n in range(2):
                                    e.tensor_tensor(RC[:, u, n * INNER:(n + 1) * INNER].rearrange("p (h c) -> p h c", c=FD),
                                                    QK[:, u, n * INNER:(n + 1) * INNER].rearrange("p (h c) -> p h c", c=FD),
                                                    xpos[:, t % TPB, 2 * n, :].unsqueeze(1).to_broadcast([P, FH, FD]), ALU.mult)\
                                     .then_inc(S["rc_ready"], 1)
                                e.wait_ge(S["rc_ready"], i * 2 * TG + 2 * t + 2)
                                e.wait_ge(S["rs_ready"], i * 4 * TG + 4 * t + 4)
                                if t >= 2:
                                    e.wait_ge(S["rT_psum"], i * 2 * TG + 2 * (t - 1))
                                e.tensor_tensor(RSN[:, u, :], RC[:, u, :], RSN[:, u, :], ALU.add).then_inc(S["r_ready"], 1)
                            for t in range(TG):
                                lengths(t)
                                rotate(t)

                            def evac(p):
                                if p % 2 == 0:
                                    b, t, bp, a = pairs[p]
                                    e.wait_ge(S["pT_psum"], i * NPAIR + p + 1)
                                    if p >= NPT:
                                        e.wait_ge(S["pv_done"], i * NPAIR + p - NPT + 1)
                                    e.tensor_copy(PT[:, p % NPT, :, 0:t + 1, :], ps[:, 3 + p % 3, 0:2 * (t + 1) * P]
                                                  .rearrange("p (a k q) -> p a k q", a=2, q=P)).then_inc(S["pT_even"], 1)

                            def divide(k):
                                e.wait_ge(S["p_ready"], i * 2 * NPAIR + 8 * k + 8)
                                e.reciprocal(RI[:, k, :], SM[:, k, :]).then_inc(S["ri_ready"], 1)
                                e.wait_ge(S["ri_ready"], i * 2 * TG + TG + k + 1)
                                e.wait_ge(S["pv_done"], i * NPAIR + 4 * k + 4)
                                e.tensor_tensor(ON[:, :].rearrange("p (h c) -> p h c", c=FD),
                                                ps[:, 6, :].rearrange("p (h c) -> p h c", c=FD),
                                                RI[:, k, :].unsqueeze(2).to_broadcast([P, FH, FD]), ALU.mult).then_inc(S["on_ready"], 1)

                            def residual(k):
                                e.wait_ge(S["o_psum"], i * TG + k + 1)
                                r = bass.ds(i * TG + k, 1)
                                e.tensor_tensor(flat(Y[:, r, :]), ps[:, 6, 0:P], flat(Y[:, r, :]), ALU.add).then_inc(S["y_ready"], 1)

                            for p in range(NPAIR + 2):
                                if p < NPAIR:
                                    b, t, bp, a = pairs[p]
                                    wait_alone(e, S["s_psum"], i * NPAIR + p + 1)
                                    n = KEYS[t]
                                    if p >= NSB:
                                        wait_alone(e, S["p_ready"], i * 2 * NPAIR + 2 * (p - NSB) + 2)
                                    for x in range(2):
                                        e.tensor_tensor_reduce(SBS[:, p % NSB, x, 0:n], ps[:, p % 3, x * 192:x * 192 + n], wmask[:, t, 0:n],
                                                               1.0, 3.0e38, ALU.add, ALU.min,
                                                               accum_out=MN[:, 2 * p + x:2 * p + x + 1]).then_inc(S["s_moved"], 1)
                                if p >= 2:
                                    evac(p - 2)
                                if p >= 6 and p % 4 == 2:
                                    divide((p - 6) // 4)
                                    residual((p - 6) // 4)
                            divide(TG - 1)
                            residual(TG - 1)

                    @block.tensor
                    def _(e):
                        e.wait_ge(S["w_in"], 160)
                        with e.Fori(0, NG) as i:
                            e.wait_ge(S["yg_ready"], i + 1)
                            for t in range(TG):
                                ins = e.transpose(ps[:, 0, t * P:(t + 1) * P], yg[:, t, :], ident[:, :])
                            ins.then_inc(S["yT_psum"], 1)
                            e.wait_ge(S["hT_ready"], i * 2 + 2)
                            hf = hT[:, :, :].rearrange("p b t -> p (b t)")

                            def project(t):
                                u = t % 2
                                if t >= 2:
                                    e.wait_ge(S["qk_ready"], i * 2 * TG + 2 * (t - 1))
                                    e.wait_ge(S["v_ready"], i * TG + t - 1)
                                for n in range(3):
                                    e.matmul(ps[:, 1 + 3 * u + n, :], hf[:, t * P:(t + 1) * P], wqkv[:, n * INNER:(n + 1) * INNER],
                                             start=True, stop=True).then_inc(S["qkv_psum"], 1)

                            def turn_qk(t):
                                u = t % 2
                                e.wait_ge(S["r_ready"], i * TG + t + 1)
                                for n in range(2):
                                    if t >= 1:
                                        e.wait_ge(S["rT_ready"], i * 2 * TG + 2 * (t - 1) + n + 1)
                                    for c4 in range(4):
                                        ins = e.transpose(ps[:, 7 * n, c4 * P:(c4 + 1) * P],
                                                          RSN[:, u, n * INNER + c4 * P:n * INNER + (c4 + 1) * P], ident[:, :])
                                    ins.then_inc(S["rT_psum"], 1)
                            project(0)
                            for t in range(TG):
                                if t + 1 < TG:
                                    project(t + 1)
                                turn_qk(t)
                            e.wait_ge(S["rT_ready"], i * 2 * TG + 2 * TG)
                            e.wait_ge(S["qk_ready"], i * 2 * TG + 2 * TG)
                            e.wait_ge(S["v_ready"], i * TG + TG)

                            def scores(p):
                                b, t, bp, a = pairs[p]
                                if p >= 3:
                                    e.wait_ge(S["s_moved"], i * 2 * NPAIR + 2 * (p - 3) + 2)
                                r = slice(64 * a, 64 * a + 64)
                                at, n = b * SEQ + t * P, KEYS[t]
                                k0 = b * SEQ + (0 if t == 0 else t * P - WIN)
                                for x in range(2):
                                    ins = e.matmul(ps[:, p % 3, x * 192:x * 192 + n], QKT[r, 0, 2 * bp + x, at:at + P],
                                                   QKT[r, 1, 2 * bp + x, k0:k0 + n], start=True, stop=True)
                                ins.then_inc(S["s_psum"], 1)

                            def taken(p):
                                e.wait_ge(S["pT_odd"] if p % 2 else S["pT_even"], i * (NPAIR // 2) + p // 2 + 1)

                            def turn(p):
                                b, t, bp, a = pairs[p]
                                if p >= 3:
                                    taken(p - 3)
                                e.wait_ge(S["p_ready"], i * 2 * NPAIR + 2 * p + 2)
                                for x in range(2):
                                    for kb in range(t + 1):
                                        at = (x * (t + 1) + kb) * P
                                        ins = e.transpose(ps[:, 3 + p % 3, at:at + P], PR[:, p % NSB, x, kb * P:(kb + 1) * P], ident[:, :])
                                ins.then_inc(S["pT_psum"], 1)

                            def weigh(p):
                                b, t, bp, a = pairs[p]
                                if p % 4 == 0 and p:
                                    e.wait_ge(S["y_ready"], i * TG + p // 4)
                                taken(p)
                                for x, h in enumerate(heads(p)):
                                    for kb in range(t + 1):
                                        r = slice(0 if kb == t else WIN, P)
                                        ins = e.matmul(ps[:, 6, h * FD:(h + 1) * FD], PT[r, p % NPT, x, kb, :],
                                                       V[r, b * TPB + kb, h * FD:(h + 1) * FD], start=(kb == 0), stop=(kb == t))
                                ins.then_inc(S["pv_done"], 1)

                            def out_turn(k):
                                e.wait_ge(S["on_ready"], i * TG + k + 1)
                                for c4 in range(4):
                                    ins = e.transpose(ps[:, 7, c4 * P:(c4 + 1) * P], ON[:, c4 * P:(c4 + 1) * P], ident[:, :])
                                ins.then_inc(S["oT_psum"], 1)

                            def out_project(k):
                                e.wait_ge(S["oT_ready"], i * TG + k + 1)
                                for c4 in range(4):
                                    ins = e.matmul(ps[:, 6, 0:P], OT[:, c4, :], wo[:, c4, :], start=(c4 == 0), stop=(c4 == 3))
                                ins.then_inc(S["o_psum"], 1)

                            for p in range(NPAIR + 3):
                                if p < NPAIR:
                                    scores(p)
                                if 2 <= p < NPAIR + 2:
                                    turn(p - 2)
                                if p >= 3:
                                    weigh(p - 3)
                                    if p % 4 == 2:
                                        out_turn((p - 6) // 4)
                                        out_project((p - 6) // 4)

        def gelu_ffn(l):
            c = ExitStack()
            with c:
                def tb(name, shape, dt=F32):
                    return c.enter_context(nc.sbuf_tensor(name + str(l), shape, dt))

                G, TG = 2, 2 * TPB
                NG = BATCH // G
                W1, W2 = tb("g_w1", [P, 2 * HID]), tb("g_w2", [114, 3, DIM])
                W1G = tb("g_w1g", [P, 2 * HID])
                lgb = tb("g_lgb", [P, 2])
                B1 = tb("g_b1", [114, 2, 3])
                center, mean = tb("g_center", [P, P]), tb("g_mean", [P, P])
                HN = tb("g_hn", [P, BATCH, SEQ])
                yg, hT = tb("g_yg", [P, TG, DIM]), tb("g_hT", [P, G, SEQ])
                HC, SQ, RT = tb("g_hc", [P, G * SEQ]), tb("g_sq", [P, G * SEQ]), tb("g_rt", [P, G * SEQ])
                GL, HG = tb("g_gl", [114, 3, G * SEQ]), tb("g_hg", [114, 3, G * SEQ])
                names = ("w_in zeroed w1_scaled b1_psum b1_ready yg_ready yT_psum hT_ready hc_psum hc_ready sq_ready var_psum ln_ready rt_ready "
                         "hn_ready a_psum g_psum gl_ready hg_ready o_psum y_ready").split()
                S = {n: sem(f"g{l}_{n}") for n in names}
                with nc.Block() as block:
                    @block.sync
                    def _(e):
                        e.dma_start(W1[:, :], d["w1"][l]).then_inc(S["w_in"], 16)
                        for n, (o, m) in enumerate(HCH):
                            e.dma_start(W2[0:m, n, :], d["w2b"][l, o:o + m, :]).then_inc(S["w_in"], 16)
                            for x in range(2):
                                e.dma_start(B1[0:m, x, n:n + 1], d["b1"][l, x * HID + o:x * HID + o + m].unsqueeze(1)).then_inc(S["w_in"], 16)
                        e.dma_start(W2[113:114, 2, :], d["w2b"][l, HID:HID + 1, :]).then_inc(S["w_in"], 16)
                        e.dma_start(lgb[:, 0:1], d["lg"][l].unsqueeze(1)).then_inc(S["w_in"], 16)
                        e.dma_start(lgb[:, 1:2], d["lb"][l].unsqueeze(1)).then_inc(S["w_in"], 16)
                        e.dma_start(center[:, :], d["center"]).then_inc(S["w_in"], 16)
                        e.wait_ge(S["w_in"], 14 * 16)

                    @block.gpsimd
                    def _(e):
                        e.memset(hT[:, :, 0:1], 0.0).then_inc(S["zeroed"], 1)
                        e.memset(mean[:, :], 1.0 / DIM).then_inc(S["zeroed"], 1)
                        e.memset(HG[:, :, :], 1.0).then_inc(S["zeroed"], 1)

                    @block.scalar
                    def _(e):
                        e.preload_act_table_set("natural_log_exp_and_others")
                        with e.Fori(0, NG) as i:
                            wait_alone(e, S["hn_ready"], i)
                            e.activation(yg[:, :, :], Y[:, bass.ds(i * TG, TG), :], ACT.Copy).then_inc(S["yg_ready"], 1)
                            e.wait_ge(S["hc_ready"], i + 1)
                            e.activation(SQ[:, :], HC[:, :], ACT.Square).then_inc(S["sq_ready"], 1)
                            e.wait_ge(S["var_psum"], i + 1)
                            e.activation(RT[:, :], ps[:, 2, :], ACT.Ln, bias=EPS[:, 0:1]).then_inc(S["ln_ready"], 1)
                            e.wait_ge(S["ln_ready"], i + 1)
                            e.activation(RT[:, :], RT[:, :], ACT.Exp, scale=-0.5).then_inc(S["rt_ready"], 1)
                        e.wait_ge(S["b1_ready"], 3)
                        with e.Fori(0, NG) as i:
                            for n, (o, m) in enumerate(HCH):
                                e.wait_ge(S["g_psum"], i * 3 + n + 1)
                                e.wait_ge(S["hg_ready"], i * 3 + n)
                                e.activation(GL[0:m, n, :], ps[0:m, 4 + n % 2, :], ACT.Gelu, bias=B1[0:m, 1, n:n + 1]).then_inc(S["gl_ready"], 1)

                    @block.vector
                    def _(e):
                        e.wait_ge(S["w_in"], 14 * 16)
                        e.wait_ge(S["zeroed"], 3)
                        e.tensor_scalar(W1G[:, :], W1[:, :], lgb[:, 0:1], None, ALU.mult).then_inc(S["w1_scaled"], 1)
                        e.wait_ge(S["b1_psum"], 1)
                        for n, (o, m) in enumerate(HCH):
                            e.tensor_tensor(B1[0:m, :, n], ps[0:m, 7, n:n + 4:3], B1[0:m, :, n], ALU.add).then_inc(S["b1_ready"], 1)
                        with e.Fori(0, NG) as i:
                            e.wait_ge(S["yT_psum"], i + 1)
                            yT = ps[:, 0, :].rearrange("p (b t) -> p b t", b=G)
                            e.tensor_copy(hT[0:64, :, :], yT[0:64, :, :]).then_inc(S["hT_ready"], 1)
                            e.tensor_copy(hT[64:128, :, 1:SEQ], yT[64:128, :, 0:SEQ - 1]).then_inc(S["hT_ready"], 1)
                            e.wait_ge(S["hc_psum"], i + 1)
                            e.tensor_copy(HC[:, :], ps[:, 1, :]).then_inc(S["hc_ready"], 1)
                            e.wait_ge(S["rt_ready"], i + 1)
                            e.tensor_tensor(HN[:, bass.ds(i * G, G), :].rearrange("p b t -> p (b t)"), HC[:, :], RT[:, :], ALU.mult)\
                             .then_inc(S["hn_ready"], 1)
                        e.wait_ge(S["b1_ready"], 3)
                        with e.Fori(0, NG) as i:
                            for n, (o, m) in enumerate(HCH):
                                e.wait_ge(S["a_psum"], i * 3 + n + 1)
                                e.wait_ge(S["gl_ready"], i * 3 + n + 1)
                                e.wait_ge(S["o_psum"], i)
                                e.scalar_tensor_tensor(HG[0:m, n, :], ps[0:m, 2 + n % 2, :], B1[0:m, 0, n:n + 1], GL[0:m, n, :],
                                                       ALU.add, ALU.mult).then_inc(S["hg_ready"], 1)
                            e.wait_ge(S["o_psum"], i + 1)
                            k = bass.ds(i * TG, TG)
                            e.tensor_tensor(flat(Y[:, k, :]), ps[:, 6, :], flat(Y[:, k, :]), ALU.add).then_inc(S["y_ready"], 1)

                    @block.tensor
                    def _(e):
                        e.wait_ge(S["w_in"], 14 * 16)
                        e.wait_ge(S["zeroed"], 3)
                        for x in range(2):
                            for n, (o, m) in enumerate(HCH):
                                ins = e.matmul(ps[0:m, 7, x * 3 + n:x * 3 + n + 1], W1[:, x * HID + o:x * HID + o + m], lgb[:, 1:2],
                                               start=True, stop=True)
                        ins.then_inc(S["b1_psum"], 1)
                        with e.Fori(0, NG) as i:
                            e.wait_ge(S["yg_ready"], i + 1)
                            for t in range(TG):
                                ins = e.transpose(ps[:, 0, t * P:(t + 1) * P], yg[:, t, :], ident[:, :])
                            ins.then_inc(S["yT_psum"], 1)
                            e.wait_ge(S["hT_ready"], i * 2 + 2)
                            e.matmul(ps[:, 1, :], center[:, :], hT[:, :, :].rearrange("p b t -> p (b t)"), start=True, stop=True)\
                             .then_inc(S["hc_psum"], 1)
                            e.wait_ge(S["sq_ready"], i + 1)
                            e.matmul(ps[:, 2, :], mean[:, :], SQ[:, :], start=True, stop=True).then_inc(S["var_psum"], 1)
                        e.wait_ge(S["w1_scaled"], 1)
                        e.wait_ge(S["hn_ready"], NG)
                        with e.Fori(0, NG) as i:
                            hn = HN[:, bass.ds(i * G, G), :].rearrange("p b t -> p (b t)")
                            e.wait_ge(S["hg_ready"], i * 3)
                            for n, (o, m) in enumerate(HCH):
                                if n >= 2:
                                    e.wait_ge(S["hg_ready"], i * 3 + n - 1)
                                e.matmul(ps[0:m, 4 + n % 2, :], W1G[:, HID + o:HID + o + m], hn, start=True, stop=True).then_inc(S["g_psum"], 1)
                                e.matmul(ps[0:m, 2 + n % 2, :], W1G[:, o:o + m], hn, start=True, stop=True).then_inc(S["a_psum"], 1)
                            e.wait_ge(S["hg_ready"], i * 3 + 3)
                            e.wait_ge(S["y_ready"], i)
                            for t in range(TG):
                                for n, (o, m) in enumerate(HCH):
                                    r = 114
                                    ins = e.matmul(ps[:, 6, t * P:(t + 1) * P], HG[0:r, n, t * P:(t + 1) * P], W2[0:r, n, :],
                                                   start=(n == 0), stop=(n == 2))
                            ins.then_inc(S["o_psum"], 1)

        def state_space():
            c = ExitStack()
            with c:
                def tb(name, shape, dt=F32):
                    return c.enter_context(nc.sbuf_tensor(name, shape, dt))
                G, TG = 2, 2 * TPB
                NG = BATCH // G
                T = G * SEQ
                Win, Wx = tb("m_win", [P, 2 * DIN]), tb("m_wx", [P, CH, DTR + 2 * NST])
                Wdt, Wout = tb("m_wdt", [DTR, DIN]), tb("m_wout", [P, CH, DIM])
                cw, cb, bdt = tb("m_cw", [P, CH, NCONV]), tb("m_cb", [P, CH]), tb("m_bdt", [P, CH])
                A, D = tb("m_A", [P, CH, NST]), tb("m_D", [P, CH])
                U = tb("m_u", [P, CH, BATCH, SEQ])
                ZS = tb("m_z", [P, CH, BATCH, SEQ])
                DT = tb("m_dt", [P, CH, BATCH, SEQ])
                BC = tb("m_bc", [2 * NST, BATCH, SEQ])
                names = ("w_in xn_ready xT_psum xT_ready in_psum xb_ready z_ready tap conv_ready u_ready dbl_psum dl_ready bc_ready "
                         "dt_psum dt_ready padded").split()
                S = {n: sem("m_" + n) for n in names}
                c1 = ExitStack()
                with c1:
                    xn, xT = c1.enter_context(nc.sbuf_tensor("m_xn", [P, TG, P], F32)), c1.enter_context(nc.sbuf_tensor("m_xT", [P, T], F32))
                    XB = c1.enter_context(nc.sbuf_tensor("m_xb", [P, CH, G, SEQ + NCONV - 1], F32))
                    CV = c1.enter_context(nc.sbuf_tensor("m_cv", [P, CH, G, SEQ], F32))
                    DL = c1.enter_context(nc.sbuf_tensor("m_dl", [DTR, T], F32))
                    with nc.Block() as block:
                        @block.sync
                        def _(e):
                            e.dma_start(Win[:, :], d["w_in"]).then_inc(S["w_in"], 16)
                            e.dma_start(Wx[:, :, :], d["w_x"].rearrange("(c p) n -> p c n", p=P)).then_inc(S["w_in"], 16)
                            e.dma_start(Wdt[:, :], d["w_dt"]).then_inc(S["w_in"], 16)
                            e.dma_start(Wout[:, :, :], d["w_out"].rearrange("(c p) n -> p c n", p=P)).then_inc(S["w_in"], 16)
                            e.dma_start(cw[:, :, :], d["conv_w"].rearrange("(c p) n -> p c n", p=P)).then_inc(S["w_in"], 16)
                            e.dma_start(A[:, :, :], d["a_log"].rearrange("(c p) n -> p c n", p=P)).then_inc(S["w_in"], 16)
                            for tile, name in ((cb, "conv_b"), (bdt, "b_dt"), (D, "d_skip")):
                                e.dma_start(tile[:, :], d[name]).then_inc(S["w_in"], 16)
                            e.wait_ge(S["w_in"], 144)

                        @block.gpsimd
                        def _(e):
                            e.memset(XB[:, :, :, 0:NCONV - 1], 0.0).then_inc(S["padded"], 1)

                        @block.scalar
                        def _(e):
                            e.preload_act_table_set("silu_and_others")
                            e.wait_ge(S["w_in"], 144)
                            with e.Fori(0, NG) as i:
                                wait_alone(e, S["xT_psum"], i)
                                for t in range(TG):
                                    k = bass.ds(i * TG + t, 1)
                                    e.activation(xn[:, t, :], flat(X[:, k, :]), ACT.Identity, scale=RSTD[:, k], bias=NMR[:, k])\
                                     .then_inc(S["xn_ready"], 1)
                                for ch in range(CH):
                                    e.wait_ge(S["in_psum"], i * 2 * CH + ch + 1)
                                    e.wait_ge(S["conv_ready"], i * CH + ch)
                                    e.activation(XB[:, ch, :, NCONV - 1:], ps[:, 1 + ch, :].rearrange("p (b t) -> p b t", b=G), ACT.Copy)\
                                     .then_inc(S["xb_ready"], 1)
                                for ch in range(CH):
                                    wait_alone(e, S["in_psum"], i * 2 * CH + CH + ch + 1)
                                    e.activation(ZS[:, ch, bass.ds(i * G, G), :].rearrange("p b t -> p (b t)"), ps[:, 3 + ch, :], ACT.Silu)\
                                     .then_inc(S["z_ready"], 1)
                                for ch in range(CH):
                                    wait_alone(e, S["conv_ready"], i * CH + ch + 1)
                                    e.activation(U[:, ch, bass.ds(i * G, G), :].rearrange("p b t -> p (b t)"),
                                                 CV[:, ch, :, :].rearrange("p b t -> p (b t)"), ACT.Silu, bias=cb[:, ch:ch + 1])\
                                     .then_inc(S["u_ready"], 1)
                                e.wait_ge(S["dbl_psum"], i + 1)
                                e.activation(DL[:, :], ps[0:DTR, 5, :], ACT.Copy).then_inc(S["dl_ready"], 1)
                                e.activation(BC[:, bass.ds(i * G, G), :].rearrange("p b t -> p (b t)"), ps[0:2 * NST, 6, :], ACT.Copy)\
                                 .then_inc(S["bc_ready"], 1)
                                for ch in range(CH):
                                    wait_alone(e, S["dt_psum"], i * CH + ch + 1)
                                    e.activation(DT[:, ch, bass.ds(i * G, G), :].rearrange("p b t -> p (b t)"), ps[:, 7 * ch, :],
                                                 ACT.Identity, bias=bdt[:, ch:ch + 1]).then_inc(S["dt_ready"], 1)

                        @block.vector
                        def _(e):
                            e.wait_ge(S["padded"], 1)
                            with e.Fori(0, NG) as i:
                                e.wait_ge(S["xT_psum"], i + 1)
                                e.tensor_copy(xT[:, :], ps[:, 0, :]).then_inc(S["xT_ready"], 1)
                                for ch in range(CH):
                                    e.wait_ge(S["xb_ready"], i * CH + ch + 1)
                                    e.wait_ge(S["u_ready"], i * CH + ch)
                                    last = NCONV - 1
                                    e.tensor_scalar(CV[:, ch, :, :], XB[:, ch, :, last:last + SEQ], cw[:, ch, last:last + 1], None, ALU.mult)\
                                     .then_inc(S["tap"], 1)
                                    for k in range(last):
                                        e.wait_ge(S["tap"], i * CH * last + ch * last + k + 1)
                                        e.scalar_tensor_tensor(CV[:, ch, :, :], XB[:, ch, :, k:k + SEQ], cw[:, ch, k:k + 1], CV[:, ch, :, :],
                                                               ALU.mult, ALU.add).then_inc(S["conv_ready"] if k == last - 1 else S["tap"], 1)

                        @block.tensor
                        def _(e):
                            e.wait_ge(S["w_in"], 144)
                            with e.Fori(0, NG) as i:
                                e.wait_ge(S["dt_ready"], i * CH)
                                for t in range(TG):
                                    e.wait_ge(S["xn_ready"], i * TG + t + 1)
                                    ins = e.transpose(ps[:, 0, t * P:(t + 1) * P], xn[:, t, :], ident[:, :])
                                ins.then_inc(S["xT_psum"], 1)
                                e.wait_ge(S["xT_ready"], i + 1)
                                for n in range(2 * CH):
                                    e.matmul(ps[:, 1 + n, :], Win[:, n * P:(n + 1) * P], xT[:, :], start=True, stop=True)\
                                     .then_inc(S["in_psum"], 1)
                                e.wait_ge(S["u_ready"], i * CH + CH)
                                for lo, m, bank in ((0, DTR, 5), (DTR, 2 * NST, 6)):
                                    for ch in range(CH):
                                        ins = e.matmul(ps[0:m, bank, :], Wx[:, ch, lo:lo + m],
                                                       U[:, ch, bass.ds(i * G, G), :].rearrange("p b t -> p (b t)"), start=(ch == 0), stop=(ch == CH - 1))
                                ins.then_inc(S["dbl_psum"], 1)
                                e.wait_ge(S["dl_ready"], i + 1)
                                for ch in range(CH):
                                    e.matmul(ps[:, 7 * ch, :], Wdt[:, ch * P:(ch + 1) * P], DL[:, :], start=True, stop=True)\
                                     .then_inc(S["dt_psum"], 1)

                NQ = 4
                PIECES = [(q, ch) for q in range(NST // NQ) for ch in range(CH)]
                NPC, NBUF = len(PIECES), 2
                sel = tb("m_sel", [2 * NST, 2 * NST, P])
                BB = tb("m_bb", [P, NQ, SEQ])
                DA = tb("m_da", [P, NBUF, NQ, SEQ])
                DU = tb("m_du", [P, CH, SEQ])
                GT = tb("m_gt", [P, CH, SEQ])
                HB = Y[:, :, :].rearrange("p t d -> p (t d)").rearrange("p (k n s) -> p k n s", n=NQ, s=SEQ)
                NH = 4
                SPN = 1024
                names2 = ("sel_in a_ready zeroed abs exp ln dt_ready du_ready b_psum c_psum bb_ready da_ready dbx_ready h_ready hc_ready hc_used "
                          "skip_ready g_ready o_psum z_ready stat").split()
                R = {n: sem("s_" + n) for n in names2}
                DTf = DT[:, :, :, :].rearrange("p c b s -> p (c b s)")
                with nc.Block() as block:
                    @block.sync
                    def _(e):
                        e.dma_start(sel[:, :, :], d["select"]).then_inc(R["sel_in"], 16)
                        e.wait_ge(R["sel_in"], 16)

                    @block.gpsimd
                    def _(e):
                        e.memset(DA[:, :, :, 0:1], 0.0).then_inc(R["zeroed"], 1)
                        with e.Fori(0, BATCH) as i:
                            for k, (q, ch) in enumerate(PIECES):
                                if q == 0:
                                    e.wait_ge(R["du_ready"], i * CH + ch + 1)
                                if ch == 0:
                                    e.wait_ge(R["bb_ready"], i * (NPC // CH) + q + 1)
                                if k >= NH:
                                    e.wait_ge(R["hc_used"], i * NPC + k - NH + 1)
                                else:
                                    e.wait_ge(R["hc_used"], i * NPC)
                                e.tensor_tensor(HB[:, k % NH, :, :], BB[:, :, :],
                                                DU[:, ch, :].unsqueeze(1).to_broadcast([P, NQ, SEQ]), ALU.mult).then_inc(R["dbx_ready"], 1)
                            for ch in range(CH):
                                e.wait_ge(R["skip_ready"], i * CH + ch + 1)
                                e.tensor_tensor(GT[:, ch, :], GT[:, ch, :], ZS[:, ch, bass.ds(i, 1), :].rearrange("p a s -> p (a s)"), ALU.mult)\
                                 .then_inc(R["g_ready"], 1)

                    @block.scalar
                    def _(e):
                        e.preload_act_table_set("natural_log_exp_and_others")
                        e.activation(A[:, :, :], A[:, :, :], ACT.Exp).then_inc(R["a_ready"], 1)
                        e.wait_ge(R["a_ready"], 1)
                        e.activation(A[:, :, :], A[:, :, :], ACT.Copy, scale=-1.0).then_inc(R["a_ready"], 1)
                        with e.Fori(0, CH * BATCH * SEQ // SPN) as i:
                            wait_alone(e, R["dt_ready"], i)
                            tmp = BB[:, :, :].rearrange("p n s -> p (n s)")
                            e.activation(tmp, DTf[:, bass.ds(i * SPN, SPN)], ACT.Abs).then_inc(R["abs"], 1)
                            e.wait_ge(R["abs"], i + 1)
                            e.activation(tmp, tmp, ACT.Exp, scale=-1.0).then_inc(R["exp"], 1)
                            e.wait_ge(R["exp"], i + 1)
                            e.activation(tmp, tmp, ACT.Ln, bias=1.0).then_inc(R["ln"], 1)
                        e.wait_ge(R["a_ready"], 2)
                        e.wait_ge(R["zeroed"], 1)
                        e.wait_ge(R["dt_ready"], CH * BATCH * SEQ // SPN)
                        with e.Fori(0, BATCH) as i:
                            for k, (q, ch) in enumerate(PIECES):
                                if ch == 0:
                                    e.wait_ge(R["b_psum"], i * (NPC // CH) + q + 1)
                                    e.wait_ge(R["dbx_ready"], i * NPC + k)
                                    e.activation(BB[:, :, :].rearrange("p n s -> p (n s)"), ps[:, 0:2, :].rearrange("p a n -> p (a n)"), ACT.Copy)\
                                     .then_inc(R["bb_ready"], 1)
                                if k >= NBUF:
                                    wait_alone(e, R["h_ready"], i * NPC + k - NBUF + 1)
                                else:
                                    wait_alone(e, R["h_ready"], i * NPC)
                                for n in range(NQ):
                                    e.activation(DA[:, k % NBUF, n, 1:SEQ], DT[:, ch, bass.ds(i, 1), 1:SEQ].rearrange("p a s -> p (a s)"), ACT.Exp,
                                                 scale=A[:, ch, q * NQ + n:q * NQ + n + 1]).then_inc(R["da_ready"], 1)
                            wait_alone(e, R["o_psum"], i + 1)
                            e.activation(flat(Z[:, bass.ds(i * TPB, TPB), :]), ps[:, 7, SEQ:2 * SEQ], ACT.Copy).then_inc(R["z_ready"], 1)

                    @block.vector
                    def _(e):
                        with e.Fori(0, CH * BATCH * SEQ // SPN) as i:
                            e.wait_ge(R["ln"], i + 1)
                            v = DTf[:, bass.ds(i * SPN, SPN)]
                            e.scalar_tensor_tensor(v, v, 0.0, BB[:, :, :].rearrange("p n s -> p (n s)"), ALU.max, ALU.add).then_inc(R["dt_ready"], 1)
                        e.wait_ge(R["dt_ready"], CH * BATCH * SEQ // SPN)
                        with e.Fori(0, BATCH) as i:
                            for ch in range(CH):
                                e.wait_ge(R["dbx_ready"], i * NPC)
                                e.tensor_tensor(DU[:, ch, :], DT[:, ch, bass.ds(i, 1), :].rearrange("p a s -> p (a s)"),
                                                U[:, ch, bass.ds(i, 1), :].rearrange("p a s -> p (a s)"), ALU.mult).then_inc(R["du_ready"], 1)
                            for k, (q, ch) in enumerate(PIECES):
                                e.wait_ge(R["dbx_ready"], i * NPC + k + 1)
                                e.wait_ge(R["da_ready"], i * NPC * NQ + (k + 1) * NQ)
                                hb = HB[:, k % NH, :, :].rearrange("p n s -> p (n s)")
                                e.tensor_tensor_scan(hb, DA[:, k % NBUF, :, :].rearrange("p n s -> p (n s)"), hb, 0.0, ALU.mult, ALU.add)\
                                 .then_inc(R["h_ready"], 1)
                                e.wait_ge(R["h_ready"], i * NPC + k + 1)
                                e.wait_ge(R["c_psum"], i * (NPC // CH) + q + 1)
                                cb0 = 2 + 2 * (q % 2)
                                e.tensor_tensor(hb, ps[:, cb0:cb0 + 2, :].rearrange("p a n -> p (a n)"), hb, ALU.mult).then_inc(R["hc_ready"], 1)
                            e.wait_ge(R["hc_used"], i * NPC + NPC)
                            e.wait_ge(R["g_ready"], i * CH)
                            e.wait_ge(R["o_psum"], i)
                            for ch in range(CH):
                                e.scalar_tensor_tensor(GT[:, ch, :], U[:, ch, bass.ds(i, 1), :].rearrange("p a s -> p (a s)"), D[:, ch:ch + 1],
                                                       ps[:, 6 + ch, 0:SEQ], ALU.mult, ALU.add).then_inc(R["skip_ready"], 1)
                            wait_alone(e, R["z_ready"], i + 1)
                            for t in range(TPB):
                                k = bass.ds(i * TPB + t, 1)
                                e.bn_stats(flat(STAT[:, k, :]), flat(Z[:, k, :])).then_inc(R["stat"], 1)

                    @block.tensor
                    def _(e):
                        e.wait_ge(R["sel_in"], 16)
                        with e.Fori(0, BATCH) as i:
                            bc = BC[:, bass.ds(i, 1), :].rearrange("p a s -> p (a s)")

                            def spread(q):
                                wait_alone(e, R["bb_ready"], i * (NPC // CH) + q)
                                for n in range(NQ):
                                    ins = e.matmul(ps[:, n // 2, n % 2 * SEQ:(n % 2 + 1) * SEQ], sel[:, q * NQ + n, :], bc, start=True, stop=True)
                                ins.then_inc(R["b_psum"], 1)
                                if q >= 2:
                                    wait_alone(e, R["hc_ready"], i * NPC + CH * (q - 1))
                                else:
                                    wait_alone(e, R["hc_ready"], i * NPC)
                                for n in range(NQ):
                                    ins = e.matmul(ps[:, 2 + 2 * (q % 2) + n // 2, n % 2 * SEQ:(n % 2 + 1) * SEQ], sel[:, NST + q * NQ + n, :], bc,
                                                   start=True, stop=True)
                                ins.then_inc(R["c_psum"], 1)
                            spread(0)
                            e.wait_ge(R["z_ready"], i)
                            e.wait_ge(R["skip_ready"], i * CH)
                            for k, (q, ch) in enumerate(PIECES):
                                if ch == 0 and q + 1 < NST // NQ:
                                    spread(q + 1)
                                e.wait_ge(R["hc_ready"], i * NPC + k + 1)
                                for n in range(NQ):
                                    ins = e.matmul(ps[:, 6 + ch, 0:SEQ], ident[:, :], HB[:, k % NH, n, :], start=(q == 0 and n == 0),
                                                   stop=(q == NST // NQ - 1 and n == NQ - 1))
                                ins.then_inc(R["hc_used"], 1)
                            e.wait_ge(R["g_ready"], i * CH + CH)
                            for t in range(TPB):
                                for ch in range(CH):
                                    ins = e.matmul(ps[:, 7, SEQ + t * P:SEQ + (t + 1) * P], GT[:, ch, t * P:(t + 1) * P], Wout[:, ch, :],
                                                   start=(ch == 0), stop=(ch == CH - 1))
                            ins.then_inc(R["o_psum"], 1)

        def silu_ffn():
            c = ExitStack()
            with c:
                def tb(name, shape, dt=F32):
                    return c.enter_context(nc.sbuf_tensor(name, shape, dt))
                G, TG = 2, 2 * TPB
                NG, NCH, T = BATCH // G, HID1 // P, G * SEQ
                WI = tb("f_wi", [P, 3, HID1], I32)
                W = tb("f_w", [P, 3, HID1])
                xn, xT = tb("f_xn", [P, TG, P]), tb("f_xT", [P, T])
                SG, H = tb("f_sg", [P, NCH, T]), tb("f_h", [P, NCH, T])
                names = "w_in w_float w_ready xn_ready xT_psum xT_ready g_psum u_psum sg_ready h_ready o_psum z_ready stat".split()
                S = {n: sem("f_" + n) for n in names}
                with nc.Block() as block:
                    @block.sync
                    def _(e):
                        e.dma_start(WI[:, 0, :], d["wg"]).then_inc(S["w_in"], 16)
                        e.dma_start(WI[:, 1, :], d["wu"]).then_inc(S["w_in"], 16)
                        e.dma_start(WI[:, 2, :].rearrange("p (c n) -> p c n", c=NCH), d["wd"].rearrange("(c p) n -> p c n", p=P))\
                         .then_inc(S["w_in"], 16)
                        e.wait_ge(S["w_in"], 48)

                    @block.scalar
                    def _(e):
                        e.preload_act_table_set("silu_and_others")
                        with e.Fori(0, NG) as i:
                            wait_alone(e, S["xT_psum"], i)
                            for t in range(TG):
                                k = bass.ds(i * TG + t, 1)
                                e.activation(xn[:, t, :], flat(X[:, k, :]), ACT.Identity, scale=RSTD[:, k], bias=NMR[:, k])\
                                 .then_inc(S["xn_ready"], 1)
                            for n in range(NCH):
                                e.wait_ge(S["g_psum"], i * NCH + n + 1)
                                e.wait_ge(S["h_ready"], i * NCH + n)
                                e.activation(SG[:, n, :], ps[:, 1 + 2 * (n % 2), :], ACT.Silu).then_inc(S["sg_ready"], 1)
                            wait_alone(e, S["o_psum"], i + 1)
                            e.activation(flat(Z[:, bass.ds(i * TG, TG), :]), ps[:, 5, :], ACT.Copy).then_inc(S["z_ready"], 1)

                    @block.vector
                    def _(e):
                        e.wait_ge(S["w_in"], 48)
                        e.tensor_copy(W[:, :, :].rearrange("p a n -> p (a n)"), WI[:, :, :].rearrange("p a n -> p (a n)")).then_inc(S["w_float"], 1)
                        e.wait_ge(S["w_float"], 1)
                        wf = W[:, :, :].rearrange("p a n -> p (a n)")
                        e.tensor_scalar(wf, wf, float(np.float32(1.0 / 127.0)), None, ALU.mult).then_inc(S["w_ready"], 1)
                        with e.Fori(0, NG) as i:
                            e.wait_ge(S["xT_psum"], i + 1)
                            e.tensor_copy(xT[:, :], ps[:, 0, :]).then_inc(S["xT_ready"], 1)
                            e.wait_ge(S["o_psum"], i)
                            for n in range(NCH):
                                e.wait_ge(S["u_psum"], i * NCH + n + 1)
                                e.wait_ge(S["sg_ready"], i * NCH + n + 1)
                                e.tensor_tensor(H[:, n, :], ps[:, 2 + 2 * (n % 2), :], SG[:, n, :], ALU.mult).then_inc(S["h_ready"], 1)
                            wait_alone(e, S["z_ready"], i + 1)
                            for t in range(TG):
                                k = bass.ds(i * TG + t, 1)
                                e.bn_stats(flat(STAT[:, k, :]), flat(Z[:, k, :])).then_inc(S["stat"], 1)

                    @block.tensor
                    def _(e):
                        e.wait_ge(S["w_ready"], 1)
                        with e.Fori(0, NG) as i:
                            for t in range(TG):
                                e.wait_ge(S["xn_ready"], i * TG + t + 1)
                                ins = e.transpose(ps[:, 0, t * P:(t + 1) * P], xn[:, t, :], ident[:, :])
                            ins.then_inc(S["xT_psum"], 1)
                            e.wait_ge(S["xT_ready"], i + 1)
                            for n in range(NCH):
                                if n >= 2:
                                    e.wait_ge(S["h_ready"], i * NCH + n - 1)
                                else:
                                    e.wait_ge(S["h_ready"], i * NCH)
                                e.matmul(ps[:, 1 + 2 * (n % 2), :], W[:, 0, n * P:(n + 1) * P], xT[:, :], start=True, stop=True).then_inc(S["g_psum"], 1)
                                e.matmul(ps[:, 2 + 2 * (n % 2), :], W[:, 1, n * P:(n + 1) * P], xT[:, :], start=True, stop=True).then_inc(S["u_psum"], 1)
                            e.wait_ge(S["h_ready"], i * NCH + NCH)
                            e.wait_ge(S["z_ready"], i)
                            for t in range(TG):
                                for n in range(NCH):
                                    ins = e.matmul(ps[:, 5, t * P:(t + 1) * P], H[:, n, t * P:(t + 1) * P], W[:, 2, n * P:(n + 1) * P],
                                                   start=(n == 0), stop=(n == NCH - 1))
                            ins.then_inc(S["o_psum"], 1)

        with stage():
            norm_stats("n0", X, True)
            attention()
            norm_stats("n1", Z, False)
            add_normed("n1", Z)
            norm_stats("n2", X, True)
            make_y()
        if stop >= 2:
            for l in range(DEPTH):
                with stage():
                    window_attention(l)
                    gelu_ffn(l)
            with stage():
                norm_stats("n3", Y, True)
                add_normed("n3", Y)
                norm_stats("n4", X, True)
        if stop >= 3:
            with stage():
                state_space()
                norm_stats("n5", Z, False)
                add_normed("n5", Z)
                norm_stats("n6", X, True)
        if stop >= 4:
            with stage():
                silu_ffn()
                norm_stats("n7", Z, False)
                add_normed("n7", Z)
        with stage():
            store()


CONST = ["rope", "dist", "headmask", "onesmask", "xpos", "wmask"]


def kernel(**inputs):
    import numpy as _np
    import concourse.bacc as _bacc
    from concourse import mybir as _mybir
    from concourse.bass_utils import run_bass_kernel_spmd as _run

    v = {k: _np.asarray(a) for k, a in inputs.items()}
    swap = _np.arange(DIM) ^ 1
    feed = {
        "x": v["L0_attn_x"], "wq": v["L0_attn_Wq"].T, "wqr": v["L0_attn_Wq"][swap].T, "wk": v["L0_attn_Wk"].T,
        "wqkv": v["L0_ffn_wqkv"], "qs": v["L0_ffn_q_scale"], "ks": v["L0_ffn_k_scale"], "wo": v["L0_ffn_wo"],
        "lg": v["L0_ffn_ln_g"], "lb": v["L0_ffn_ln_b"], "w1": v["L0_ffn_w1"], "b1": v["L0_ffn_b1"],
        "w2b": _np.concatenate([v["L0_ffn_w2"], v["L0_ffn_b2"][:, None, :]], 1),
        "w_in": v["L1_attn_W_in"], "w_x": v["L1_attn_W_x"], "w_dt": v["L1_attn_W_dt"], "w_out": v["L1_attn_W_out"],
        "conv_w": v["L1_attn_conv_w"], "a_log": v["L1_attn_A_log"],
        "conv_b": v["L1_attn_conv_b"].reshape(CH, P).T, "b_dt": v["L1_attn_b_dt"].reshape(CH, P).T,
        "d_skip": v["L1_attn_D"].reshape(CH, P).T,
        "wg": v["L1_ffn_w_gate"].T, "wu": v["L1_ffn_w_up"].T, "wd": v["L1_ffn_w_down"].T,
        "wkr": v["L0_attn_Wk"][swap].T, "wv": v["L0_attn_Wv"].T, "wo0": v["L0_attn_Wo"].T,
        **shape_constants(),
    }
    nc = _bacc.Bacc("TRN2", target_bir_lowering=False, num_devices=1)
    arrays, aps = {}, {}
    for name, a in feed.items():
        a = _np.ascontiguousarray(a)
        arrays["in_" + name] = a
        aps[name] = nc.dram_tensor("in_" + name, a.shape, _mybir.dt.from_np(a.dtype), kind="ExternalInput").ap()
    y = nc.dram_tensor("out_x", (BATCH, SEQ, DIM), _mybir.dt.float32, kind="ExternalOutput").ap()
    build(nc, aps, y)
    r = _run(nc, [arrays], core_ids=[0])
    return r.results[0]["out_x"]
```

```python
import numpy as np
from contextlib import ExitStack, contextmanager

import concourse.bass as bass
from concourse import mybir

F32 = mybir.dt.float32
I32 = mybir.dt.int32
F32R = mybir.dt.float32r
ALU = mybir.AluOpType
ACT = mybir.ActivationFunctionType
AX = mybir.AxisListType

P = 128
BATCH, SEQ, DIM = 16, 256, 128
TPB = SEQ // P
NT = BATCH * TPB
LN_EPS = 1e-5
LEN_SCALE = 2.0 ** 8

AH, ADK = 16, 8
AG = 4
DEPTH, FH, FD, WIN = 2, 8, 64, 64
INNER = FH * FD
HID = DIM * 4 * 2 // 3
HCH = [(0, 114), (114, 114), (228, 113)]
MASKED = 1e30
DIN, NST, DTR, NCONV = 256, 16, 64, 4
CH = DIN // P
HID1 = 384


def shape_constants():
    f = np.float32
    pos = np.arange(SEQ, dtype=f)
    inv = (1.0 / 10000.0 ** (np.arange(0, ADK, 2, dtype=f) / ADK)).astype(f)
    fr = (pos[:, None] * inv[None, :]).astype(f)
    sin = np.repeat(np.sin(fr), 2, axis=-1).T
    cos = np.repeat(np.cos(fr), 2, axis=-1).T
    sign = np.where(np.arange(ADK) % 2 == 0, -1.0, 1.0)[:, None]
    slopes = 2.0 ** (-8.0 * np.arange(AH, dtype=np.float64) / AH)
    qs = np.repeat(-1.0 / (np.sqrt(ADK) * slopes), ADK)[:, None]
    cosr, sinr = np.tile(cos, (AH, 1)), np.tile(sin * sign, (AH, 1))
    rope = np.stack([cosr * qs, sinr * qs, cosr, sinr], 1).astype(f)
    dist = np.abs(pos[:, None] - pos[None, :]).reshape(TPB, P, SEQ).transpose(1, 0, 2).astype(f)
    copies = np.zeros((P, 4, 4, P), f)
    for s in range(4):
        for r in range(AG):
            for n, stacks in enumerate(((0, 2), (1, 3), (0, 1), (2, 3))):
                for c in stacks:
                    for x in range(ADK):
                        copies[(4 * s + r) * ADK + x, s, n, 32 * r + 8 * c + x] = 1.0
    ones = np.zeros((P, AG, 32), f)
    for j in range(AG):
        ones[:, j, j * ADK:(j + 1) * ADK] = 1.0

    half = np.arange(0, FD, 2, dtype=f)
    finv = (1.0 / 10000.0 ** (half / FD)).astype(f)
    ff = (pos[:, None] * finv[None, :]).astype(f)
    ff = np.concatenate([ff, ff], -1)
    base = (half + f(0.4 * FD)) / f(1.4 * FD)
    power = (pos - SEQ // 2) / f(WIN // 2)
    sc = (base[None, :] ** power[:, None]).astype(f)
    sc = np.concatenate([sc, sc], -1).astype(np.float64)
    s2 = np.where(np.arange(FD) < FD // 2, -1.0, 1.0)
    c64, s64 = np.cos(ff).astype(np.float64), np.sin(ff).astype(np.float64)
    xpos = np.stack([c64 * sc * -8.0, s64 * sc * s2 * -8.0, c64 / sc, s64 / sc * s2], 1) * LEN_SCALE
    xpos = xpos.reshape(TPB, P, 4, FD).transpose(1, 0, 2, 3).astype(f)
    wmask = np.full((P, TPB, 192), MASKED, f)
    for t in range(TPB):
        first = 0 if t == 0 else t * P - WIN
        i = np.arange(P)[:, None] + t * P
        j = np.arange(192)[None, :] + first
        wmask[:, t] = np.where((j <= i) & (j >= i - WIN), 0.0, MASKED)
    center = (np.eye(P) - 1.0 / P).astype(f)
    select = np.concatenate([np.eye(2 * NST, dtype=f)] * 2)
    return {"center": center, "select": select, "rope": rope, "dist": dist, "copies": copies, "onesmask": ones, "xpos": xpos, "wmask": wmask}


def flat(ap):
    return ap.rearrange("p a c -> p (a c)")


def build(nc, d, out, stop=99):
    ctx = ExitStack()
    names = {}

    def sb(name, shape, dt=F32):
        return ctx.enter_context(nc.sbuf_tensor(name, shape, dt))

    stage_semaphores = []

    def sem(name):
        stage_semaphores[-1].append(nc.alloc_semaphore(name=name))
        return stage_semaphores[-1][-1]

    @contextmanager
    def stage():
        stage_semaphores.append([])
        yield
        nc.clear_and_free_semaphores(stage_semaphores.pop())
        nc.all_engine_barrier()

    with ctx:
        X = sb("X", [P, NT, DIM])
        Z = sb("Z", [P, NT, DIM])
        Y = sb("Y", [P, NT, DIM])
        STAT = sb("STAT", [P, NT, 6])
        RSTD = sb("RSTD", [P, NT])
        NMR = sb("NMR", [P, NT])
        EPS = sb("EPS", [P, 2])
        ident = sb("ident", [P, P])
        ps = ctx.enter_context(nc.psum_tensor("ps", [P, 8, 512], F32))

        xv = d["x"].rearrange("b (t p) d -> p (b t) d", p=P)
        ov = out.rearrange("b (t p) d -> p (b t) d", p=P)

        x_in = nc.alloc_semaphore(name="x_in")

        passed = {}

        def wait_alone(e, semaphore, value):
            if e.engine not in passed:
                passed[e.engine] = nc.alloc_semaphore(name=f"passed_{len(passed)}")
            e.wait_ge(semaphore, value)
            e.sem_inc(passed[e.engine], 1)

        with stage(), nc.Block() as block:
            ident_zero, ident_made = sem("ident_zero"), sem("ident_made")

            @block.sync
            def _(e):
                e.dma_start(X[:, :, :], xv).then_inc(x_in, 16)
                e.wait_ge(x_in, 16)

            @block.gpsimd
            def _(e):
                e.memset(ident[:, :], 0.0).then_inc(ident_zero, 1)
                e.memset(EPS[:, 0:1], LN_EPS)
                e.memset(EPS[:, 1:2], 1e-24)
                e.wait_ge(ident_zero, 1)
                e.affine_select(out=ident[:, :], in_=ident[:, :], compare_op=ALU.not_equal, fill=1.0,
                                base=0, pattern=[[-1, P]], channel_multiplier=1).then_inc(ident_made, 1)

        def norm_stats(tag, src, count):
            sq, tmp = names["small"][:, 0:NT], names["small"][:, NT:2 * NT]
            s_sum, s_rstd = sem(tag + "_moments"), sem(tag + "_rstd")
            s_link = sem(tag + "_link")
            with nc.Block() as block:
                @block.vector
                def _(e):
                    if count:
                        with e.Fori(0, NT // 4) as i:
                            for t in range(4):
                                e.bn_stats(STAT[:, bass.ds(i * 4 + t, 1), :].rearrange("p a c -> p (a c)"),
                                           src[:, bass.ds(i * 4 + t, 1), :].rearrange("p a c -> p (a c)")).then_inc(s_link, 1)
                        e.wait_ge(s_link, NT)
                    base = NT if count else 0
                    e.tensor_tensor(tmp, STAT[:, :, 1], STAT[:, :, 4], ALU.subtract).then_inc(s_link, 1)
                    e.tensor_tensor(sq, STAT[:, :, 2], STAT[:, :, 5], ALU.add).then_inc(s_link, 1)
                    e.tensor_tensor(NMR[:, :], STAT[:, :, 1], STAT[:, :, 4], ALU.add).then_inc(s_link, 1)
                    e.wait_ge(s_link, base + 3)
                    e.tensor_tensor(tmp, tmp, tmp, ALU.mult).then_inc(s_link, 1)
                    e.wait_ge(s_link, base + 4)
                    e.scalar_tensor_tensor(tmp, tmp, DIM / 4.0, sq, ALU.mult, ALU.add).then_inc(s_sum, 1)
                    e.wait_ge(s_rstd, 2)
                    e.scalar_tensor_tensor(NMR[:, :], NMR[:, :], -0.5, RSTD[:, :], ALU.mult, ALU.mult)

                @block.scalar
                def _(e):
                    e.preload_act_table_set("natural_log_exp_and_others")
                    e.wait_ge(s_sum, 1)
                    e.activation(sq, tmp, ACT.Ln, scale=1.0 / DIM, bias=EPS[:, 0:1]).then_inc(s_rstd, 1)
                    e.wait_ge(s_rstd, 1)
                    e.activation(RSTD[:, :], sq, ACT.Exp, scale=-0.5).then_inc(s_rstd, 1)

        small = sb("small", [P, 2 * NT])
        names["small"] = small

        def add_normed(tag, Z):
            s_t, s_x = sem(tag + "_normed"), sem(tag + "_added")
            with nc.Block() as block:
                @block.scalar
                def _(e):
                    with e.Fori(0, NT // 4) as i:
                        for t in range(4):
                            k = bass.ds(i * 4 + t, 1)
                            e.activation(Z[:, k, :].rearrange("p a c -> p (a c)"), Z[:, k, :].rearrange("p a c -> p (a c)"),
                                         ACT.Identity, scale=RSTD[:, k], bias=NMR[:, k]).then_inc(s_t, 1)

                @block.vector
                def _(e):
                    with e.Fori(0, NT // 4) as i:
                        e.wait_ge(s_t, i * 4 + 4)
                        k = bass.ds(i * 4, 4)
                        e.tensor_tensor(X[:, k, :], X[:, k, :], Z[:, k, :], ALU.add).then_inc(s_x, 1)

        def store():
            s_out = sem("stored")
            with nc.Block() as block:
                @block.sync
                def _(e):
                    e.dma_start(ov, X[:, :, :]).then_inc(s_out, 16)
                    e.wait_ge(s_out, 16)

        def attention():
            with ExitStack() as c:
                def tb(name, shape, dt=F32):
                    return c.enter_context(nc.sbuf_tensor(name, shape, dt))
                W = tb("a_w", [P, 6, P])
                rope = tb("a_rope", [P, 4, SEQ])
                dist = tb("a_dist", [P, TPB, SEQ])
                onesm = tb("a_ones", [P, AG, 32])
                copies_in = tb("a_copies_in", [P, 4, 4, P])
                copies = tb("a_copies", [P, 4, 4, P], F32R)
                xn = tb("a_xn", [P, TPB, P])
                xT = tb("a_xT", [P, SEQ])
                rot = tb("a_rot", [P, 2, 2, SEQ])
                QK = tb("a_qk", [P, 2, SEQ])
                QKh, QKl = tb("a_qk_high", [P, 2, SEQ], F32R), tb("a_qk_low", [P, 2, SEQ], F32R)
                QKX = tb("a_qkx", [P, 2, 4, 2, SEQ], F32R)
                VM = tb("a_VM", [P, 2, TPB, AG, AG, 32])
                NSB = NPT = 4
                SBS = tb("a_scores", [P, NSB, 2, SEQ])
                PR = tb("a_probs", [P, NSB, 2, SEQ])
                PT = tb("a_probsT", [P, NPT, 2, TPB, P])
                MN = tb("a_min", [P, 2, 32])
                RS = tb("a_rsum", [P, SEQ])
                OT = tb("a_oT", [P, SEQ])
                names = ("w_in copies_ready vm_zero xn_ready xT_psum xT_ready q_psum k_psum v_psum rot_q rot_k qk_ready "
                         "high_ready low_ready vm_ready x_psum x_ready s_psum s_moved p_ready pT_psum pT_even pT_odd pv_done "
                         "rs_ready oT_ready z_psum z_ready stat_done").split()
                S = {n: sem("a_" + n) for n in names}
                pairs = [(qt, r, sp) for qt in range(TPB) for r in range(AG) for sp in range(2)]
                NPAIR, NQUAD = len(pairs), len(pairs) // 2
                SBANK, TBANK, OBANK, XBANK = 0, 2, 4, 6

                def past(e, semaphore, value):
                    if not (isinstance(value, int) and value <= 0):
                        e.wait_ge(semaphore, value)

                def sequences(prepare, attend, finish, prepare_first):
                    def both(i, u, before, ahead):
                        for step in range(NPAIR):
                            if ahead is not None and prepare_first:
                                prepare(ahead, 1 - u, step)
                            attend(i, u, step, before)
                            if ahead is not None and not prepare_first:
                                prepare(ahead, 1 - u, step)
                    for step in range(NPAIR):
                        prepare(0, 0, step)
                    both(0, 0, None, 1)
                    return both

                def run(e, prepare, attend, finish, prepare_first=False):
                    both = sequences(prepare, attend, finish, prepare_first)
                    with e.Fori(0, BATCH // 2 - 1) as k:
                        both(2 * k + 1, 1, 2 * k, 2 * k + 2)
                        both(2 * k + 2, 0, 2 * k + 1, 2 * k + 3)
                    both(BATCH - 1, 1, BATCH - 2, None)
                    for step in range(NPAIR):
                        finish(BATCH - 1, 1, step)

                with nc.Block() as block:
                    @block.sync
                    def _(e):
                        for n, name in enumerate(["wq", "wqr", "wk", "wkr", "wv", "wo0"]):
                            e.dma_start(W[:, n, :], d[name]).then_inc(S["w_in"], 16)
                        e.dma_start(rope[:, :, :], d["rope"]).then_inc(S["w_in"], 16)
                        e.dma_start(dist[:, :, :], d["dist"]).then_inc(S["w_in"], 16)
                        e.dma_start(onesm[:, :, :], d["onesmask"]).then_inc(S["w_in"], 16)
                        e.dma_start(copies_in[:, :, :, :], d["copies"]).then_inc(S["w_in"], 16)
                        e.wait_ge(S["w_in"], 160)

                    @block.gpsimd
                    def _(e):
                        e.memset(VM[:, :, :, :, :, :], 0.0).then_inc(S["vm_zero"], 1)

                        def halves(i):
                            past(e, S["low_ready"], i)
                            for n, s in enumerate(("rot_q", "rot_k")):
                                e.wait_ge(S[s], i + 1)
                                e.tensor_tensor(QK[:, n, :], rot[:, n, 0, :], rot[:, n, 1, :], ALU.add).then_inc(S["qk_ready"], 1)
                        halves(0)
                        with e.Fori(1, BATCH) as i:
                            halves(i)

                    @block.scalar
                    def _(e):
                        e.wait_ge(S["vm_zero"], 1)

                        def prepare(i, u, step):
                            if step == 0:
                                if not (isinstance(i, int) and i == 0):
                                    wait_alone(e, S["xT_psum"], i)
                                for t in range(TPB):
                                    k = bass.ds(i * TPB + t, 1)
                                    e.activation(xn[:, t, :], flat(X[:, k, :]), ACT.Identity, scale=RSTD[:, k], bias=NMR[:, k])\
                                     .then_inc(S["xn_ready"], 1)
                            if step == 5:
                                e.wait_ge(S["v_psum"], i + 1)
                                past(e, S["pv_done"], (i - 1) * NQUAD)
                                for r in range(AG):
                                    e.activation(VM[:, u, :, :, r, r * ADK:(r + 1) * ADK].rearrange("p t g c -> p (t g) c"),
                                                 ps[:, XBANK + 1, 0:SEQ].rearrange("p (tg j c) -> p tg j c", j=AG, c=ADK)[:, :, r, :],
                                                 ACT.Copy).then_inc(S["vm_ready"], 1)
                            if step == 7:
                                e.wait_ge(S["qk_ready"], i * 2 + 2)
                                past(e, S["x_psum"], i * 4)
                                e.activation(QKh[:, :, :], QK[:, :, :], ACT.Copy).then_inc(S["high_ready"], 1)
                            if step in (9, 10, 12, 13):
                                s = (9, 10, 12, 13).index(step)
                                e.wait_ge(S["x_psum"], i * 4 + s + 1)
                                past(e, S["s_psum"], (i - 1) * NPAIR)
                                e.activation(QKX[:, u, s, :, :].rearrange("p a t -> p (a t)"), ps[:, XBANK + s % 2, :], ACT.Copy)\
                                 .then_inc(S["x_ready"], 1)

                        def evac(i, p):
                            if p % 2:
                                e.wait_ge(S["pT_psum"], i * NPAIR + p + 1)
                                past(e, S["pv_done"], i * NQUAD + p // 2 - 1)
                                e.activation(PT[:, p % NPT, :, :, :].rearrange("p a b c -> p (a b c)"), ps[:, TBANK + p % 2, :],
                                             ACT.Copy).then_inc(S["pT_odd"], 1)

                        def finish(i, u, step):
                            if step < 2:
                                evac(i, NPAIR - 2 + step)
                            if step == 10:
                                wait_alone(e, S["z_psum"], i + 1)
                                e.activation(flat(Z[:, bass.ds(i * TPB, TPB), :]), ps[:, OBANK + u, 0:SEQ], ACT.Copy)\
                                 .then_inc(S["z_ready"], 1)

                        def attend(i, u, p, before):
                            past(e, S["pT_psum"], i * NPAIR + p - NSB + 1)
                            for a in range(2):
                                e.wait_ge(S["s_moved"], i * 2 * NPAIR + 2 * p + a + 1)
                                e.activation(PR[:, p % NSB, a, :], SBS[:, p % NSB, a, :], ACT.Exp, scale=-1.0,
                                             bias=MN[:, u, 2 * p + a:2 * p + a + 1]).then_inc(S["p_ready"], 1)
                            if p >= 2:
                                evac(i, p - 2)
                            if before is not None:
                                finish(before, 1 - u, p)
                        run(e, prepare, attend, finish, prepare_first=True)

                    @block.vector
                    def _(e):
                        e.wait_ge(S["w_in"], 160)
                        e.tensor_copy(copies[:, :, :, :], copies_in[:, :, :, :]).then_inc(S["copies_ready"], 1)

                        def prepare(i, u, step):
                            if step == 1:
                                e.wait_ge(S["xT_psum"], i + 1)
                                past(e, S["v_psum"], i)
                                e.tensor_copy(xT[:, :], ps[:, XBANK, 0:SEQ]).then_inc(S["xT_ready"], 1)
                            for at, n, ready, psum in ((3, 0, "rot_q", "q_psum"), (4, 1, "rot_k", "k_psum")):
                                if step == at:
                                    e.wait_ge(S[psum], i + 1)
                                    past(e, S["qk_ready"], i * 2)
                                    e.tensor_tensor(rot[:, n, :, :].rearrange("p a t -> p (a t)"), ps[:, XBANK + 1 - n, :],
                                                    rope[:, 2 * n:2 * n + 2, :].rearrange("p a t -> p (a t)"), ALU.mult).then_inc(S[ready], 1)
                            if step == 7:
                                e.wait_ge(S["high_ready"], i + 1)
                                e.tensor_tensor(QKl[:, :, :].rearrange("p a t -> p (a t)"), QK[:, :, :].rearrange("p a t -> p (a t)"),
                                                QKh[:, :, :].bitcast(F32).rearrange("p a t -> p (a t)"), ALU.subtract).then_inc(S["low_ready"], 1)

                        def evac(i, p):
                            if p % 2 == 0:
                                e.wait_ge(S["pT_psum"], i * NPAIR + p + 1)
                                past(e, S["pv_done"], i * NQUAD + p // 2 - 1)
                                e.tensor_copy(PT[:, p % NPT, :, :, :].rearrange("p a b c -> p (a b c)"), ps[:, TBANK + p % 2, :])\
                                 .then_inc(S["pT_even"], 1)

                        def finish(i, u, step):
                            if step < 2:
                                evac(i, NPAIR - 2 + step)
                            if step == 5:
                                e.wait_ge(S["pv_done"], (i + 1) * NQUAD)
                                e.reciprocal(RS[:, :], ps[:, OBANK + u, SEQ:2 * SEQ]).then_inc(S["rs_ready"], 1)
                                e.wait_ge(S["rs_ready"], i + 1)
                                past(e, S["z_psum"], i)
                                e.tensor_tensor(OT[:, :], ps[:, OBANK + u, 0:SEQ], RS[:, :], ALU.mult).then_inc(S["oT_ready"], 1)
                            if step == 12:
                                wait_alone(e, S["z_ready"], i + 1)
                                for t in range(TPB):
                                    k = bass.ds(i * TPB + t, 1)
                                    e.bn_stats(flat(STAT[:, k, :]), flat(Z[:, k, :])).then_inc(S["stat_done"], 1)

                        def attend(i, u, p, before):
                            qt, r, sp = pairs[p]
                            if not (isinstance(i, int) and i == 0 and p < NSB):
                                wait_alone(e, S["p_ready"], i * 2 * NPAIR + 2 * (p - NSB) + 2)
                            wait_alone(e, S["s_psum"], i * NPAIR + p + 1)
                            for a in range(2):
                                h = 4 * (2 * sp + a) + r
                                e.tensor_tensor_reduce(SBS[:, p % NSB, a, :], ps[:, SBANK + p % 2, a * SEQ:(a + 1) * SEQ], dist[:, qt, :],
                                                       2.0 ** (-8.0 * h / AH), 3.0e38, ALU.add, ALU.min,
                                                       accum_out=MN[:, u, 2 * p + a:2 * p + a + 1]).then_inc(S["s_moved"], 1)
                            if p >= 2:
                                evac(i, p - 2)
                            if before is not None:
                                finish(before, 1 - u, p)
                        run(e, prepare, attend, finish)

                    @block.tensor
                    def _(e):
                        e.wait_ge(S["w_in"], 160)
                        e.wait_ge(S["copies_ready"], 1)

                        def prepare(i, u, step):
                            if step == 0:
                                e.wait_ge(S["xn_ready"], i * TPB + TPB)
                                past(e, S["x_ready"], i * 4)
                                for t in range(TPB):
                                    ins = e.transpose(ps[:, XBANK, t * P:(t + 1) * P], xn[:, t, :], ident[:, :])
                                ins.then_inc(S["xT_psum"], 1)
                            if step == 2:
                                e.wait_ge(S["xT_ready"], i + 1)
                                for n in range(2):
                                    ins = e.matmul(ps[:, XBANK + 1, n * SEQ:(n + 1) * SEQ], W[:, n, :], xT[:, :], start=True, stop=True)
                                ins.then_inc(S["q_psum"], 1)
                            if step == 3:
                                for n in range(2):
                                    ins = e.matmul(ps[:, XBANK, n * SEQ:(n + 1) * SEQ], W[:, 2 + n, :], xT[:, :], start=True, stop=True)
                                ins.then_inc(S["k_psum"], 1)
                            if step == 4:
                                e.wait_ge(S["rot_q"], i + 1)
                                for t in range(TPB):
                                    ins = e.matmul(ps[:, XBANK + 1, t * P:(t + 1) * P], xT[:, t * P:(t + 1) * P], W[:, 4, :], start=True, stop=True)
                                ins.then_inc(S["v_psum"], 1)
                            if step in (8, 9, 11, 12):
                                s = (8, 9, 11, 12).index(step)
                                if s == 0:
                                    e.wait_ge(S["low_ready"], i + 1)
                                    e.wait_ge(S["rot_k"], i + 1)
                                elif s == 1:
                                    e.wait_ge(S["vm_ready"], i * AG + AG)
                                else:
                                    e.wait_ge(S["x_ready"], i * 4 + s - 1)
                                for n in range(2):
                                    for m, part in enumerate((QKh, QKl)):
                                        ins = e.matmul(ps[:, XBANK + s % 2, n * SEQ:(n + 1) * SEQ], copies[:, s, 2 * n + m, :], part[:, n, :],
                                                       start=(m == 0), stop=(m == 1))
                                ins.then_inc(S["x_psum"], 1)

                        def turn(i, p):
                            if p % 2:
                                past(e, S["pT_odd"], i * NQUAD + p // 2)
                            else:
                                past(e, S["pT_even"], i * NQUAD + p // 2)
                            e.wait_ge(S["p_ready"], i * 2 * NPAIR + 2 * p + 2)
                            for a in range(2):
                                for kb in range(TPB):
                                    at = (a * TPB + kb) * P
                                    ins = e.transpose(ps[:, TBANK + p % 2, at:at + P], PR[:, p % NSB, a, kb * P:(kb + 1) * P], ident[:, :])
                            ins.then_inc(S["pT_psum"], 1)

                        def weigh(i, u, k):
                            qt, r, _ = pairs[2 * k]
                            e.wait_ge(S["pT_even"], i * NQUAD + k + 1)
                            e.wait_ge(S["pT_odd"], i * NQUAD + k + 1)
                            if k == 0:
                                past(e, S["z_ready"], i - 1)
                                e.wait_ge(S["vm_ready"], i * AG + AG)
                            for kb in range(TPB):
                                for what in range(2):
                                    for g in range(AG):
                                        o = slice(32 * g, 32 * g + 32)
                                        at = what * SEQ + qt * P
                                        w = onesm[:, r, :] if what else VM[:, u, kb, g, r, :]
                                        ins = e.matmul(ps[o, OBANK + u, at:at + P], w, PT[:, (2 * k + g // 2) % NPT, g % 2, kb, :],
                                                       start=(k == 0 and kb == 0 and what == 0), stop=(k == NQUAD - 1 and kb == TPB - 1),
                                                       skip_group_check=True)
                            ins.then_inc(S["pv_done"], 1)

                        def finish(i, u, step):
                            if step < 2:
                                turn(i, NPAIR - 2 + step)
                            if step in (1, 3):
                                weigh(i, u, NQUAD - 2 + step // 2)
                            if step == 9:
                                e.wait_ge(S["oT_ready"], i + 1)
                                for t in range(TPB):
                                    ins = e.matmul(ps[:, OBANK + u, t * P:(t + 1) * P], OT[:, t * P:(t + 1) * P], W[:, 5, :], start=True, stop=True)
                                ins.then_inc(S["z_psum"], 1)

                        def attend(i, u, p, before):
                            qt, r, sp = pairs[p]
                            if p == 0:
                                e.wait_ge(S["x_ready"], i * 4 + 4)
                            past(e, S["s_moved"], i * 2 * NPAIR + 2 * (p - 2) + 2)
                            rows = slice(32 * r, 32 * r + 32)
                            for a in range(2):
                                ins = e.matmul(ps[:, SBANK + p % 2, a * SEQ:(a + 1) * SEQ], QKX[rows, u, 2 * sp + a, 0, qt * P:(qt + 1) * P],
                                               QKX[rows, u, 2 * sp + a, 1, :], start=True, stop=True)
                            ins.then_inc(S["s_psum"], 1)
                            if p >= 2:
                                turn(i, p - 2)
                            if p >= 5 and p % 2:
                                weigh(i, u, (p - 5) // 2)
                            if before is not None:
                                finish(before, 1 - u, p)
                        run(e, prepare, attend, finish)

        def make_y():
            y_made = sem("y_made")
            with nc.Block() as block:
                @block.scalar
                def _(e):
                    with e.Fori(0, NT // 4) as i:
                        for t in range(4):
                            k = bass.ds(i * 4 + t, 1)
                            e.activation(flat(Y[:, k, :]), flat(X[:, k, :]), ACT.Identity, scale=RSTD[:, k],
                                         bias=NMR[:, k]).then_inc(y_made, 1)

        def window_attention(l):
            c = ExitStack()
            with c:
                def tb(name, shape, dt=F32):
                    return c.enter_context(nc.sbuf_tensor(name + str(l), shape, dt))

                NC = INNER // P
                wqkv, wo = tb("w_qkv", [P, 3 * INNER]), tb("w_wo", [P, NC, DIM])
                xpos, wmask = tb("w_xpos", [P, TPB, 4, FD]), tb("w_mask", [P, TPB, 192])
                scl = tb("w_scl", [P, 4, FD])
                yg, hT = tb("w_yg", [P, 2, DIM]), tb("w_hT", [P, SEQ + 1])
                SQ = tb("w_sq", [P, 2 * INNER])
                SS, RN = tb("w_ss", [P, 2, 2 * FH]), tb("w_rn", [P, 2, 2 * FH])
                QK = tb("w_qk", [P, 2 * INNER])
                RC, RSN = tb("w_rc", [P, 2 * INNER]), tb("w_rs", [P, 2, 2 * INNER])
                V = tb("w_v", [P, 4, INNER])
                QT, KT = tb("w_qT", [P, 2, NC, P]), tb("w_kT", [P, 2, NC, SEQ])
                SBS, PR = tb("w_scores", [P, 4, 2, 192]), tb("w_probs", [P, 4, 2, SEQ])
                PT = tb("w_probsT", [P, 4, 2, TPB, P])
                MN, SM = tb("w_min", [P, 4, 4, 2]), tb("w_sum", [P, 4, 4, 2])
                OT = tb("w_oT", [P, 2, NC, P])
                names = ("w_in zeroed tables yg_ready yT_psum hT_ready qk_psum v_psum sq_ready sum_ready ss_ready ln_ready rn_ready "
                         "v_ready qk_ready rs_ready rc_ready r_ready rT_psum rT_ready s_psum s_moved p_ready ri_ready n_ready pT_psum "
                         "pT_even pT_odd pv_done oT_ready o_psum y_ready").split()
                S = {n: sem(f"w{l}_{n}") for n in names}
                KEYS = [P, 192]
                SBANK, TBANK, OBANK, QBANK, YBANK, VBANK = 0, 2, 4, 5, 6, 7

                STEPS = 4

                def heads(s):
                    return [4 * (s // 2) + 2 * x + s % 2 for x in range(2)]

                def past(e, semaphore, value, alone=False):
                    if not (isinstance(value, int) and value <= 0):
                        (wait_alone if alone else lambda e, s, v: e.wait_ge(s, v))(e, semaphore, value)

                def run(e, step):
                    def steps(T, m):
                        for s in range(STEPS):
                            def pair(lag, f):
                                back, sp = divmod(s - lag, STEPS)
                                if not isinstance(T, int) or 0 <= T + back < NT:
                                    f(T + back, (m + back) % 4, sp)

                            def prep(at, f):
                                if (s - at) % STEPS == 0:
                                    ahead = 2 + (s - at) // STEPS
                                    if not isinstance(T, int) or 0 <= T + ahead < NT:
                                        f(T + ahead, (m + ahead) % 4)
                            step(pair, prep)
                    for T in range(-3, 4):
                        steps(T, T % 4)
                    with e.Fori(1, NT // 4 - 1) as k:
                        for m in range(4):
                            steps(4 * k + m, m)
                    for T in range(NT - 4, NT + 4):
                        steps(T, T % 4)

                with nc.Block() as block:
                    @block.sync
                    def _(e):
                        e.dma_start(wqkv[:, :], d["wqkv"][l]).then_inc(S["w_in"], 16)
                        e.dma_start(wo[:, :, :], d["wo"][l].rearrange("(c p) n -> p c n", p=P)).then_inc(S["w_in"], 16)
                        e.dma_start(xpos[:, :, :, :], d["xpos"]).then_inc(S["w_in"], 16)
                        e.dma_start(wmask[:, :, :], d["wmask"]).then_inc(S["w_in"], 16)
                        for n, name in enumerate(("qs", "ks")):
                            row = d[name][l:l + 1, :]
                            e.dma_start(scl[:, 2 * n, :], row.to_broadcast([P, FD])).then_inc(S["w_in"], 16)
                            for x in range(2):
                                o = (1 - x) * FD // 2
                                e.dma_start(scl[:, 2 * n + 1, x * FD // 2:(x + 1) * FD // 2],
                                            row[:, o:o + FD // 2].to_broadcast([P, FD // 2])).then_inc(S["w_in"], 16)
                        e.wait_ge(S["w_in"], 160)

                    @block.gpsimd
                    def _(e):
                        e.memset(hT[:, 0:1], 0.0).then_inc(S["zeroed"], 1)
                        e.memset(PR[:, :, :, :], 0.0).then_inc(S["zeroed"], 1)
                        e.wait_ge(S["w_in"], 160)
                        for t in range(TPB):
                            e.tensor_tensor(xpos[:, t, :, :], xpos[:, t, :, :], scl[:, :, :], ALU.mult).then_inc(S["tables"], 1)
                        e.wait_ge(S["tables"], TPB)

                        def sines(T, m, n):
                            past(e, S["rT_psum"], 2 * (T - 1))
                            e.wait_ge(S["qk_ready"], 2 * T + n + 1)
                            src = QK[:, n * INNER:(n + 1) * INNER].rearrange("p (h x c) -> p h x c", h=FH, x=2)
                            dst = RSN[:, m % 2, n * INNER:(n + 1) * INNER].rearrange("p (h x c) -> p h x c", h=FH, x=2)
                            tab = xpos[:, m % TPB, 2 * n + 1, :].rearrange("p (x c) -> p x c", x=2)
                            for x in range(2):
                                e.tensor_tensor(dst[:, :, x, :], src[:, :, 1 - x, :],
                                                tab[:, x, :].unsqueeze(1).to_broadcast([P, FH, FD // 2]), ALU.mult)\
                                 .then_inc(S["rs_ready"], 1)

                        def divide(T, m, s):
                            t = m % TPB
                            n, to = KEYS[t], 0 if t == 0 else WIN
                            wait_alone(e, S["ri_ready"], T * STEPS + s + 1)
                            for x in range(2):
                                pr = PR[:, s, x, to:to + n]
                                e.tensor_scalar(pr, pr, SM[:, m, s, x:x + 1], 1.0, ALU.mult, ALU.mult).then_inc(S["n_ready"], 1)

                        def step(pair, prep):
                            prep(4, lambda T, m: sines(T, m, 0))
                            pair(2, divide)
                            prep(4, lambda T, m: sines(T, m, 1))
                        run(e, step)

                    @block.scalar
                    def _(e):
                        e.preload_act_table_set("natural_log_exp_and_others")
                        e.wait_ge(S["zeroed"], 2)

                        def stream(T, m):
                            past(e, S["yT_psum"], T - 1, alone=True)
                            e.activation(yg[:, m % 2, :], flat(Y[:, bass.ds(T, 1), :]), ACT.Copy).then_inc(S["yg_ready"], 1)

                        def squares(T, m):
                            past(e, S["ss_ready"], T)
                            for n in range(2):
                                e.wait_ge(S["qk_psum"], 2 * T + n + 1)
                                e.activation(SQ[:, n * INNER:(n + 1) * INNER], ps[:, QBANK + n, :], ACT.Square).then_inc(S["sq_ready"], 1)

                        def roots(T, m):
                            rn = RN[:, m % 2, :]
                            e.wait_ge(S["ss_ready"], T + 1)
                            e.activation(rn, SS[:, m % 2, :], ACT.Ln, scale=LEN_SCALE ** 2).then_inc(S["ln_ready"], 1)
                            e.wait_ge(S["ln_ready"], T + 1)
                            e.activation(rn, rn, ACT.Exp, scale=-0.5).then_inc(S["rn_ready"], 1)

                        def values(T, m):
                            past(e, S["pv_done"], 2 * (T - 2 - m % 2))
                            e.wait_ge(S["v_psum"], T + 1)
                            e.activation(V[:, m, :], ps[:, VBANK, :], ACT.Copy).then_inc(S["v_ready"], 1)

                        def queries(T, m):
                            e.wait_ge(S["rT_psum"], 2 * T + 1)
                            e.activation(QT[:, m % 2, :, :], ps[:, VBANK, :].rearrange("p (c q) -> p c q", q=P), ACT.Copy)\
                             .then_inc(S["rT_ready"], 1)

                        def keys(T, m):
                            e.wait_ge(S["rT_psum"], 2 * T + 2)
                            e.activation(KT[:, m // 2, :, m % 2 * P:(m % 2 + 1) * P], ps[:, VBANK, :].rearrange("p (c q) -> p c q", q=P),
                                         ACT.Copy).then_inc(S["rT_ready"], 1)

                        def exps(T, m, s):
                            t = m % TPB
                            n, to = KEYS[t], 0 if t == 0 else WIN
                            past(e, S["pT_psum"], T * STEPS + s - 3)
                            for x in range(2):
                                e.wait_ge(S["s_moved"], (T * STEPS + s) * 2 + x + 1)
                                e.activation(PR[:, s, x, to:to + n], SBS[:, s, x, 0:n], ACT.Exp, scale=-1.0,
                                             bias=MN[:, m, s, x:x + 1], accum_out=SM[:, m, s, x:x + 1]).then_inc(S["p_ready"], 1)

                        def evac(T, m, s):
                            if s % 2 == 1:
                                t = m % TPB
                                e.wait_ge(S["pT_psum"], T * STEPS + s + 1)
                                past(e, S["pv_done"], (T - 1) * 2 + s // 2 + 1)
                                e.activation(PT[:, s, :, 0:t + 1, :], ps[:, TBANK + 1, 0:2 * (t + 1) * P]
                                             .rearrange("p (a k q) -> p a k q", a=2, q=P), ACT.Copy).then_inc(S["pT_odd"], 1)

                        def out_copy(T, m, s):
                            if s % 2 == 1:
                                b = s // 2
                                past(e, S["o_psum"], T - 1)
                                e.wait_ge(S["pv_done"], 2 * T + b + 1)
                                e.activation(OT[:, m % 2, 2 * b:2 * b + 2, :],
                                             ps[:, OBANK, 2 * b * P:(2 * b + 2) * P].rearrange("p (c q) -> p c q", q=P), ACT.Copy)\
                                 .then_inc(S["oT_ready"], 1)

                        def step(pair, prep):
                            prep(4, roots)
                            pair(5, evac)
                            pair(7, out_copy)
                            pair(1, exps)
                            prep(5, values)
                            prep(2, squares)
                            prep(-1, stream)
                            prep(6, queries)
                            prep(7, keys)
                        run(e, step)

                    @block.vector
                    def _(e):
                        e.wait_ge(S["tables"], TPB)
                        e.wait_ge(S["zeroed"], 2)

                        def shift(T, m):
                            t, yT = m % TPB, ps[:, YBANK, 0:P]
                            past(e, S["v_psum"], T)
                            e.wait_ge(S["yT_psum"], T + 1)
                            e.tensor_copy(hT[0:64, t * P:(t + 1) * P], yT[0:64, :]).then_inc(S["hT_ready"], 1)
                            e.tensor_copy(hT[64:128, t * P + 1:(t + 1) * P + 1], yT[64:128, :]).then_inc(S["hT_ready"], 1)

                        def lengths(T, m):
                            ss = SS[:, m % 2, :]
                            e.wait_ge(S["sq_ready"], 2 * T + 2)
                            e.tensor_reduce(ss, SQ[:, :].rearrange("p (h c) -> p h c", c=FD), AX.X, ALU.add).then_inc(S["sum_ready"], 1)
                            e.wait_ge(S["sum_ready"], T + 1)
                            e.tensor_scalar(ss, ss, 1e-24, None, ALU.max).then_inc(S["ss_ready"], 1)

                        def norm(T, m):
                            e.wait_ge(S["rn_ready"], T + 1)
                            past(e, S["rs_ready"], 4 * T)
                            for n in range(2):
                                e.tensor_tensor(QK[:, n * INNER:(n + 1) * INNER].rearrange("p (h c) -> p h c", c=FD),
                                                ps[:, QBANK + n, :].rearrange("p (h c) -> p h c", c=FD),
                                                RN[:, m % 2, n * FH:(n + 1) * FH].unsqueeze(2).to_broadcast([P, FH, FD]), ALU.mult)\
                                 .then_inc(S["qk_ready"], 1)

                        def cosines(T, m):
                            for n in range(2):
                                e.wait_ge(S["qk_ready"], 2 * T + n + 1)
                                e.tensor_tensor(RC[:, n * INNER:(n + 1) * INNER].rearrange("p (h c) -> p h c", c=FD),
                                                QK[:, n * INNER:(n + 1) * INNER].rearrange("p (h c) -> p h c", c=FD),
                                                xpos[:, m % TPB, 2 * n, :].unsqueeze(1).to_broadcast([P, FH, FD]), ALU.mult)\
                                 .then_inc(S["rc_ready"], 1)

                        def rotate(T, m):
                            e.wait_ge(S["rc_ready"], 2 * T + 2)
                            e.wait_ge(S["rs_ready"], 4 * T + 4)
                            e.tensor_tensor(RSN[:, m % 2, :], RC[:, :], RSN[:, m % 2, :], ALU.add).then_inc(S["r_ready"], 1)

                        def move(T, m, s):
                            t = m % TPB
                            n = KEYS[t]
                            past(e, S["p_ready"], (T - 1) * STEPS * 2 + 2 * s + 2)
                            wait_alone(e, S["s_psum"], T * STEPS + s + 1)
                            for x in range(2):
                                e.tensor_tensor_reduce(SBS[:, s, x, 0:n], ps[:, SBANK + s % 2, x * 192:x * 192 + n], wmask[:, t, 0:n],
                                                       1.0, 3.0e38, ALU.add, ALU.min, accum_out=MN[:, m, s, x:x + 1])\
                                 .then_inc(S["s_moved"], 1)

                        def invert(T, m, s):
                            e.wait_ge(S["p_ready"], (T * STEPS + s) * 2 + 2)
                            e.reciprocal(SM[:, m, s, :], SM[:, m, s, :]).then_inc(S["ri_ready"], 1)

                        def evac(T, m, s):
                            if s % 2 == 0:
                                t = m % TPB
                                e.wait_ge(S["pT_psum"], T * STEPS + s + 1)
                                past(e, S["pv_done"], (T - 1) * 2 + s // 2 + 1)
                                e.tensor_copy(PT[:, s, :, 0:t + 1, :], ps[:, TBANK, 0:2 * (t + 1) * P]
                                              .rearrange("p (a k q) -> p a k q", a=2, q=P)).then_inc(S["pT_even"], 1)

                        def residual(T, m, s):
                            if s == STEPS - 1:
                                e.wait_ge(S["o_psum"], T + 1)
                                r = bass.ds(T, 1)
                                e.tensor_tensor(flat(Y[:, r, :]), ps[:, QBANK, 0:P], flat(Y[:, r, :]), ALU.add).then_inc(S["y_ready"], 1)

                        def step(pair, prep):
                            pair(11, residual)
                            prep(6, rotate)
                            prep(4, norm)
                            pair(5, evac)
                            pair(1, move)
                            pair(2, invert)
                            prep(1, shift)
                            prep(3, lengths)
                            prep(4, cosines)
                        run(e, step)

                    @block.tensor
                    def _(e):
                        e.wait_ge(S["w_in"], 160)

                        def turn_stream(T, m):
                            e.wait_ge(S["yg_ready"], T + 1)
                            past(e, S["qk_ready"], 2 * T)
                            e.transpose(ps[:, YBANK, 0:P], yg[:, m % 2, :], ident[:, :]).then_inc(S["yT_psum"], 1)

                        def project(T, m, n):
                            at = m % TPB * P
                            return e.matmul(ps[:, QBANK + n, :], hT[:, at:at + P], wqkv[:, n * INNER:(n + 1) * INNER], start=True, stop=True)

                        def project_qk(T, m):
                            e.wait_ge(S["hT_ready"], 2 * T + 2)
                            past(e, S["y_ready"], T - 4)
                            for n in range(2):
                                project(T, m, n).then_inc(S["qk_psum"], 1)

                        def project_v(T, m):
                            past(e, S["rT_ready"], 2 * T)
                            project(T, m, 2).then_inc(S["v_psum"], 1)

                        def turn_rotated(T, m, n):
                            e.wait_ge(S["r_ready"], T + 1)
                            if n == 0:
                                e.wait_ge(S["v_ready"], T + 1)
                            else:
                                e.wait_ge(S["rT_ready"], 2 * T + 1)
                            for c4 in range(NC):
                                ins = e.transpose(ps[:, VBANK, c4 * P:(c4 + 1) * P],
                                                  RSN[:, m % 2, n * INNER + c4 * P:n * INNER + (c4 + 1) * P], ident[:, :])
                            ins.then_inc(S["rT_psum"], 1)

                        def scores(T, m, s):
                            t, a = m % TPB, s % 2
                            if s == 0:
                                e.wait_ge(S["rT_ready"], 2 * T + 2)
                            past(e, S["s_moved"], (T * STEPS + s - 1) * 2)
                            r, n, k0 = slice(64 * a, 64 * a + 64), KEYS[t], 0 if t == 0 else t * P - WIN
                            for x in range(2):
                                ins = e.matmul(ps[:, SBANK + s % 2, x * 192:x * 192 + n], QT[r, m % 2, 2 * (s // 2) + x, :],
                                               KT[r, m // 2, 2 * (s // 2) + x, k0:k0 + n], start=True, stop=True)
                            ins.then_inc(S["s_psum"], 1)

                        def taken(T, s):
                            past(e, S["pT_odd"] if s % 2 else S["pT_even"], 2 * T + s // 2 + 1)

                        def turn(T, m, s):
                            t = m % TPB
                            taken(T + (s - 2) // STEPS, (s - 2) % STEPS)
                            e.wait_ge(S["n_ready"], (T * STEPS + s) * 2 + 2)
                            for x in range(2):
                                for kb in range(t + 1):
                                    at = (x * (t + 1) + kb) * P
                                    ins = e.transpose(ps[:, TBANK + s % 2, at:at + P], PR[:, s, x, kb * P:(kb + 1) * P], ident[:, :])
                            ins.then_inc(S["pT_psum"], 1)

                        def weigh(T, m, s):
                            if s % 2 == 0:
                                return
                            t, b = m % TPB, s // 2
                            past(e, S["oT_ready"], 2 * T + b)
                            taken(T, s - 1)
                            taken(T, s)
                            for x in range(2):
                                for kb in reversed(range(t + 1)):
                                    r = slice(0 if kb == t else WIN, P)
                                    for a in range(2):
                                        h = heads(2 * b + a)[x]
                                        ins = e.matmul(ps[64 * a:64 * a + 64, OBANK, (2 * b + x) * P:(2 * b + x + 1) * P],
                                                       V[r, (m - t + kb) % 4, h * FD:(h + 1) * FD], PT[r, 2 * b + a, x, kb, :],
                                                       start=(kb == t), stop=(kb == 0))
                            ins.then_inc(S["pv_done"], 1)

                        def out_project(T, m, s):
                            if s == STEPS - 1:
                                e.wait_ge(S["oT_ready"], 2 * T + 2)
                                past(e, S["y_ready"], T)
                                if not isinstance(T, int) or T + 5 <= NT:
                                    e.wait_ge(S["qk_ready"], 2 * (T + 5))
                                for c4 in range(NC):
                                    ins = e.matmul(ps[:, QBANK, 0:P], OT[:, m % 2, c4, :], wo[:, c4, :], start=(c4 == 0), stop=(c4 == NC - 1))
                                ins.then_inc(S["o_psum"], 1)

                        def step(pair, prep):
                            pair(10, out_project)
                            prep(1, turn_stream)
                            pair(4, turn)
                            pair(6, weigh)
                            prep(2, project_qk)
                            prep(4, project_v)
                            prep(6, lambda T, m: turn_rotated(T, m, 0))
                            prep(7, lambda T, m: turn_rotated(T, m, 1))
                            pair(0, scores)
                        run(e, step)

        def gelu_ffn(l):
            c = ExitStack()
            with c:
                def tb(name, shape, dt=F32):
                    return c.enter_context(nc.sbuf_tensor(name + str(l), shape, dt))

                G, TG = 2, 2 * TPB
                NG = BATCH // G
                W1, W2 = tb("g_w1", [P, 2 * HID]), tb("g_w2", [114, 3, DIM])
                W1G = tb("g_w1g", [P, 2 * HID])
                lgb = tb("g_lgb", [P, 2])
                B1 = tb("g_b1", [114, 2, 3])
                center, mean = tb("g_center", [P, P]), tb("g_mean", [P, P])
                HN = tb("g_hn", [P, BATCH, SEQ])
                yg, hT = tb("g_yg", [P, TG, DIM]), tb("g_hT", [P, G, SEQ])
                HC, SQ, RT = tb("g_hc", [P, G * SEQ]), tb("g_sq", [P, G * SEQ]), tb("g_rt", [P, G * SEQ])
                GL, HG = tb("g_gl", [114, 3, G * SEQ]), tb("g_hg", [114, 3, G * SEQ])
                names = ("w_in zeroed w1_scaled b1_psum b1_ready yg_ready yT_psum hT_ready hc_psum hc_ready sq_ready var_psum ln_ready rt_ready "
                         "hn_ready a_psum g_psum gl_ready hg_ready o_psum y_ready").split()
                S = {n: sem(f"g{l}_{n}") for n in names}
                with nc.Block() as block:
                    @block.sync
                    def _(e):
                        e.dma_start(W1[:, :], d["w1"][l]).then_inc(S["w_in"], 16)
                        for n, (o, m) in enumerate(HCH):
                            e.dma_start(W2[0:m, n, :], d["w2b"][l, o:o + m, :]).then_inc(S["w_in"], 16)
                            for x in range(2):
                                e.dma_start(B1[0:m, x, n:n + 1], d["b1"][l, x * HID + o:x * HID + o + m].unsqueeze(1)).then_inc(S["w_in"], 16)
                        e.dma_start(W2[113:114, 2, :], d["w2b"][l, HID:HID + 1, :]).then_inc(S["w_in"], 16)
                        e.dma_start(lgb[:, 0:1], d["lg"][l].unsqueeze(1)).then_inc(S["w_in"], 16)
                        e.dma_start(lgb[:, 1:2], d["lb"][l].unsqueeze(1)).then_inc(S["w_in"], 16)
                        e.dma_start(center[:, :], d["center"]).then_inc(S["w_in"], 16)
                        e.wait_ge(S["w_in"], 14 * 16)

                    @block.gpsimd
                    def _(e):
                        e.memset(hT[:, :, 0:1], 0.0).then_inc(S["zeroed"], 1)
                        e.memset(mean[:, :], 1.0 / DIM).then_inc(S["zeroed"], 1)
                        e.memset(HG[:, :, :], 1.0).then_inc(S["zeroed"], 1)

                    @block.scalar
                    def _(e):
                        e.preload_act_table_set("natural_log_exp_and_others")
                        with e.Fori(0, NG) as i:
                            wait_alone(e, S["hn_ready"], i)
                            e.activation(yg[:, :, :], Y[:, bass.ds(i * TG, TG), :], ACT.Copy).then_inc(S["yg_ready"], 1)
                            e.wait_ge(S["hc_ready"], i + 1)
                            e.activation(SQ[:, :], HC[:, :], ACT.Square).then_inc(S["sq_ready"], 1)
                            e.wait_ge(S["var_psum"], i + 1)
                            e.activation(RT[:, :], ps[:, 2, :], ACT.Ln, bias=EPS[:, 0:1]).then_inc(S["ln_ready"], 1)
                            e.wait_ge(S["ln_ready"], i + 1)
                            e.activation(RT[:, :], RT[:, :], ACT.Exp, scale=-0.5).then_inc(S["rt_ready"], 1)
                        e.wait_ge(S["b1_ready"], 3)
                        with e.Fori(0, NG) as i:
                            for n, (o, m) in enumerate(HCH):
                                e.wait_ge(S["g_psum"], i * 3 + n + 1)
                                e.wait_ge(S["hg_ready"], i * 3 + n)
                                e.activation(GL[0:m, n, :], ps[0:m, 4 + n % 2, :], ACT.Gelu, bias=B1[0:m, 1, n:n + 1]).then_inc(S["gl_ready"], 1)

                    @block.vector
                    def _(e):
                        e.wait_ge(S["w_in"], 14 * 16)
                        e.wait_ge(S["zeroed"], 3)
                        e.tensor_scalar(W1G[:, :], W1[:, :], lgb[:, 0:1], None, ALU.mult).then_inc(S["w1_scaled"], 1)
                        e.wait_ge(S["b1_psum"], 1)
                        for n, (o, m) in enumerate(HCH):
                            e.tensor_tensor(B1[0:m, :, n], ps[0:m, 7, n:n + 4:3], B1[0:m, :, n], ALU.add).then_inc(S["b1_ready"], 1)
                        with e.Fori(0, NG) as i:
                            e.wait_ge(S["yT_psum"], i + 1)
                            yT = ps[:, 0, :].rearrange("p (b t) -> p b t", b=G)
                            e.tensor_copy(hT[0:64, :, :], yT[0:64, :, :]).then_inc(S["hT_ready"], 1)
                            e.tensor_copy(hT[64:128, :, 1:SEQ], yT[64:128, :, 0:SEQ - 1]).then_inc(S["hT_ready"], 1)
                            e.wait_ge(S["hc_psum"], i + 1)
                            e.tensor_copy(HC[:, :], ps[:, 1, :]).then_inc(S["hc_ready"], 1)
                            e.wait_ge(S["rt_ready"], i + 1)
                            e.tensor_tensor(HN[:, bass.ds(i * G, G), :].rearrange("p b t -> p (b t)"), HC[:, :], RT[:, :], ALU.mult)\
                             .then_inc(S["hn_ready"], 1)
                        e.wait_ge(S["b1_ready"], 3)
                        with e.Fori(0, NG) as i:
                            for n, (o, m) in enumerate(HCH):
                                e.wait_ge(S["a_psum"], i * 3 + n + 1)
                                e.wait_ge(S["gl_ready"], i * 3 + n + 1)
                                e.wait_ge(S["o_psum"], i)
                                e.scalar_tensor_tensor(HG[0:m, n, :], ps[0:m, 2 + n % 2, :], B1[0:m, 0, n:n + 1], GL[0:m, n, :],
                                                       ALU.add, ALU.mult).then_inc(S["hg_ready"], 1)
                            e.wait_ge(S["o_psum"], i + 1)
                            k = bass.ds(i * TG, TG)
                            e.tensor_tensor(flat(Y[:, k, :]), ps[:, 6, :], flat(Y[:, k, :]), ALU.add).then_inc(S["y_ready"], 1)

                    @block.tensor
                    def _(e):
                        e.wait_ge(S["w_in"], 14 * 16)
                        e.wait_ge(S["zeroed"], 3)
                        for x in range(2):
                            for n, (o, m) in enumerate(HCH):
                                ins = e.matmul(ps[0:m, 7, x * 3 + n:x * 3 + n + 1], W1[:, x * HID + o:x * HID + o + m], lgb[:, 1:2],
                                               start=True, stop=True)
                        ins.then_inc(S["b1_psum"], 1)
                        with e.Fori(0, NG) as i:
                            e.wait_ge(S["yg_ready"], i + 1)
                            for t in range(TG):
                                ins = e.transpose(ps[:, 0, t * P:(t + 1) * P], yg[:, t, :], ident[:, :])
                            ins.then_inc(S["yT_psum"], 1)
                            e.wait_ge(S["hT_ready"], i * 2 + 2)
                            e.matmul(ps[:, 1, :], center[:, :], hT[:, :, :].rearrange("p b t -> p (b t)"), start=True, stop=True)\
                             .then_inc(S["hc_psum"], 1)
                            e.wait_ge(S["sq_ready"], i + 1)
                            e.matmul(ps[:, 2, :], mean[:, :], SQ[:, :], start=True, stop=True).then_inc(S["var_psum"], 1)
                        e.wait_ge(S["w1_scaled"], 1)
                        e.wait_ge(S["hn_ready"], NG)
                        with e.Fori(0, NG) as i:
                            hn = HN[:, bass.ds(i * G, G), :].rearrange("p b t -> p (b t)")
                            e.wait_ge(S["hg_ready"], i * 3)
                            for n, (o, m) in enumerate(HCH):
                                if n >= 2:
                                    e.wait_ge(S["hg_ready"], i * 3 + n - 1)
                                e.matmul(ps[0:m, 4 + n % 2, :], W1G[:, HID + o:HID + o + m], hn, start=True, stop=True).then_inc(S["g_psum"], 1)
                                e.matmul(ps[0:m, 2 + n % 2, :], W1G[:, o:o + m], hn, start=True, stop=True).then_inc(S["a_psum"], 1)
                            e.wait_ge(S["hg_ready"], i * 3 + 3)
                            e.wait_ge(S["y_ready"], i)
                            for t in range(TG):
                                for n, (o, m) in enumerate(HCH):
                                    r = 114
                                    ins = e.matmul(ps[:, 6, t * P:(t + 1) * P], HG[0:r, n, t * P:(t + 1) * P], W2[0:r, n, :],
                                                   start=(n == 0), stop=(n == 2))
                            ins.then_inc(S["o_psum"], 1)

        def state_space():
            c = ExitStack()
            with c:
                def tb(name, shape, dt=F32):
                    return c.enter_context(nc.sbuf_tensor(name, shape, dt))
                G, TG = 2, 2 * TPB
                NG = BATCH // G
                T = G * SEQ
                Win, Wx = tb("m_win", [P, 2 * DIN]), tb("m_wx", [P, CH, DTR + 4 * NST])
                Wdt, Wout = tb("m_wdt", [DTR, DIN]), tb("m_wout", [P, CH, DIM])
                cw, cb, bdt = tb("m_cw", [P, CH, NCONV]), tb("m_cb", [P, CH]), tb("m_bdt", [P, CH])
                A, D = tb("m_A", [P, CH, NST]), tb("m_D", [P, CH])
                U = tb("m_u", [P, CH, BATCH, SEQ])
                ZS = tb("m_z", [P, CH, BATCH, SEQ])
                DT = tb("m_dt", [P, CH, BATCH, SEQ])
                BC = tb("m_bc", [4 * NST, BATCH, SEQ], F32R)
                names = ("w_in xn_ready xT_psum xT_ready in_psum xb_ready z_ready tap conv_ready u_ready dbl_psum dl_ready bc_ready "
                         "dt_psum dt_ready padded bc_low").split()
                S = {n: sem("m_" + n) for n in names}
                c1 = ExitStack()
                with c1:
                    xn, xT = c1.enter_context(nc.sbuf_tensor("m_xn", [P, TG, P], F32)), c1.enter_context(nc.sbuf_tensor("m_xT", [P, T], F32))
                    XB = c1.enter_context(nc.sbuf_tensor("m_xb", [P, CH, G, SEQ + NCONV - 1], F32))
                    CV = c1.enter_context(nc.sbuf_tensor("m_cv", [P, CH, G, SEQ], F32))
                    DL = c1.enter_context(nc.sbuf_tensor("m_dl", [DTR, T], F32))
                    with nc.Block() as block:
                        @block.sync
                        def _(e):
                            e.dma_start(Win[:, :], d["w_in"]).then_inc(S["w_in"], 16)
                            w_x = d["w_x"].rearrange("(c p) n -> p c n", p=P)
                            e.dma_start(Wx[:, :, 0:DTR + 2 * NST], w_x).then_inc(S["w_in"], 16)
                            e.dma_start(Wx[:, :, DTR + 2 * NST:], w_x[:, :, DTR:]).then_inc(S["w_in"], 16)
                            e.dma_start(Wdt[:, :], d["w_dt"]).then_inc(S["w_in"], 16)
                            e.dma_start(Wout[:, :, :], d["w_out"].rearrange("(c p) n -> p c n", p=P)).then_inc(S["w_in"], 16)
                            e.dma_start(cw[:, :, :], d["conv_w"].rearrange("(c p) n -> p c n", p=P)).then_inc(S["w_in"], 16)
                            e.dma_start(A[:, :, :], d["a_log"].rearrange("(c p) n -> p c n", p=P)).then_inc(S["w_in"], 16)
                            for tile, name in ((cb, "conv_b"), (bdt, "b_dt"), (D, "d_skip")):
                                e.dma_start(tile[:, :], d[name]).then_inc(S["w_in"], 16)
                            e.wait_ge(S["w_in"], 160)

                        @block.gpsimd
                        def _(e):
                            e.memset(XB[:, :, :, 0:NCONV - 1], 0.0).then_inc(S["padded"], 1)

                        @block.scalar
                        def _(e):
                            e.preload_act_table_set("silu_and_others")
                            e.wait_ge(S["w_in"], 160)
                            with e.Fori(0, NG) as i:
                                wait_alone(e, S["xT_psum"], i)
                                for t in range(TG):
                                    k = bass.ds(i * TG + t, 1)
                                    e.activation(xn[:, t, :], flat(X[:, k, :]), ACT.Identity, scale=RSTD[:, k], bias=NMR[:, k])\
                                     .then_inc(S["xn_ready"], 1)
                                for ch in range(CH):
                                    e.wait_ge(S["in_psum"], i * 2 * CH + ch + 1)
                                    e.wait_ge(S["conv_ready"], i * CH + ch)
                                    e.activation(XB[:, ch, :, NCONV - 1:], ps[:, 1 + ch, :].rearrange("p (b t) -> p b t", b=G), ACT.Copy)\
                                     .then_inc(S["xb_ready"], 1)
                                for ch in range(CH):
                                    wait_alone(e, S["in_psum"], i * 2 * CH + CH + ch + 1)
                                    e.activation(ZS[:, ch, bass.ds(i * G, G), :].rearrange("p b t -> p (b t)"), ps[:, 3 + ch, :], ACT.Silu)\
                                     .then_inc(S["z_ready"], 1)
                                for ch in range(CH):
                                    wait_alone(e, S["conv_ready"], i * CH + ch + 1)
                                    e.activation(U[:, ch, bass.ds(i * G, G), :].rearrange("p b t -> p (b t)"),
                                                 CV[:, ch, :, :].rearrange("p b t -> p (b t)"), ACT.Silu, bias=cb[:, ch:ch + 1])\
                                     .then_inc(S["u_ready"], 1)
                                e.wait_ge(S["dbl_psum"], i + 1)
                                e.activation(DL[:, :], ps[0:DTR, 5, :], ACT.Copy).then_inc(S["dl_ready"], 1)
                                e.activation(BC[:, bass.ds(i * G, G), :].rearrange("p b t -> p (b t)"), ps[0:4 * NST, 6, :], ACT.Copy)\
                                 .then_inc(S["bc_ready"], 1)
                                for ch in range(CH):
                                    wait_alone(e, S["dt_psum"], i * CH + ch + 1)
                                    e.activation(DT[:, ch, bass.ds(i * G, G), :].rearrange("p b t -> p (b t)"), ps[:, 7 * ch, :],
                                                 ACT.Identity, bias=bdt[:, ch:ch + 1]).then_inc(S["dt_ready"], 1)

                        @block.vector
                        def _(e):
                            e.wait_ge(S["padded"], 1)
                            with e.Fori(0, NG) as i:
                                e.wait_ge(S["xT_psum"], i + 1)
                                e.tensor_copy(xT[:, :], ps[:, 0, :]).then_inc(S["xT_ready"], 1)
                                for ch in range(CH):
                                    e.wait_ge(S["xb_ready"], i * CH + ch + 1)
                                    e.wait_ge(S["u_ready"], i * CH + ch)
                                    last = NCONV - 1
                                    e.tensor_scalar(CV[:, ch, :, :], XB[:, ch, :, last:last + SEQ], cw[:, ch, last:last + 1], None, ALU.mult)\
                                     .then_inc(S["tap"], 1)
                                    for k in range(last):
                                        e.wait_ge(S["tap"], i * CH * last + ch * last + k + 1)
                                        e.scalar_tensor_tensor(CV[:, ch, :, :], XB[:, ch, :, k:k + SEQ], cw[:, ch, k:k + 1], CV[:, ch, :, :],
                                                               ALU.mult, ALU.add).then_inc(S["conv_ready"] if k == last - 1 else S["tap"], 1)
                                e.wait_ge(S["bc_ready"], i + 1)
                                low = BC[2 * NST:4 * NST, bass.ds(i * G, G), :].rearrange("p b t -> p (b t)")
                                e.tensor_tensor(low, ps[2 * NST:4 * NST, 6, :], low, ALU.subtract).then_inc(S["bc_low"], 1)

                        @block.tensor
                        def _(e):
                            e.wait_ge(S["w_in"], 160)
                            with e.Fori(0, NG) as i:
                                e.wait_ge(S["dt_ready"], i * CH)
                                e.wait_ge(S["bc_low"], i)
                                for t in range(TG):
                                    e.wait_ge(S["xn_ready"], i * TG + t + 1)
                                    ins = e.transpose(ps[:, 0, t * P:(t + 1) * P], xn[:, t, :], ident[:, :])
                                ins.then_inc(S["xT_psum"], 1)
                                e.wait_ge(S["xT_ready"], i + 1)
                                for n in range(2 * CH):
                                    e.matmul(ps[:, 1 + n, :], Win[:, n * P:(n + 1) * P], xT[:, :], start=True, stop=True)\
                                     .then_inc(S["in_psum"], 1)
                                e.wait_ge(S["u_ready"], i * CH + CH)
                                for lo, m, bank in ((0, DTR, 5), (DTR, 4 * NST, 6)):
                                    for ch in range(CH):
                                        ins = e.matmul(ps[0:m, bank, :], Wx[:, ch, lo:lo + m],
                                                       U[:, ch, bass.ds(i * G, G), :].rearrange("p b t -> p (b t)"), start=(ch == 0), stop=(ch == CH - 1))
                                ins.then_inc(S["dbl_psum"], 1)
                                e.wait_ge(S["dl_ready"], i + 1)
                                for ch in range(CH):
                                    e.matmul(ps[:, 7 * ch, :], Wdt[:, ch * P:(ch + 1) * P], DL[:, :], start=True, stop=True)\
                                     .then_inc(S["dt_psum"], 1)

                NQ, NH, NBUF = 4, 4, 2
                NPC, NSH = CH * NST // NQ, NST // NQ
                sel_in, sel = tb("m_sel_in", [4 * NST, 2 * NST]), tb("m_sel", [4 * NST, 2 * NST, P], F32R)
                BB = tb("m_bb", [P, NBUF, NQ, SEQ])
                DA = tb("m_da", [P, NBUF, NQ, SEQ])
                DU = tb("m_du", [P, 2, CH, SEQ])
                GT = tb("m_gt", [P, CH, SEQ])
                HB = Y[:, :, :].rearrange("p t d -> p (t d)").rearrange("p (k n s) -> p k n s", n=NQ, s=SEQ)
                SPN = 1024
                names2 = ("sel_in a_ready zeroed abs exp ln dt_ready sel_ready du_ready b_psum c_psum bb_ready da_ready dbx_ready h_ready "
                          "hc_ready hc_used skip_ready g_ready o_psum z_ready stat").split()
                R = {n: sem("s_" + n) for n in names2}
                DTf = DT[:, :, :, :].rearrange("p c b s -> p (c b s)")
                BBANK, CBANK, ABANK = 0, 2, 6

                def past(e, semaphore, value, alone=False):
                    if not (isinstance(value, int) and value <= 0):
                        (wait_alone if alone else lambda e, s, v: e.wait_ge(s, v))(e, semaphore, value)

                def run(e, step):
                    def steps(i, m):
                        for k in range(NPC):
                            def piece(ahead, f):
                                di, kk = divmod(k + ahead, NPC)
                                if not isinstance(i, int) or 0 <= i + di < BATCH:
                                    f(i + di, (m + di) % 2, kk)

                            def sequence(back, f):
                                if not isinstance(i, int) or 0 <= i - back < BATCH:
                                    f(i - back, (m - back) % 2)
                            step(k, piece, sequence)
                    for i in range(-1, 2):
                        steps(i, i % 2)
                    with e.Fori(1, BATCH // 2 - 1) as k:
                        for m in range(2):
                            steps(2 * k + m, m)
                    for i in range(BATCH - 2, BATCH + 2):
                        steps(i, i % 2)

                def rows(tile, ch, i):
                    return tile[:, ch, bass.ds(i, 1), :].rearrange("p a s -> p (a s)")

                with nc.Block() as block:
                    @block.sync
                    def _(e):
                        e.dma_start(sel_in[:, :], d["select"]).then_inc(R["sel_in"], 16)
                        e.wait_ge(R["sel_in"], 16)

                    @block.gpsimd
                    def _(e):
                        e.memset(DA[:, :, :, 0:1], 0.0).then_inc(R["zeroed"], 1)

                        def inputs(i, m, k):
                            q, ch = k // CH, k % CH
                            if q == 0:
                                e.wait_ge(R["du_ready"], i * CH + ch + 1)
                            e.wait_ge(R["bb_ready"], i * NSH + q + 1)
                            past(e, R["hc_used"], i * NPC + k - NH + 1)
                            e.tensor_tensor(HB[:, k % NH, :, :], BB[:, q % NBUF, :, :],
                                            DU[:, m, ch, :].unsqueeze(1).to_broadcast([P, NQ, SEQ]), ALU.mult).then_inc(R["dbx_ready"], 1)

                        def gate(i, m):
                            for ch in range(CH):
                                e.wait_ge(R["skip_ready"], i * CH + ch + 1)
                                e.tensor_tensor(GT[:, ch, :], GT[:, ch, :], rows(ZS, ch, i), ALU.mult).then_inc(R["g_ready"], 1)

                        def step(k, piece, sequence):
                            piece(0, inputs)
                            if k == 6:
                                sequence(1, gate)
                        run(e, step)

                    @block.scalar
                    def _(e):
                        e.preload_act_table_set("natural_log_exp_and_others")
                        e.activation(A[:, :, :], A[:, :, :], ACT.Exp).then_inc(R["a_ready"], 1)
                        e.wait_ge(R["a_ready"], 1)
                        e.activation(A[:, :, :], A[:, :, :], ACT.Copy, scale=-1.0).then_inc(R["a_ready"], 1)

                        def softplus(i, u):
                            tmp = BB[:, u, :, :].rearrange("p n s -> p (n s)")
                            past(e, R["dt_ready"], i - 1, alone=True)
                            e.activation(tmp, DTf[:, bass.ds(i * SPN, SPN)], ACT.Abs).then_inc(R["abs"], 1)
                            e.wait_ge(R["abs"], i + 1)
                            e.activation(tmp, tmp, ACT.Exp, scale=-1.0).then_inc(R["exp"], 1)
                            e.wait_ge(R["exp"], i + 1)
                            e.activation(tmp, tmp, ACT.Ln, bias=1.0).then_inc(R["ln"], 1)
                        for u in range(2):
                            softplus(u, u)
                        with e.Fori(1, CH * BATCH * SEQ // SPN // 2) as i:
                            for u in range(2):
                                softplus(2 * i + u, u)
                        e.wait_ge(R["a_ready"], 2)
                        e.wait_ge(R["zeroed"], 1)
                        e.wait_ge(R["dt_ready"], CH * BATCH * SEQ // SPN)

                        def spread_copy(i, m, k):
                            q = k // CH
                            e.wait_ge(R["b_psum"], i * NSH + q + 1)
                            past(e, R["dbx_ready"], i * NPC + CH * (q - 1))
                            e.activation(BB[:, q % NBUF, :, :].rearrange("p n s -> p (n s)"),
                                         ps[:, BBANK:BBANK + 2, :].rearrange("p a n -> p (a n)"), ACT.Copy).then_inc(R["bb_ready"], 1)

                        def decays(i, m, k):
                            q, ch = k // CH, k % CH
                            past(e, R["h_ready"], i * NPC + k - NBUF + 1, alone=True)
                            for n in range(NQ):
                                e.activation(DA[:, k % NBUF, n, 1:SEQ], DT[:, ch, bass.ds(i, 1), 1:SEQ].rearrange("p a s -> p (a s)"), ACT.Exp,
                                             scale=A[:, ch, q * NQ + n:q * NQ + n + 1]).then_inc(R["da_ready"], 1)

                        def z_copy(i, m):
                            wait_alone(e, R["o_psum"], i + 1)
                            e.activation(flat(Z[:, bass.ds(i * TPB, TPB), :]), ps[:, ABANK + m, 0:SEQ], ACT.Copy).then_inc(R["z_ready"], 1)

                        def step(k, piece, sequence):
                            if k == 0:
                                sequence(2, z_copy)
                            piece(0, decays)
                            if k % CH == 0:
                                piece(CH, spread_copy)
                        run(e, step)

                    @block.vector
                    def _(e):
                        e.wait_ge(R["sel_in"], 16)
                        e.tensor_copy(sel[:, :, :], sel_in[:, :].unsqueeze(2).to_broadcast([4 * NST, 2 * NST, P])).then_inc(R["sel_ready"], 1)
                        with e.Fori(0, CH * BATCH * SEQ // SPN // 2) as i:
                            for u in range(2):
                                e.wait_ge(R["ln"], 2 * i + u + 1)
                                v = DTf[:, bass.ds((2 * i + u) * SPN, SPN)]
                                e.scalar_tensor_tensor(v, v, 0.0, BB[:, u, :, :].rearrange("p n s -> p (n s)"), ALU.max, ALU.add)\
                                 .then_inc(R["dt_ready"], 1)
                        e.wait_ge(R["dt_ready"], CH * BATCH * SEQ // SPN)

                        def dt_u(i, m):
                            past(e, R["dbx_ready"], (i - 1) * NPC)
                            for ch in range(CH):
                                e.tensor_tensor(DU[:, m, ch, :], rows(DT, ch, i), rows(U, ch, i), ALU.mult).then_inc(R["du_ready"], 1)

                        def scan(i, m, k):
                            hb = HB[:, k % NH, :, :].rearrange("p n s -> p (n s)")
                            e.wait_ge(R["dbx_ready"], i * NPC + k + 1)
                            e.wait_ge(R["da_ready"], (i * NPC + k + 1) * NQ)
                            e.tensor_tensor_scan(hb, DA[:, k % NBUF, :, :].rearrange("p n s -> p (n s)"), hb, 0.0, ALU.mult, ALU.add)\
                             .then_inc(R["h_ready"], 1)

                        def outputs(i, m, k):
                            q = k // CH
                            hb, bank = HB[:, k % NH, :, :].rearrange("p n s -> p (n s)"), CBANK + 2 * (q % 2)
                            e.wait_ge(R["h_ready"], i * NPC + k + 1)
                            e.wait_ge(R["c_psum"], i * NSH + q + 1)
                            e.tensor_tensor(hb, ps[:, bank:bank + 2, :].rearrange("p a n -> p (a n)"), hb, ALU.mult).then_inc(R["hc_ready"], 1)

                        def skip(i, m):
                            e.wait_ge(R["hc_used"], (i + 1) * NPC)
                            past(e, R["o_psum"], i)
                            for ch in range(CH):
                                e.scalar_tensor_tensor(GT[:, ch, :], rows(U, ch, i), D[:, ch:ch + 1],
                                                       ps[:, ABANK + m, ch * SEQ:(ch + 1) * SEQ], ALU.mult, ALU.add).then_inc(R["skip_ready"], 1)

                        def stats(i, m):
                            wait_alone(e, R["z_ready"], i + 1)
                            for t in range(TPB):
                                k = bass.ds(i * TPB + t, 1)
                                e.bn_stats(flat(STAT[:, k, :]), flat(Z[:, k, :])).then_inc(R["stat"], 1)

                        def step(k, piece, sequence):
                            piece(0, scan)
                            piece(0, outputs)
                            if k == 1:
                                sequence(2, stats)
                            if k == 2:
                                sequence(1, skip)
                            if k == 3:
                                sequence(-1, dt_u)
                        run(e, step)

                    @block.tensor
                    def _(e):
                        e.wait_ge(R["sel_ready"], 1)

                        def spread(i, q, kind):
                            bank = CBANK + 2 * (q % 2) if kind else BBANK
                            bc = BC[:, bass.ds(i, 1), :].rearrange("p a s -> p (a s)")
                            for n in range(NQ):
                                at = n % 2 * SEQ
                                ins = e.matmul(ps[:, bank + n // 2, at:at + SEQ], sel[:, kind * NST + q * NQ + n, :], bc, start=True, stop=True)
                            return ins

                        def spread_b(i, m, k):
                            q = k // CH
                            past(e, R["bb_ready"], i * NSH + q, alone=True)
                            spread(i, q, 0).then_inc(R["b_psum"], 1)

                        def spread_c(i, m, k):
                            q = k // CH
                            past(e, R["hc_ready"], i * NPC + CH * (q - 1), alone=True)
                            spread(i, q, 1).then_inc(R["c_psum"], 1)

                        def total(i, m, k):
                            ch = k % CH
                            e.wait_ge(R["hc_ready"], i * NPC + k + 1)
                            if k == 0:
                                past(e, R["z_ready"], i - 1)
                            for n in range(NQ):
                                ins = e.matmul(ps[:, ABANK + m, ch * SEQ:(ch + 1) * SEQ], ident[:, :], HB[:, k % NH, n, :],
                                               start=(k == 0 and n == 0), stop=(k == NPC - 1 and n == NQ - 1))
                            ins.then_inc(R["hc_used"], 1)

                        def project(i, m):
                            e.wait_ge(R["g_ready"], i * CH + CH)
                            for t in range(TPB):
                                for ch in range(CH):
                                    ins = e.matmul(ps[:, ABANK + m, t * P:(t + 1) * P], GT[:, ch, t * P:(t + 1) * P], Wout[:, ch, :],
                                                   start=(ch == 0), stop=(ch == CH - 1))
                            ins.then_inc(R["o_psum"], 1)

                        def step(k, piece, sequence):
                            if k % CH == 0:
                                piece(2 * CH, spread_b)
                                piece(CH, spread_c)
                            piece(0, total)
                            if k == 5:
                                sequence(1, project)
                        run(e, step)

        def silu_ffn():
            c = ExitStack()
            with c:
                def tb(name, shape, dt=F32):
                    return c.enter_context(nc.sbuf_tensor(name, shape, dt))
                G, TG = 2, 2 * TPB
                NG, NCH, T = BATCH // G, HID1 // P, G * SEQ
                WI = tb("f_wi", [P, 3, HID1], I32)
                W = tb("f_w", [P, 3, HID1])
                xn, xT = tb("f_xn", [P, TG, P]), tb("f_xT", [P, T])
                SG, H = tb("f_sg", [P, NCH, T]), tb("f_h", [P, NCH, T])
                names = "w_in w_float w_ready xn_ready xT_psum xT_ready g_psum u_psum sg_ready h_ready o_psum z_ready stat".split()
                S = {n: sem("f_" + n) for n in names}
                with nc.Block() as block:
                    @block.sync
                    def _(e):
                        e.dma_start(WI[:, 0, :], d["wg"]).then_inc(S["w_in"], 16)
                        e.dma_start(WI[:, 1, :], d["wu"]).then_inc(S["w_in"], 16)
                        e.dma_start(WI[:, 2, :].rearrange("p (c n) -> p c n", c=NCH), d["wd"].rearrange("(c p) n -> p c n", p=P))\
                         .then_inc(S["w_in"], 16)
                        e.wait_ge(S["w_in"], 48)

                    @block.scalar
                    def _(e):
                        e.preload_act_table_set("silu_and_others")
                        with e.Fori(0, NG) as i:
                            wait_alone(e, S["xT_psum"], i)
                            for t in range(TG):
                                k = bass.ds(i * TG + t, 1)
                                e.activation(xn[:, t, :], flat(X[:, k, :]), ACT.Identity, scale=RSTD[:, k], bias=NMR[:, k])\
                                 .then_inc(S["xn_ready"], 1)
                            for n in range(NCH):
                                e.wait_ge(S["g_psum"], i * NCH + n + 1)
                                e.wait_ge(S["h_ready"], i * NCH + n)
                                e.activation(SG[:, n, :], ps[:, 1 + 2 * (n % 2), :], ACT.Silu).then_inc(S["sg_ready"], 1)
                            wait_alone(e, S["o_psum"], i + 1)
                            e.activation(flat(Z[:, bass.ds(i * TG, TG), :]), ps[:, 5, :], ACT.Copy).then_inc(S["z_ready"], 1)

                    @block.vector
                    def _(e):
                        e.wait_ge(S["w_in"], 48)
                        e.tensor_copy(W[:, :, :].rearrange("p a n -> p (a n)"), WI[:, :, :].rearrange("p a n -> p (a n)")).then_inc(S["w_float"], 1)
                        e.wait_ge(S["w_float"], 1)
                        wf = W[:, :, :].rearrange("p a n -> p (a n)")
                        e.tensor_scalar(wf, wf, float(np.float32(1.0 / 127.0)), None, ALU.mult).then_inc(S["w_ready"], 1)
                        with e.Fori(0, NG) as i:
                            e.wait_ge(S["xT_psum"], i + 1)
                            e.tensor_copy(xT[:, :], ps[:, 0, :]).then_inc(S["xT_ready"], 1)
                            e.wait_ge(S["o_psum"], i)
                            for n in range(NCH):
                                e.wait_ge(S["u_psum"], i * NCH + n + 1)
                                e.wait_ge(S["sg_ready"], i * NCH + n + 1)
                                e.tensor_tensor(H[:, n, :], ps[:, 2 + 2 * (n % 2), :], SG[:, n, :], ALU.mult).then_inc(S["h_ready"], 1)
                            wait_alone(e, S["z_ready"], i + 1)
                            for t in range(TG):
                                k = bass.ds(i * TG + t, 1)
                                e.bn_stats(flat(STAT[:, k, :]), flat(Z[:, k, :])).then_inc(S["stat"], 1)

                    @block.tensor
                    def _(e):
                        e.wait_ge(S["w_ready"], 1)
                        with e.Fori(0, NG) as i:
                            for t in range(TG):
                                e.wait_ge(S["xn_ready"], i * TG + t + 1)
                                ins = e.transpose(ps[:, 0, t * P:(t + 1) * P], xn[:, t, :], ident[:, :])
                            ins.then_inc(S["xT_psum"], 1)
                            e.wait_ge(S["xT_ready"], i + 1)
                            for n in range(NCH):
                                if n >= 2:
                                    e.wait_ge(S["h_ready"], i * NCH + n - 1)
                                else:
                                    e.wait_ge(S["h_ready"], i * NCH)
                                e.matmul(ps[:, 1 + 2 * (n % 2), :], W[:, 0, n * P:(n + 1) * P], xT[:, :], start=True, stop=True).then_inc(S["g_psum"], 1)
                                e.matmul(ps[:, 2 + 2 * (n % 2), :], W[:, 1, n * P:(n + 1) * P], xT[:, :], start=True, stop=True).then_inc(S["u_psum"], 1)
                            e.wait_ge(S["h_ready"], i * NCH + NCH)
                            e.wait_ge(S["z_ready"], i)
                            for t in range(TG):
                                for n in range(NCH):
                                    ins = e.matmul(ps[:, 5, t * P:(t + 1) * P], H[:, n, t * P:(t + 1) * P], W[:, 2, n * P:(n + 1) * P],
                                                   start=(n == 0), stop=(n == NCH - 1))
                            ins.then_inc(S["o_psum"], 1)

        with stage():
            norm_stats("n0", X, True)
            attention()
            norm_stats("n1", Z, False)
            add_normed("n1", Z)
            norm_stats("n2", X, True)
            make_y()
        if stop >= 2:
            for l in range(DEPTH):
                with stage():
                    window_attention(l)
                    gelu_ffn(l)
            with stage():
                norm_stats("n3", Y, True)
                add_normed("n3", Y)
                norm_stats("n4", X, True)
        if stop >= 3:
            with stage():
                state_space()
                norm_stats("n5", Z, False)
                add_normed("n5", Z)
                norm_stats("n6", X, True)
        if stop >= 4:
            with stage():
                silu_ffn()
                norm_stats("n7", Z, False)
                add_normed("n7", Z)
        with stage():
            store()


CONST = ["rope", "dist", "headmask", "onesmask", "xpos", "wmask"]


def kernel(**inputs):
    import numpy as _np
    import concourse.bacc as _bacc
    from concourse import mybir as _mybir
    from concourse.bass_utils import run_bass_kernel_spmd as _run

    v = {k: _np.asarray(a) for k, a in inputs.items()}
    swap = _np.arange(DIM) ^ 1
    feed = {
        "x": v["L0_attn_x"], "wq": v["L0_attn_Wq"].T, "wqr": v["L0_attn_Wq"][swap].T, "wk": v["L0_attn_Wk"].T,
        "wqkv": v["L0_ffn_wqkv"], "qs": v["L0_ffn_q_scale"], "ks": v["L0_ffn_k_scale"], "wo": v["L0_ffn_wo"],
        "lg": v["L0_ffn_ln_g"], "lb": v["L0_ffn_ln_b"], "w1": v["L0_ffn_w1"], "b1": v["L0_ffn_b1"],
        "w2b": _np.concatenate([v["L0_ffn_w2"], v["L0_ffn_b2"][:, None, :]], 1),
        "w_in": v["L1_attn_W_in"], "w_x": v["L1_attn_W_x"], "w_dt": v["L1_attn_W_dt"], "w_out": v["L1_attn_W_out"],
        "conv_w": v["L1_attn_conv_w"], "a_log": v["L1_attn_A_log"],
        "conv_b": v["L1_attn_conv_b"].reshape(CH, P).T, "b_dt": v["L1_attn_b_dt"].reshape(CH, P).T,
        "d_skip": v["L1_attn_D"].reshape(CH, P).T,
        "wg": v["L1_ffn_w_gate"].T, "wu": v["L1_ffn_w_up"].T, "wd": v["L1_ffn_w_down"].T,
        "wkr": v["L0_attn_Wk"][swap].T, "wv": v["L0_attn_Wv"].T, "wo0": v["L0_attn_Wo"].T,
        **shape_constants(),
    }
    nc = _bacc.Bacc("TRN2", target_bir_lowering=False, num_devices=1)
    arrays, aps = {}, {}
    for name, a in feed.items():
        a = _np.ascontiguousarray(a)
        arrays["in_" + name] = a
        aps[name] = nc.dram_tensor("in_" + name, a.shape, _mybir.dt.from_np(a.dtype), kind="ExternalInput").ap()
    y = nc.dram_tensor("out_x", (BATCH, SEQ, DIM), _mybir.dt.float32, kind="ExternalOutput").ap()
    build(nc, aps, y)
    r = _run(nc, [arrays], core_ids=[0])
    return r.results[0]["out_x"]
```

```python
import numpy as np
from contextlib import ExitStack, contextmanager

import concourse.bass as bass
from concourse import mybir

F32 = mybir.dt.float32
I32 = mybir.dt.int32
F32R = mybir.dt.float32r
ALU = mybir.AluOpType
ACT = mybir.ActivationFunctionType
AX = mybir.AxisListType

P = 128
BATCH, SEQ, DIM = 16, 256, 128
TPB = SEQ // P
NT = BATCH * TPB
LN_EPS = 1e-5
LEN_SCALE = 2.0 ** 8

AH, ADK = 16, 8
AG = 4
DEPTH, FH, FD, WIN = 2, 8, 64, 64
INNER = FH * FD
HID = DIM * 4 * 2 // 3
HCH = [(0, 114), (114, 114), (228, 113)]
MASKED = 1e30
DIN, NST, DTR, NCONV = 256, 16, 64, 4
CH = DIN // P
HID1 = 384


def shape_constants():
    f = np.float32
    pos = np.arange(SEQ, dtype=f)
    inv = (1.0 / 10000.0 ** (np.arange(0, ADK, 2, dtype=f) / ADK)).astype(f)
    fr = (pos[:, None] * inv[None, :]).astype(f)
    sin = np.repeat(np.sin(fr), 2, axis=-1).T
    cos = np.repeat(np.cos(fr), 2, axis=-1).T
    sign = np.where(np.arange(ADK) % 2 == 0, -1.0, 1.0)[:, None]
    slopes = 2.0 ** (-8.0 * np.arange(AH, dtype=np.float64) / AH)
    qs = np.repeat(-1.0 / (np.sqrt(ADK) * slopes), ADK)[:, None]
    cosr, sinr = np.tile(cos, (AH, 1)), np.tile(sin * sign, (AH, 1))
    rope = np.stack([cosr * qs, sinr * qs, cosr, sinr], 1).astype(f)
    dist = np.abs(pos[:, None] - pos[None, :]).reshape(TPB, P, SEQ).transpose(1, 0, 2).astype(f)
    copies = np.zeros((P, 4, 4, P), f)
    for s in range(4):
        for r in range(AG):
            for n, stacks in enumerate(((0, 2), (1, 3), (0, 1), (2, 3))):
                for c in stacks:
                    for x in range(ADK):
                        copies[(4 * s + r) * ADK + x, s, n, 32 * r + 8 * c + x] = 1.0

    half = np.arange(0, FD, 2, dtype=f)
    finv = (1.0 / 10000.0 ** (half / FD)).astype(f)
    ff = (pos[:, None] * finv[None, :]).astype(f)
    ff = np.concatenate([ff, ff], -1)
    base = (half + f(0.4 * FD)) / f(1.4 * FD)
    power = (pos - SEQ // 2) / f(WIN // 2)
    sc = (base[None, :] ** power[:, None]).astype(f)
    sc = np.concatenate([sc, sc], -1).astype(np.float64)
    s2 = np.where(np.arange(FD) < FD // 2, -1.0, 1.0)
    c64, s64 = np.cos(ff).astype(np.float64), np.sin(ff).astype(np.float64)
    xpos = np.stack([c64 * sc * -8.0, s64 * sc * s2 * -8.0, c64 / sc, s64 / sc * s2], 1) * LEN_SCALE
    xpos = xpos.reshape(TPB, P, 4, FD).transpose(1, 0, 2, 3).astype(f)
    wmask = np.full((P, TPB, 192), MASKED, f)
    for t in range(TPB):
        first = 0 if t == 0 else t * P - WIN
        i = np.arange(P)[:, None] + t * P
        j = np.arange(192)[None, :] + first
        wmask[:, t] = np.where((j <= i) & (j >= i - WIN), 0.0, MASKED)
    center = (np.eye(P) - 1.0 / P).astype(f)
    select = np.concatenate([np.eye(2 * NST, dtype=f)] * 2)
    return {"center": center, "select": select, "rope": rope, "dist": dist, "copies": copies, "xpos": xpos, "wmask": wmask}


def flat(ap):
    return ap.rearrange("p a c -> p (a c)")


def build(nc, d, out):
    ctx = ExitStack()
    def sb(name, shape, dt=F32):
        return ctx.enter_context(nc.sbuf_tensor(name, shape, dt))

    stage_semaphores = []

    def sem(name):
        stage_semaphores[-1].append(nc.alloc_semaphore(name=name))
        return stage_semaphores[-1][-1]

    @contextmanager
    def stage():
        stage_semaphores.append([])
        yield
        nc.clear_and_free_semaphores(stage_semaphores.pop())
        nc.all_engine_barrier()

    with ctx:
        X = sb("X", [P, NT, DIM])
        Z = sb("Z", [P, NT, DIM])
        Y = sb("Y", [P, NT, DIM])
        STAT = sb("STAT", [P, NT, 6])
        RSTD = sb("RSTD", [P, NT])
        NMR = sb("NMR", [P, NT])
        EPS = sb("EPS", [P, 2])
        ident = sb("ident", [P, P])
        ps = ctx.enter_context(nc.psum_tensor("ps", [P, 8, 512], F32))

        xv = d["x"].rearrange("b (t p) d -> p (b t) d", p=P)
        ov = out.rearrange("b (t p) d -> p (b t) d", p=P)

        passed = {}

        def wait_alone(e, semaphore, value):
            if e.engine not in passed:
                passed[e.engine] = nc.alloc_semaphore(name=f"passed_{len(passed)}")
            e.wait_ge(semaphore, value)
            e.sem_inc(passed[e.engine], 1)

        def past(e, semaphore, value, alone=False):
            if not (isinstance(value, int) and value <= 0):
                (wait_alone if alone else lambda e, s, v: e.wait_ge(s, v))(e, semaphore, value)

        def pipeline(e, step, ahead=0, back=0):
            first, last = 2 * (back // 2 + 1), BATCH - 2 * ((ahead + 1) // 2)

            def one(i, m):
                def at(lag, f):
                    if not isinstance(i, int) or 0 <= i - lag < BATCH:
                        f(i - lag, (m - lag) % 2)
                step(at)
            for i in range(-ahead, first):
                one(i, i % 2)
            with e.Fori(first // 2, last // 2) as k:
                for m in range(2):
                    one(2 * k + m, m)
            for i in range(last, BATCH + back):
                one(i, i % 2)

        small = sb("small", [P, 2 * NT])

        class Norm:
            def __init__(self, tag):
                self.rounds, self.links = {}, {}
                self.linked, self.moments = sem(tag + "_linked"), sem(tag + "_moments")
                self.rstd, self.nmr = sem(tag + "_rstd"), sem(tag + "_nmr")

            def vector(self, e):
                n = self.rounds[e.engine] = self.rounds.get(e.engine, 0) + 1
                sq, tmp, base = small[:, 0:NT], small[:, NT:2 * NT], 4 * (n - 1)
                e.tensor_tensor(tmp, STAT[:, :, 1], STAT[:, :, 4], ALU.subtract).then_inc(self.linked, 1)
                e.tensor_tensor(sq, STAT[:, :, 2], STAT[:, :, 5], ALU.add).then_inc(self.linked, 1)
                e.tensor_tensor(NMR[:, :], STAT[:, :, 1], STAT[:, :, 4], ALU.add).then_inc(self.linked, 1)
                e.wait_ge(self.linked, base + 3)
                e.tensor_tensor(tmp, tmp, tmp, ALU.mult).then_inc(self.linked, 1)
                e.wait_ge(self.linked, base + 4)
                e.scalar_tensor_tensor(tmp, tmp, DIM / 4.0, sq, ALU.mult, ALU.add).then_inc(self.moments, 1)
                e.wait_ge(self.rstd, 2 * n)
                e.scalar_tensor_tensor(NMR[:, :], NMR[:, :], -0.5, RSTD[:, :], ALU.mult, ALU.mult).then_inc(self.nmr, 1)
                e.wait_ge(self.nmr, n)

            def scalar(self, e):
                n = self.rounds[e.engine] = self.rounds.get(e.engine, 0) + 1
                sq, tmp = small[:, 0:NT], small[:, NT:2 * NT]
                e.wait_ge(self.moments, n)
                e.activation(sq, tmp, ACT.Ln, scale=1.0 / DIM, bias=EPS[:, 0:1]).then_inc(self.rstd, 1)
                e.wait_ge(self.rstd, 2 * n - 1)
                e.activation(RSTD[:, :], sq, ACT.Exp, scale=-0.5).then_inc(self.rstd, 1)
                e.wait_ge(self.nmr, n)

        GROUP = 4

        with stage(), nc.Block() as block:
            ident_zero, ident_made, stat_done = sem("ident_zero"), sem("ident_made"), sem("stat_done")
            NLOAD = 4
            x_in = [sem(f"x_in_{c}") for c in range(NLOAD)]
            norm = Norm("x")

            @block.sync
            def _(e):
                for c in range(NLOAD):
                    part = slice(c * NT // NLOAD, (c + 1) * NT // NLOAD)
                    e.dma_start(X[:, part, :], xv[:, part, :]).then_inc(x_in[c], 16)
                for c in range(NLOAD):
                    e.wait_ge(x_in[c], 16)

            @block.vector
            def _(e):
                for c in range(NLOAD):
                    e.wait_ge(x_in[c], 16)
                    with e.Fori(c * NT // NLOAD // GROUP, (c + 1) * NT // NLOAD // GROUP) as i:
                        for t in range(GROUP):
                            k = bass.ds(i * GROUP + t, 1)
                            e.bn_stats(flat(STAT[:, k, :]), flat(X[:, k, :])).then_inc(stat_done, 1)
                e.wait_ge(stat_done, NT)
                norm.vector(e)

            @block.scalar
            def _(e):
                e.preload_act_table_set("natural_log_exp_and_others")
                e.wait_ge(ident_made, 1)
                norm.scalar(e)

            @block.gpsimd
            def _(e):
                e.memset(ident[:, :], 0.0).then_inc(ident_zero, 1)
                e.memset(EPS[:, 0:1], LN_EPS)
                e.memset(EPS[:, 1:2], 1e-24)
                e.wait_ge(ident_zero, 1)
                e.affine_select(out=ident[:, :], in_=ident[:, :], compare_op=ALU.not_equal, fill=1.0,
                                base=0, pattern=[[-1, P]], channel_multiplier=1).then_inc(ident_made, 1)

        def seam(tag, Z, into_y=False, final=False):
            normed, added, stat_done, y_made = sem(tag + "_normed"), sem(tag + "_added"), sem(tag + "_stat"), sem(tag + "_y")
            stored = sem(tag + "_stored")
            norm = Norm(tag)
            with nc.Block() as block:
                @block.vector
                def _(e):
                    norm.vector(e)
                    with e.Fori(0, NT // GROUP) as i:
                        e.wait_ge(normed, i * GROUP + GROUP)
                        k = bass.ds(i * GROUP, GROUP)
                        e.tensor_tensor(X[:, k, :], X[:, k, :], Z[:, k, :], ALU.add).then_inc(added, 1)
                        if not final:
                            wait_alone(e, added, i + 1)
                            for t in range(GROUP):
                                k = bass.ds(i * GROUP + t, 1)
                                e.bn_stats(flat(STAT[:, k, :]), flat(X[:, k, :])).then_inc(stat_done, 1)
                    if final:
                        return
                    e.wait_ge(stat_done, NT)
                    norm.vector(e)
                    if into_y:
                        with e.Fori(0, NT // GROUP) as i:
                            for t in range(1, GROUP):
                                k = bass.ds(i * GROUP + t, 1)
                                e.tensor_scalar(flat(Y[:, k, :]), flat(X[:, k, :]), RSTD[:, k], NMR[:, k], ALU.mult, ALU.add).then_inc(y_made, 1)

                @block.scalar
                def _(e):
                    e.preload_act_table_set("natural_log_exp_and_others")
                    norm.scalar(e)
                    with e.Fori(0, NT // GROUP) as i:
                        for t in range(GROUP):
                            k = bass.ds(i * GROUP + t, 1)
                            e.activation(flat(Z[:, k, :]), flat(Z[:, k, :]), ACT.Identity, scale=RSTD[:, k], bias=NMR[:, k])\
                             .then_inc(normed, 1)
                    if final:
                        return
                    norm.scalar(e)
                    if into_y:
                        with e.Fori(0, NT // GROUP) as i:
                            k = bass.ds(i * GROUP, 1)
                            e.activation(flat(Y[:, k, :]), flat(X[:, k, :]), ACT.Identity, scale=RSTD[:, k], bias=NMR[:, k])\
                             .then_inc(y_made, 1)

                @block.sync
                def _(e):
                    if final:
                        for c in range(NT // GROUP):
                            e.wait_ge(added, c + 1)
                            e.dma_start(ov[:, c * GROUP:(c + 1) * GROUP, :], X[:, c * GROUP:(c + 1) * GROUP, :]).then_inc(stored, 16)
                        e.wait_ge(stored, 16 * NT // GROUP)

        Win, Wx = sb("m_win", [P, 2 * DIN]), sb("m_wx", [P, CH, DTR + 4 * NST])
        Wdt, Wout = sb("m_wdt", [DTR, DIN]), sb("m_wout", [P, CH, DIM])
        cw, cb, bdt = sb("m_cw", [P, CH, NCONV]), sb("m_cb", [P, CH]), sb("m_bdt", [P, CH])
        A, D = sb("m_A", [P, CH, NST]), sb("m_D", [P, CH])
        wide = ctx.enter_context(ExitStack())

        def by_layer(name, shape):
            return [wide.enter_context(nc.sbuf_tensor(name + str(l), shape, F32)) for l in range(DEPTH)]
        HR = max(m for _, m in HCH)
        wqkv_l, wo_l, xpos_l = by_layer("w_qkv", [P, 3 * INNER]), by_layer("w_wo", [P, INNER // P, DIM]), by_layer("w_xpos", [P, TPB, 4, FD])
        scl_l = by_layer("w_scl", [P, 4, FD])
        W1_l, W2_l, B1_l, lgb_l = by_layer("g_w1", [P, 2 * HID]), by_layer("g_w2", [HR, len(HCH), DIM]), by_layer("g_b1", [HR, 2, len(HCH)]), by_layer("g_lgb", [P, 2])
        wmask = wide.enter_context(nc.sbuf_tensor("w_mask", [P, TPB, 192], F32))
        center = wide.enter_context(nc.sbuf_tensor("g_center", [P, P], F32))
        window_in = [nc.alloc_semaphore(name=f"window_in_{l}") for l in range(DEPTH)]
        gelu_in = [nc.alloc_semaphore(name=f"gelu_in_{l}") for l in range(DEPTH)]
        space_in = nc.alloc_semaphore(name="space_in")
        WINDOW_IN, GELU_IN, SPACE_IN = 16 * (4 + 6), 16 * (5 + 3 * len(HCH)), 16 * 10

        def load_weights(e):
            for l in range(DEPTH):
                e.dma_start(wqkv_l[l][:, :], d["wqkv"][l]).then_inc(window_in[l], 16)
                e.dma_start(wo_l[l][:, :, :], d["wo"][l].rearrange("(c p) n -> p c n", p=P)).then_inc(window_in[l], 16)
                e.dma_start(xpos_l[l][:, :, :, :], d["xpos"]).then_inc(window_in[l], 16)
                if l == 0:
                    e.dma_start(wmask[:, :, :], d["wmask"]).then_inc(window_in[l], 16)
                for n, name in enumerate(("qs", "ks")):
                    row = d[name][l:l + 1, :]
                    e.dma_start(scl_l[l][:, 2 * n, :], row.to_broadcast([P, FD])).then_inc(window_in[l], 16)
                    for x in range(2):
                        o = (1 - x) * FD // 2
                        e.dma_start(scl_l[l][:, 2 * n + 1, x * FD // 2:(x + 1) * FD // 2],
                                    row[:, o:o + FD // 2].to_broadcast([P, FD // 2])).then_inc(window_in[l], 16)
                if l == 0:
                    e.dma_start(center[:, :], d["center"]).then_inc(gelu_in[l], 16)
                e.dma_start(W1_l[l][:, :], d["w1"][l]).then_inc(gelu_in[l], 16)
                for n, (o, m) in enumerate(HCH):
                    e.dma_start(W2_l[l][0:m, n, :], d["w2b"][l, o:o + m, :]).then_inc(gelu_in[l], 16)
                    for x in range(2):
                        e.dma_start(B1_l[l][0:m, x, n:n + 1], d["b1"][l, x * HID + o:x * HID + o + m].unsqueeze(1)).then_inc(gelu_in[l], 16)
                e.dma_start(W2_l[l][HR - 1:HR, len(HCH) - 1, :], d["w2b"][l, HID:HID + 1, :]).then_inc(gelu_in[l], 16)
                e.dma_start(lgb_l[l][:, 0:1], d["lg"][l].unsqueeze(1)).then_inc(gelu_in[l], 16)
                e.dma_start(lgb_l[l][:, 1:2], d["lb"][l].unsqueeze(1)).then_inc(gelu_in[l], 16)
            e.dma_start(Win[:, :], d["w_in"]).then_inc(space_in, 16)
            w_x = d["w_x"].rearrange("(c p) n -> p c n", p=P)
            e.dma_start(Wx[:, :, 0:DTR + 2 * NST], w_x).then_inc(space_in, 16)
            e.dma_start(Wx[:, :, DTR + 2 * NST:], w_x[:, :, DTR:]).then_inc(space_in, 16)
            e.dma_start(Wdt[:, :], d["w_dt"]).then_inc(space_in, 16)
            e.dma_start(Wout[:, :, :], d["w_out"].rearrange("(c p) n -> p c n", p=P)).then_inc(space_in, 16)
            e.dma_start(cw[:, :, :], d["conv_w"].rearrange("(c p) n -> p c n", p=P)).then_inc(space_in, 16)
            e.dma_start(A[:, :, :], d["a_log"].rearrange("(c p) n -> p c n", p=P)).then_inc(space_in, 16)
            for tile, name in ((cb, "conv_b"), (bdt, "b_dt"), (D, "d_skip")):
                e.dma_start(tile[:, :], d[name]).then_inc(space_in, 16)

        def attention():
            with ExitStack() as c:
                def tb(name, shape, dt=F32):
                    return c.enter_context(nc.sbuf_tensor(name, shape, dt))
                W = tb("a_w", [P, 6, P])
                rope = tb("a_rope", [P, 4, SEQ])
                dist = tb("a_dist", [P, TPB, SEQ])
                copies_in = tb("a_copies_in", [P, 4, 4, P])
                copies = tb("a_copies", [P, 4, 4, P], F32R)
                xn = tb("a_xn", [P, TPB, P])
                xT = tb("a_xT", [P, SEQ])
                rot = tb("a_rot", [P, 2, 2, SEQ])
                QK = tb("a_qk", [P, 2, SEQ])
                QKh, QKl = tb("a_qk_high", [P, 2, SEQ], F32R), tb("a_qk_low", [P, 2, SEQ], F32R)
                QKX = tb("a_qkx", [P, 2, 4, 2, SEQ], F32R)
                VM = tb("a_VM", [P, 2, TPB, AG, AG, 32])
                NSB, NPT = 4, 8
                SBS = tb("a_scores", [P, NSB, 2, SEQ])
                PR = tb("a_probs", [P, NSB, 2, SEQ])
                PT = tb("a_probsT", [P, NPT, 2, TPB, P])
                MN = tb("a_min", [P, 2, 32])
                SM = tb("a_sum", [P, 2, 32])
                OT = tb("a_oT", [P, SEQ])
                names = ("w_in copies_ready vm_zero xn_ready xT_psum xT_ready q_psum k_psum v_psum rot_q rot_k qk_ready "
                         "high_ready low_ready vm_ready x_psum x_even x_odd s_psum s_moved p_ready pT_psum pT_even pT_odd pv_done "
                         "ri_ready n_ready oT_ready z_psum z_ready stat_done").split()
                S = {n: sem("a_" + n) for n in names}
                pairs = [(qt, r, sp) for qt in range(TPB) for r in range(AG) for sp in range(2)]
                NPAIR, NQUAD = len(pairs), len(pairs) // 2
                SBANK, TBANK, OBANK, XBANK = 0, 2, 4, 6

                def run(e, prepare, attend, finish, prepare_first=False):
                    def both(i, u, before, ahead):
                        for step in range(NPAIR):
                            if ahead is not None and prepare_first:
                                prepare(ahead, 1 - u, step)
                            attend(i, u, step, before)
                            if ahead is not None and not prepare_first:
                                prepare(ahead, 1 - u, step)
                    for step in range(NPAIR):
                        prepare(0, 0, step)
                    both(0, 0, None, 1)
                    both(1, 1, 0, 2)
                    both(2, 0, 1, 3)
                    with e.Fori(1, BATCH // 2 - 1) as k:
                        both(2 * k + 1, 1, 2 * k, 2 * k + 2)
                        both(2 * k + 2, 0, 2 * k + 1, 2 * k + 3)
                    both(BATCH - 1, 1, BATCH - 2, None)
                    for step in range(NPAIR):
                        finish(BATCH - 1, 1, step)

                with nc.Block() as block:
                    @block.sync
                    def _(e):
                        for n, name in enumerate(["wq", "wqr", "wk", "wkr", "wv", "wo0"]):
                            e.dma_start(W[:, n, :], d[name]).then_inc(S["w_in"], 16)
                        e.dma_start(rope[:, :, :], d["rope"]).then_inc(S["w_in"], 16)
                        e.dma_start(dist[:, :, :], d["dist"]).then_inc(S["w_in"], 16)
                        e.dma_start(copies_in[:, :, :, :], d["copies"]).then_inc(S["w_in"], 16)
                        e.wait_ge(S["w_in"], 144)
                        load_weights(e)

                    @block.gpsimd
                    def _(e):
                        e.memset(VM[:, :, :, :, :, :], 0.0).then_inc(S["vm_zero"], 1)

                        def prepare(i, u, step):
                            if step in (4, 5):
                                n = step - 4
                                past(e, S["low_ready"], i)
                                e.wait_ge(S[("rot_q", "rot_k")[n]], i + 1)
                                e.tensor_tensor(QK[:, n, :], rot[:, n, 0, :], rot[:, n, 1, :], ALU.add).then_inc(S["qk_ready"], 1)

                        def divide(i, u, p):
                            wait_alone(e, S["ri_ready"], i * NPAIR + p + 1)
                            for a in range(2):
                                pr = PR[:, p % NSB, a, :]
                                e.tensor_scalar(pr, pr, SM[:, u, 2 * p + a:2 * p + a + 1], 1.0, ALU.mult, ALU.mult).then_inc(S["n_ready"], 1)

                        def finish(i, u, step):
                            if step == 0:
                                divide(i, u, NPAIR - 1)

                        def attend(i, u, p, before):
                            if before is not None:
                                finish(before, 1 - u, p)
                            if p:
                                divide(i, u, p - 1)
                        run(e, prepare, attend, finish)

                    @block.scalar
                    def _(e):
                        e.wait_ge(S["vm_zero"], 1)

                        def prepare(i, u, step):
                            if step == 0:
                                if not (isinstance(i, int) and i == 0):
                                    wait_alone(e, S["xT_psum"], i)
                                for t in range(TPB):
                                    k = bass.ds(i * TPB + t, 1)
                                    e.activation(xn[:, t, :], flat(X[:, k, :]), ACT.Identity, scale=RSTD[:, k], bias=NMR[:, k])\
                                     .then_inc(S["xn_ready"], 1)
                            if step == 5:
                                e.wait_ge(S["v_psum"], i + 1)
                                past(e, S["pv_done"], (i - 1) * NQUAD)
                                for r in range(AG):
                                    e.activation(VM[:, u, :, :, r, r * ADK:(r + 1) * ADK].rearrange("p t g c -> p (t g) c"),
                                                 ps[:, XBANK + 1, 0:SEQ].rearrange("p (tg j c) -> p tg j c", j=AG, c=ADK)[:, :, r, :],
                                                 ACT.Copy).then_inc(S["vm_ready"], 1)
                            if step == 7:
                                e.wait_ge(S["qk_ready"], i * 2 + 2)
                                past(e, S["x_psum"], i * 4)
                                e.activation(QKh[:, :, :], QK[:, :, :], ACT.Copy).then_inc(S["high_ready"], 1)
                            if step in (10, 13):
                                s = (10, 13).index(step) * 2 + 1
                                e.wait_ge(S["x_psum"], i * 4 + s + 1)
                                past(e, S["s_psum"], (i - 1) * NPAIR)
                                e.activation(QKX[:, u, s, :, :].rearrange("p a t -> p (a t)"), ps[:, XBANK + s % 2, :], ACT.Copy)\
                                 .then_inc(S["x_odd"], 1)

                        def evac(i, p):
                            if p % 2:
                                e.wait_ge(S["pT_psum"], i * NPAIR + p + 1)
                                past(e, S["pv_done"], i * NQUAD + p // 2 - NPT // 2 + 1)
                                e.activation(PT[:, p % NPT, :, :, :].rearrange("p a b c -> p (a b c)"), ps[:, TBANK + p % 2, :],
                                             ACT.Copy).then_inc(S["pT_odd"], 1)

                        def finish(i, u, step):
                            if step < 3:
                                evac(i, NPAIR - 3 + step)
                            if step == 10:
                                wait_alone(e, S["z_psum"], i + 1)
                                e.activation(flat(Z[:, bass.ds(i * TPB, TPB), :]), ps[:, OBANK + u, 0:SEQ], ACT.Copy)\
                                 .then_inc(S["z_ready"], 1)

                        def attend(i, u, p, before):
                            past(e, S["pT_psum"], i * NPAIR + p - NSB + 1)
                            for a in range(2):
                                e.wait_ge(S["s_moved"], i * 2 * NPAIR + 2 * p + a + 1)
                                e.activation(PR[:, p % NSB, a, :], SBS[:, p % NSB, a, :], ACT.Exp, scale=-1.0,
                                             bias=MN[:, u, 2 * p + a:2 * p + a + 1],
                                             accum_out=SM[:, u, 2 * p + a:2 * p + a + 1]).then_inc(S["p_ready"], 1)
                            if p >= 3:
                                evac(i, p - 3)
                            if before is not None:
                                finish(before, 1 - u, p)
                        run(e, prepare, attend, finish, prepare_first=True)

                    @block.vector
                    def _(e):
                        e.wait_ge(S["w_in"], 144)
                        e.tensor_copy(copies[:, :, :, :], copies_in[:, :, :, :]).then_inc(S["copies_ready"], 1)

                        def prepare(i, u, step):
                            if step == 1:
                                e.wait_ge(S["xT_psum"], i + 1)
                                past(e, S["v_psum"], i)
                                e.tensor_copy(xT[:, :], ps[:, XBANK, 0:SEQ]).then_inc(S["xT_ready"], 1)
                            for at, n, ready, psum in ((3, 0, "rot_q", "q_psum"), (4, 1, "rot_k", "k_psum")):
                                if step == at:
                                    e.wait_ge(S[psum], i + 1)
                                    past(e, S["qk_ready"], i * 2)
                                    e.tensor_tensor(rot[:, n, :, :].rearrange("p a t -> p (a t)"), ps[:, XBANK + 1 - n, :],
                                                    rope[:, 2 * n:2 * n + 2, :].rearrange("p a t -> p (a t)"), ALU.mult).then_inc(S[ready], 1)
                            if step in (8, 11):
                                s = (8, 11).index(step) * 2
                                e.wait_ge(S["x_psum"], i * 4 + s + 1)
                                past(e, S["s_psum"], (i - 1) * NPAIR)
                                e.tensor_copy(QKX[:, u, s, :, :].rearrange("p a t -> p (a t)"), ps[:, XBANK + s % 2, :])\
                                 .then_inc(S["x_even"], 1)
                            if step == 7:
                                e.wait_ge(S["high_ready"], i + 1)
                                e.tensor_tensor(QKl[:, :, :].rearrange("p a t -> p (a t)"), QK[:, :, :].rearrange("p a t -> p (a t)"),
                                                QKh[:, :, :].bitcast(F32).rearrange("p a t -> p (a t)"), ALU.subtract).then_inc(S["low_ready"], 1)

                        def evac(i, p):
                            if p % 2 == 0:
                                e.wait_ge(S["pT_psum"], i * NPAIR + p + 1)
                                past(e, S["pv_done"], i * NQUAD + p // 2 - NPT // 2 + 1)
                                e.tensor_copy(PT[:, p % NPT, :, :, :].rearrange("p a b c -> p (a b c)"), ps[:, TBANK + p % 2, :])\
                                 .then_inc(S["pT_even"], 1)

                        def invert(i, u, p):
                            e.wait_ge(S["p_ready"], (i * NPAIR + p) * 2 + 2)
                            e.reciprocal(SM[:, u, 2 * p:2 * p + 2], SM[:, u, 2 * p:2 * p + 2]).then_inc(S["ri_ready"], 1)

                        def finish(i, u, step):
                            if step == 0:
                                invert(i, u, NPAIR - 1)
                            if step < 3:
                                evac(i, NPAIR - 3 + step)
                            if step == 7:
                                e.wait_ge(S["pv_done"], (i + 1) * NQUAD)
                                past(e, S["z_psum"], i)
                                e.tensor_copy(OT[:, :], ps[:, OBANK + u, 0:SEQ]).then_inc(S["oT_ready"], 1)
                            if step == 12:
                                wait_alone(e, S["z_ready"], i + 1)
                                for t in range(TPB):
                                    k = bass.ds(i * TPB + t, 1)
                                    e.bn_stats(flat(STAT[:, k, :]), flat(Z[:, k, :])).then_inc(S["stat_done"], 1)

                        def attend(i, u, p, before):
                            qt, r, sp = pairs[p]
                            if not (isinstance(i, int) and i == 0 and p < NSB):
                                wait_alone(e, S["p_ready"], i * 2 * NPAIR + 2 * (p - NSB) + 2)
                            wait_alone(e, S["s_psum"], i * NPAIR + p + 1)
                            for a in range(2):
                                h = 4 * (2 * sp + a) + r
                                e.tensor_tensor_reduce(SBS[:, p % NSB, a, :], ps[:, SBANK + p % 2, a * SEQ:(a + 1) * SEQ], dist[:, qt, :],
                                                       2.0 ** (-8.0 * h / AH), 3.0e38, ALU.add, ALU.min,
                                                       accum_out=MN[:, u, 2 * p + a:2 * p + a + 1]).then_inc(S["s_moved"], 1)
                            if p:
                                invert(i, u, p - 1)
                            if p >= 3:
                                evac(i, p - 3)
                            if before is not None:
                                finish(before, 1 - u, p)
                        run(e, prepare, attend, finish)

                    @block.tensor
                    def _(e):
                        e.wait_ge(S["w_in"], 144)
                        e.wait_ge(S["copies_ready"], 1)

                        def prepare(i, u, step):
                            if step == 0:
                                e.wait_ge(S["xn_ready"], i * TPB + TPB)
                                past(e, S["x_even"], i * 2)
                                for t in range(TPB):
                                    ins = e.transpose(ps[:, XBANK, t * P:(t + 1) * P], xn[:, t, :], ident[:, :])
                                ins.then_inc(S["xT_psum"], 1)
                            if step == 2:
                                e.wait_ge(S["xT_ready"], i + 1)
                                past(e, S["x_odd"], i * 2)
                                for n in range(2):
                                    ins = e.matmul(ps[:, XBANK + 1, n * SEQ:(n + 1) * SEQ], W[:, n, :], xT[:, :], start=True, stop=True)
                                ins.then_inc(S["q_psum"], 1)
                            if step == 3:
                                for n in range(2):
                                    ins = e.matmul(ps[:, XBANK, n * SEQ:(n + 1) * SEQ], W[:, 2 + n, :], xT[:, :], start=True, stop=True)
                                ins.then_inc(S["k_psum"], 1)
                            if step == 4:
                                e.wait_ge(S["rot_q"], i + 1)
                                for t in range(TPB):
                                    ins = e.matmul(ps[:, XBANK + 1, t * P:(t + 1) * P], xT[:, t * P:(t + 1) * P], W[:, 4, :], start=True, stop=True)
                                ins.then_inc(S["v_psum"], 1)
                            if step in (8, 9, 11, 12):
                                s = (8, 9, 11, 12).index(step)
                                if s == 0:
                                    e.wait_ge(S["low_ready"], i + 1)
                                    e.wait_ge(S["rot_k"], i + 1)
                                elif s == 1:
                                    e.wait_ge(S["vm_ready"], i * AG + AG)
                                else:
                                    e.wait_ge(S["x_odd"] if s % 2 else S["x_even"], i * 2 + 1)
                                for n in range(2):
                                    for m, part in enumerate((QKh, QKl)):
                                        ins = e.matmul(ps[:, XBANK + s % 2, n * SEQ:(n + 1) * SEQ], copies[:, s, 2 * n + m, :], part[:, n, :],
                                                       start=(m == 0), stop=(m == 1))
                                ins.then_inc(S["x_psum"], 1)

                        def turn(i, p):
                            if p % 2:
                                past(e, S["pT_odd"], i * NQUAD + p // 2)
                            else:
                                past(e, S["pT_even"], i * NQUAD + p // 2)
                            e.wait_ge(S["n_ready"], i * 2 * NPAIR + 2 * p + 2)
                            for a in range(2):
                                for kb in range(TPB):
                                    at = (a * TPB + kb) * P
                                    ins = e.transpose(ps[:, TBANK + p % 2, at:at + P], PR[:, p % NSB, a, kb * P:(kb + 1) * P], ident[:, :])
                            ins.then_inc(S["pT_psum"], 1)

                        def weigh(i, u, k):
                            qt, r, _ = pairs[2 * k]
                            e.wait_ge(S["pT_even"], i * NQUAD + k + 1)
                            e.wait_ge(S["pT_odd"], i * NQUAD + k + 1)
                            if k == 0:
                                past(e, S["z_ready"], i - 1)
                                e.wait_ge(S["vm_ready"], i * AG + AG)
                            for kb in range(TPB):
                                for g in range(AG):
                                    ins = e.matmul(ps[32 * g:32 * g + 32, OBANK + u, qt * P:(qt + 1) * P], VM[:, u, kb, g, r, :],
                                                   PT[:, (2 * k + g // 2) % NPT, g % 2, kb, :], start=(k == 0 and kb == 0),
                                                   stop=(k == NQUAD - 1 and kb == TPB - 1), skip_group_check=True)
                            ins.then_inc(S["pv_done"], 1)

                        def finish(i, u, step):
                            if step < 3:
                                turn(i, NPAIR - 3 + step)
                            if step in (1, 3, 5):
                                weigh(i, u, NQUAD - 3 + step // 2)
                            if step == 9:
                                e.wait_ge(S["oT_ready"], i + 1)
                                for t in range(TPB):
                                    ins = e.matmul(ps[:, OBANK + u, t * P:(t + 1) * P], OT[:, t * P:(t + 1) * P], W[:, 5, :], start=True, stop=True)
                                ins.then_inc(S["z_psum"], 1)

                        def attend(i, u, p, before):
                            qt, r, sp = pairs[p]
                            if p == 0:
                                e.wait_ge(S["x_even"], i * 2 + 2)
                                e.wait_ge(S["x_odd"], i * 2 + 2)
                            past(e, S["s_moved"], i * 2 * NPAIR + 2 * (p - 2) + 2)
                            rows = slice(32 * r, 32 * r + 32)
                            for a in range(2):
                                ins = e.matmul(ps[:, SBANK + p % 2, a * SEQ:(a + 1) * SEQ], QKX[rows, u, 2 * sp + a, 0, qt * P:(qt + 1) * P],
                                               QKX[rows, u, 2 * sp + a, 1, :], start=True, stop=True)
                            ins.then_inc(S["s_psum"], 1)
                            if p >= 3:
                                turn(i, p - 3)
                            if p >= 7 and p % 2:
                                weigh(i, u, (p - 7) // 2)
                            if before is not None:
                                finish(before, 1 - u, p)
                        run(e, prepare, attend, finish)

        def window_attention(l):
            c = ExitStack()
            with c:
                def tb(name, shape, dt=F32):
                    return c.enter_context(nc.sbuf_tensor(name + str(l), shape, dt))

                NC = INNER // P
                wqkv, wo, xpos, scl = wqkv_l[l], wo_l[l], xpos_l[l], scl_l[l]
                yg, hT = tb("w_yg", [P, 2, DIM]), tb("w_hT", [P, SEQ + 1])
                SQ = tb("w_sq", [P, 2 * INNER])
                SS, RN = tb("w_ss", [P, 2, 2 * FH]), tb("w_rn", [P, 2, 2 * FH])
                QK = tb("w_qk", [P, 2 * INNER])
                RC, RSN = tb("w_rc", [P, 2 * INNER]), tb("w_rs", [P, 2, 2 * INNER])
                V = tb("w_v", [P, 4, INNER])
                QT, KT = tb("w_qT", [P, 2, NC, P]), tb("w_kT", [P, 2, NC, SEQ])
                SBS, PR = tb("w_scores", [P, 4, 2, 192]), tb("w_probs", [P, 4, 2, SEQ])
                PT = tb("w_probsT", [P, 4, 2, TPB, P])
                MN, SM = tb("w_min", [P, 4, 4, 2]), tb("w_sum", [P, 4, 4, 2])
                OT = tb("w_oT", [P, 2, NC, P])
                names = ("zeroed tables yg_ready yT_psum hT_ready qk_psum v_psum sq_ready sum_ready ss_ready ln_ready rn_ready "
                         "v_ready qk_ready rs_ready rc_ready r_ready rT_psum rT_ready s_psum s_moved p_ready ri_ready n_ready pT_psum "
                         "pT_even pT_odd pv_done oT_ready o_psum y_ready").split()
                S = {n: sem(f"w{l}_{n}") for n in names}
                KEYS = [P, 192]
                SBANK, TBANK, OBANK, QBANK, YBANK, VBANK = 0, 2, 4, 5, 6, 7

                STEPS = 4

                def heads(s):
                    return [4 * (s // 2) + 2 * x + s % 2 for x in range(2)]

                def run(e, step):
                    def steps(T, m):
                        for s in range(STEPS):
                            def pair(lag, f):
                                back, sp = divmod(s - lag, STEPS)
                                if not isinstance(T, int) or 0 <= T + back < NT:
                                    f(T + back, (m + back) % 4, sp)

                            def prep(at, f):
                                if (s - at) % STEPS == 0:
                                    ahead = 2 + (s - at) // STEPS
                                    if not isinstance(T, int) or 0 <= T + ahead < NT:
                                        f(T + ahead, (m + ahead) % 4)
                            step(pair, prep)
                    for T in range(-3, 4):
                        steps(T, T % 4)
                    with e.Fori(1, NT // 4 - 1) as k:
                        for m in range(4):
                            steps(4 * k + m, m)
                    for T in range(NT - 4, NT + 4):
                        steps(T, T % 4)

                def wait_window(e):
                    e.wait_ge(window_in[0], WINDOW_IN)
                    if l:
                        e.wait_ge(window_in[l], WINDOW_IN - 16)

                with nc.Block() as block:
                    @block.gpsimd
                    def _(e):
                        e.memset(hT[:, 0:1], 0.0).then_inc(S["zeroed"], 1)
                        e.memset(PR[:, :, :, :], 0.0).then_inc(S["zeroed"], 1)
                        wait_window(e)
                        for t in range(TPB):
                            e.tensor_tensor(xpos[:, t, :, :], xpos[:, t, :, :], scl[:, :, :], ALU.mult).then_inc(S["tables"], 1)
                        e.wait_ge(S["tables"], TPB)

                        def sines(T, m, n):
                            past(e, S["rT_psum"], 2 * (T - 1))
                            e.wait_ge(S["qk_ready"], 2 * T + n + 1)
                            src = QK[:, n * INNER:(n + 1) * INNER].rearrange("p (h x c) -> p h x c", h=FH, x=2)
                            dst = RSN[:, m % 2, n * INNER:(n + 1) * INNER].rearrange("p (h x c) -> p h x c", h=FH, x=2)
                            tab = xpos[:, m % TPB, 2 * n + 1, :].rearrange("p (x c) -> p x c", x=2)
                            for x in range(2):
                                e.tensor_tensor(dst[:, :, x, :], src[:, :, 1 - x, :],
                                                tab[:, x, :].unsqueeze(1).to_broadcast([P, FH, FD // 2]), ALU.mult)\
                                 .then_inc(S["rs_ready"], 1)

                        def divide(T, m, s):
                            t = m % TPB
                            n, to = KEYS[t], 0 if t == 0 else WIN
                            wait_alone(e, S["ri_ready"], T * STEPS + s + 1)
                            for x in range(2):
                                pr = PR[:, s, x, to:to + n]
                                e.tensor_scalar(pr, pr, SM[:, m, s, x:x + 1], 1.0, ALU.mult, ALU.mult).then_inc(S["n_ready"], 1)

                        def step(pair, prep):
                            prep(4, lambda T, m: sines(T, m, 0))
                            pair(2, divide)
                            prep(4, lambda T, m: sines(T, m, 1))
                        run(e, step)

                    @block.scalar
                    def _(e):
                        e.preload_act_table_set("natural_log_exp_and_others")
                        e.wait_ge(S["zeroed"], 2)

                        def stream(T, m):
                            past(e, S["yT_psum"], T - 1, alone=True)
                            e.activation(yg[:, m % 2, :], flat(Y[:, bass.ds(T, 1), :]), ACT.Copy).then_inc(S["yg_ready"], 1)

                        def squares(T, m):
                            past(e, S["ss_ready"], T)
                            for n in range(2):
                                e.wait_ge(S["qk_psum"], 2 * T + n + 1)
                                e.activation(SQ[:, n * INNER:(n + 1) * INNER], ps[:, QBANK + n, :], ACT.Square).then_inc(S["sq_ready"], 1)

                        def roots(T, m):
                            rn = RN[:, m % 2, :]
                            e.wait_ge(S["ss_ready"], T + 1)
                            e.activation(rn, SS[:, m % 2, :], ACT.Ln, scale=LEN_SCALE ** 2).then_inc(S["ln_ready"], 1)
                            e.wait_ge(S["ln_ready"], T + 1)
                            e.activation(rn, rn, ACT.Exp, scale=-0.5).then_inc(S["rn_ready"], 1)

                        def values(T, m):
                            past(e, S["pv_done"], 2 * (T - 2 - m % 2))
                            e.wait_ge(S["v_psum"], T + 1)
                            e.activation(V[:, m, :], ps[:, VBANK, :], ACT.Copy).then_inc(S["v_ready"], 1)

                        def queries(T, m):
                            e.wait_ge(S["rT_psum"], 2 * T + 1)
                            e.activation(QT[:, m % 2, :, :], ps[:, VBANK, :].rearrange("p (c q) -> p c q", q=P), ACT.Copy)\
                             .then_inc(S["rT_ready"], 1)

                        def keys(T, m):
                            e.wait_ge(S["rT_psum"], 2 * T + 2)
                            e.activation(KT[:, m // 2, :, m % 2 * P:(m % 2 + 1) * P], ps[:, VBANK, :].rearrange("p (c q) -> p c q", q=P),
                                         ACT.Copy).then_inc(S["rT_ready"], 1)

                        def exps(T, m, s):
                            t = m % TPB
                            n, to = KEYS[t], 0 if t == 0 else WIN
                            past(e, S["pT_psum"], T * STEPS + s - 3)
                            for x in range(2):
                                e.wait_ge(S["s_moved"], (T * STEPS + s) * 2 + x + 1)
                                e.activation(PR[:, s, x, to:to + n], SBS[:, s, x, 0:n], ACT.Exp, scale=-1.0,
                                             bias=MN[:, m, s, x:x + 1], accum_out=SM[:, m, s, x:x + 1]).then_inc(S["p_ready"], 1)

                        def evac(T, m, s):
                            if s % 2 == 1:
                                t = m % TPB
                                e.wait_ge(S["pT_psum"], T * STEPS + s + 1)
                                past(e, S["pv_done"], (T - 1) * 2 + s // 2 + 1)
                                e.activation(PT[:, s, :, 0:t + 1, :], ps[:, TBANK + 1, 0:2 * (t + 1) * P]
                                             .rearrange("p (a k q) -> p a k q", a=2, q=P), ACT.Copy).then_inc(S["pT_odd"], 1)

                        def out_copy(T, m, s):
                            if s % 2 == 1:
                                b = s // 2
                                past(e, S["o_psum"], T - 1)
                                e.wait_ge(S["pv_done"], 2 * T + b + 1)
                                e.activation(OT[:, m % 2, 2 * b:2 * b + 2, :],
                                             ps[:, OBANK, 2 * b * P:(2 * b + 2) * P].rearrange("p (c q) -> p c q", q=P), ACT.Copy)\
                                 .then_inc(S["oT_ready"], 1)

                        def step(pair, prep):
                            prep(4, roots)
                            pair(5, evac)
                            pair(7, out_copy)
                            pair(1, exps)
                            prep(5, values)
                            prep(2, squares)
                            prep(-1, stream)
                            prep(6, queries)
                            prep(7, keys)
                        run(e, step)

                    @block.vector
                    def _(e):
                        e.wait_ge(S["tables"], TPB)
                        e.wait_ge(S["zeroed"], 2)

                        def shift(T, m):
                            t, yT = m % TPB, ps[:, YBANK, 0:P]
                            past(e, S["v_psum"], T)
                            e.wait_ge(S["yT_psum"], T + 1)
                            e.tensor_copy(hT[0:64, t * P:(t + 1) * P], yT[0:64, :]).then_inc(S["hT_ready"], 1)
                            e.tensor_copy(hT[64:128, t * P + 1:(t + 1) * P + 1], yT[64:128, :]).then_inc(S["hT_ready"], 1)

                        def lengths(T, m):
                            ss = SS[:, m % 2, :]
                            e.wait_ge(S["sq_ready"], 2 * T + 2)
                            e.tensor_reduce(ss, SQ[:, :].rearrange("p (h c) -> p h c", c=FD), AX.X, ALU.add).then_inc(S["sum_ready"], 1)
                            e.wait_ge(S["sum_ready"], T + 1)
                            e.tensor_scalar(ss, ss, 1e-24, None, ALU.max).then_inc(S["ss_ready"], 1)

                        def norm(T, m):
                            e.wait_ge(S["rn_ready"], T + 1)
                            past(e, S["rs_ready"], 4 * T)
                            for n in range(2):
                                e.tensor_tensor(QK[:, n * INNER:(n + 1) * INNER].rearrange("p (h c) -> p h c", c=FD),
                                                ps[:, QBANK + n, :].rearrange("p (h c) -> p h c", c=FD),
                                                RN[:, m % 2, n * FH:(n + 1) * FH].unsqueeze(2).to_broadcast([P, FH, FD]), ALU.mult)\
                                 .then_inc(S["qk_ready"], 1)

                        def cosines(T, m):
                            for n in range(2):
                                e.wait_ge(S["qk_ready"], 2 * T + n + 1)
                                e.tensor_tensor(RC[:, n * INNER:(n + 1) * INNER].rearrange("p (h c) -> p h c", c=FD),
                                                QK[:, n * INNER:(n + 1) * INNER].rearrange("p (h c) -> p h c", c=FD),
                                                xpos[:, m % TPB, 2 * n, :].unsqueeze(1).to_broadcast([P, FH, FD]), ALU.mult)\
                                 .then_inc(S["rc_ready"], 1)

                        def rotate(T, m):
                            e.wait_ge(S["rc_ready"], 2 * T + 2)
                            e.wait_ge(S["rs_ready"], 4 * T + 4)
                            e.tensor_tensor(RSN[:, m % 2, :], RC[:, :], RSN[:, m % 2, :], ALU.add).then_inc(S["r_ready"], 1)

                        def move(T, m, s):
                            t = m % TPB
                            n = KEYS[t]
                            past(e, S["p_ready"], (T - 1) * STEPS * 2 + 2 * s + 2)
                            wait_alone(e, S["s_psum"], T * STEPS + s + 1)
                            for x in range(2):
                                e.tensor_tensor_reduce(SBS[:, s, x, 0:n], ps[:, SBANK + s % 2, x * 192:x * 192 + n], wmask[:, t, 0:n],
                                                       1.0, 3.0e38, ALU.add, ALU.min, accum_out=MN[:, m, s, x:x + 1])\
                                 .then_inc(S["s_moved"], 1)

                        def invert(T, m, s):
                            e.wait_ge(S["p_ready"], (T * STEPS + s) * 2 + 2)
                            e.reciprocal(SM[:, m, s, :], SM[:, m, s, :]).then_inc(S["ri_ready"], 1)

                        def evac(T, m, s):
                            if s % 2 == 0:
                                t = m % TPB
                                e.wait_ge(S["pT_psum"], T * STEPS + s + 1)
                                past(e, S["pv_done"], (T - 1) * 2 + s // 2 + 1)
                                e.tensor_copy(PT[:, s, :, 0:t + 1, :], ps[:, TBANK, 0:2 * (t + 1) * P]
                                              .rearrange("p (a k q) -> p a k q", a=2, q=P)).then_inc(S["pT_even"], 1)

                        def residual(T, m, s):
                            if s == STEPS - 1:
                                e.wait_ge(S["o_psum"], T + 1)
                                r = bass.ds(T, 1)
                                e.tensor_tensor(flat(Y[:, r, :]), ps[:, QBANK, 0:P], flat(Y[:, r, :]), ALU.add).then_inc(S["y_ready"], 1)

                        def step(pair, prep):
                            pair(11, residual)
                            prep(6, rotate)
                            prep(4, norm)
                            pair(5, evac)
                            pair(1, move)
                            pair(2, invert)
                            prep(1, shift)
                            prep(3, lengths)
                            prep(4, cosines)
                        run(e, step)

                    @block.tensor
                    def _(e):
                        wait_window(e)

                        def turn_stream(T, m):
                            e.wait_ge(S["yg_ready"], T + 1)
                            past(e, S["qk_ready"], 2 * T)
                            e.transpose(ps[:, YBANK, 0:P], yg[:, m % 2, :], ident[:, :]).then_inc(S["yT_psum"], 1)

                        def project(T, m, n):
                            at = m % TPB * P
                            return e.matmul(ps[:, QBANK + n, :], hT[:, at:at + P], wqkv[:, n * INNER:(n + 1) * INNER], start=True, stop=True)

                        def project_qk(T, m):
                            e.wait_ge(S["hT_ready"], 2 * T + 2)
                            past(e, S["y_ready"], T - 4)
                            for n in range(2):
                                project(T, m, n).then_inc(S["qk_psum"], 1)

                        def project_v(T, m):
                            past(e, S["rT_ready"], 2 * T)
                            project(T, m, 2).then_inc(S["v_psum"], 1)

                        def turn_rotated(T, m, n):
                            e.wait_ge(S["r_ready"], T + 1)
                            if n == 0:
                                e.wait_ge(S["v_ready"], T + 1)
                            else:
                                e.wait_ge(S["rT_ready"], 2 * T + 1)
                            for c4 in range(NC):
                                ins = e.transpose(ps[:, VBANK, c4 * P:(c4 + 1) * P],
                                                  RSN[:, m % 2, n * INNER + c4 * P:n * INNER + (c4 + 1) * P], ident[:, :])
                            ins.then_inc(S["rT_psum"], 1)

                        def scores(T, m, s):
                            t, a = m % TPB, s % 2
                            if s == 0:
                                e.wait_ge(S["rT_ready"], 2 * T + 2)
                            past(e, S["s_moved"], (T * STEPS + s - 1) * 2)
                            r, n, k0 = slice(64 * a, 64 * a + 64), KEYS[t], 0 if t == 0 else t * P - WIN
                            for x in range(2):
                                ins = e.matmul(ps[:, SBANK + s % 2, x * 192:x * 192 + n], QT[r, m % 2, 2 * (s // 2) + x, :],
                                               KT[r, m // 2, 2 * (s // 2) + x, k0:k0 + n], start=True, stop=True)
                            ins.then_inc(S["s_psum"], 1)

                        def taken(T, s):
                            past(e, S["pT_odd"] if s % 2 else S["pT_even"], 2 * T + s // 2 + 1)

                        def turn(T, m, s):
                            t = m % TPB
                            taken(T + (s - 2) // STEPS, (s - 2) % STEPS)
                            e.wait_ge(S["n_ready"], (T * STEPS + s) * 2 + 2)
                            for x in range(2):
                                for kb in range(t + 1):
                                    at = (x * (t + 1) + kb) * P
                                    ins = e.transpose(ps[:, TBANK + s % 2, at:at + P], PR[:, s, x, kb * P:(kb + 1) * P], ident[:, :])
                            ins.then_inc(S["pT_psum"], 1)

                        def weigh(T, m, s):
                            if s % 2 == 0:
                                return
                            t, b = m % TPB, s // 2
                            past(e, S["oT_ready"], 2 * T + b)
                            taken(T, s - 1)
                            taken(T, s)
                            for x in range(2):
                                for kb in reversed(range(t + 1)):
                                    r = slice(0 if kb == t else WIN, P)
                                    for a in range(2):
                                        h = heads(2 * b + a)[x]
                                        ins = e.matmul(ps[64 * a:64 * a + 64, OBANK, (2 * b + x) * P:(2 * b + x + 1) * P],
                                                       V[r, (m - t + kb) % 4, h * FD:(h + 1) * FD], PT[r, 2 * b + a, x, kb, :],
                                                       start=(kb == t), stop=(kb == 0))
                            ins.then_inc(S["pv_done"], 1)

                        def out_project(T, m, s):
                            if s == STEPS - 1:
                                e.wait_ge(S["oT_ready"], 2 * T + 2)
                                past(e, S["y_ready"], T)
                                if not isinstance(T, int) or T + 5 <= NT:
                                    e.wait_ge(S["qk_ready"], 2 * (T + 5))
                                for c4 in range(NC):
                                    ins = e.matmul(ps[:, QBANK, 0:P], OT[:, m % 2, c4, :], wo[:, c4, :], start=(c4 == 0), stop=(c4 == NC - 1))
                                ins.then_inc(S["o_psum"], 1)

                        def step(pair, prep):
                            pair(10, out_project)
                            prep(1, turn_stream)
                            pair(4, turn)
                            pair(6, weigh)
                            prep(2, project_qk)
                            prep(4, project_v)
                            prep(6, lambda T, m: turn_rotated(T, m, 0))
                            prep(7, lambda T, m: turn_rotated(T, m, 1))
                            pair(0, scores)
                        run(e, step)

        def gelu_ffn(l):
            c = ExitStack()
            with c:
                def tb(name, shape, dt=F32):
                    return c.enter_context(nc.sbuf_tensor(name + str(l), shape, dt))

                NCH = len(HCH)
                W1, W2, B1, lgb = W1_l[l], W2_l[l], B1_l[l], lgb_l[l]
                W1G = tb("g_w1g", [P, 2 * HID])
                mean = tb("g_mean", [P, P])
                HN = tb("g_hn", [P, BATCH, SEQ])
                yg, hT = tb("g_yg", [P, 2, TPB, DIM]), tb("g_hT", [P, 2, SEQ])
                SQ, RT = tb("g_sq", [P, 2, SEQ]), tb("g_rt", [P, 2, SEQ])
                GL, HG = tb("g_gl", [HR, 2, NCH, SEQ]), tb("g_hg", [HR, 2, NCH, SEQ])
                names = ("zeroed w1_scaled b1_psum b1_ready yg_ready yT_psum hT_ready hc_psum hc_ready sq_ready var_psum ln_ready rt_ready "
                         "hn_ready a_psum gl_ready hg_ready g_psum o_psum y_ready stat").split()
                S = {n: sem(f"g{l}_{n}") for n in names}
                TBANK, CBANK, VBANK, BBANK = 0, 2, 4, 7
                GBANK, ABANK, OBANK = 0, 3, 6

                def row(i):
                    return HN[:, bass.ds(i, 1), :].rearrange("p b t -> p (b t)")

                def wait_gelu(e):
                    e.wait_ge(gelu_in[0], GELU_IN)
                    if l:
                        e.wait_ge(gelu_in[l], GELU_IN - 16)

                with nc.Block() as block:
                    @block.gpsimd
                    def _(e):
                        e.memset(hT[:, :, 0:1], 0.0).then_inc(S["zeroed"], 1)
                        e.memset(mean[:, :], 1.0 / DIM).then_inc(S["zeroed"], 1)
                        e.memset(HG[:, :, :, :], 1.0).then_inc(S["zeroed"], 1)

                    @block.scalar
                    def _(e):
                        e.preload_act_table_set("natural_log_exp_and_others")

                        def stream(i, m):
                            past(e, S["yT_psum"], i - 1, alone=True)
                            e.activation(flat(yg[:, m, :, :]), flat(Y[:, bass.ds(i * TPB, TPB), :]), ACT.Copy).then_inc(S["yg_ready"], 1)

                        def squares(i, m):
                            past(e, S["var_psum"], i - 1)
                            wait_alone(e, S["hc_ready"], i + 1)
                            e.activation(SQ[:, m, :], row(i), ACT.Square).then_inc(S["sq_ready"], 1)

                        def roots(i, m):
                            past(e, S["hn_ready"], i - 1)
                            e.wait_ge(S["var_psum"], i + 1)
                            e.activation(RT[:, m, :], ps[:, VBANK + m, 0:SEQ], ACT.Ln, bias=EPS[:, 0:1]).then_inc(S["ln_ready"], 1)
                            e.wait_ge(S["ln_ready"], i + 1)
                            e.activation(RT[:, m, :], RT[:, m, :], ACT.Exp, scale=-0.5).then_inc(S["rt_ready"], 1)

                        def norm(at):
                            at(2, squares)
                            at(-1, stream)
                            at(3, roots)
                        pipeline(e, norm, ahead=1, back=4)
                        e.wait_ge(S["b1_ready"], NCH)

                        def gelus(i, m):
                            past(e, S["hg_ready"], (i - 1) * NCH)
                            for n, (o, r) in enumerate(HCH):
                                e.wait_ge(S["g_psum"], i * NCH + n + 1)
                                e.activation(GL[0:r, m, n, :], ps[0:r, GBANK + n, 0:SEQ], ACT.Gelu, bias=B1[0:r, 1, n:n + 1]).then_inc(S["gl_ready"], 1)
                        pipeline(e, lambda at: at(0, gelus), back=2)

                    @block.vector
                    def _(e):
                        wait_gelu(e)
                        e.wait_ge(S["zeroed"], 3)
                        e.tensor_scalar(W1G[:, :], W1[:, :], lgb[:, 0:1], None, ALU.mult).then_inc(S["w1_scaled"], 1)
                        e.wait_ge(S["b1_psum"], 1)
                        for n, (o, m) in enumerate(HCH):
                            e.tensor_tensor(B1[0:m, :, n], ps[0:m, BBANK, n:n + NCH + 1:NCH], B1[0:m, :, n], ALU.add).then_inc(S["b1_ready"], 1)

                        def shift(i, m):
                            past(e, S["hc_psum"], i - 1)
                            e.wait_ge(S["yT_psum"], i + 1)
                            e.tensor_copy(hT[0:64, m, :], ps[0:64, TBANK + m, 0:SEQ]).then_inc(S["hT_ready"], 1)
                            e.tensor_copy(hT[64:128, m, 1:SEQ], ps[64:128, TBANK + m, 0:SEQ - 1]).then_inc(S["hT_ready"], 1)

                        def centred(i, m):
                            e.wait_ge(S["hc_psum"], i + 1)
                            e.tensor_copy(row(i), ps[:, CBANK + m, 0:SEQ]).then_inc(S["hc_ready"], 1)

                        def normed(i, m):
                            past(e, S["sq_ready"], i + 1)
                            e.wait_ge(S["rt_ready"], i + 1)
                            e.tensor_tensor(row(i), row(i), RT[:, m, :], ALU.mult).then_inc(S["hn_ready"], 1)

                        def norm(at):
                            at(1, shift)
                            at(2, centred)
                            at(4, normed)
                        pipeline(e, norm, back=4)

                        def gate(i, m):
                            past(e, S["o_psum"], i - 1)
                            for n, (o, r) in enumerate(HCH):
                                e.wait_ge(S["a_psum"], i * NCH + n + 1)
                                e.wait_ge(S["gl_ready"], i * NCH + n + 1)
                                e.scalar_tensor_tensor(HG[0:r, m, n, :], ps[0:r, ABANK + n, 0:SEQ], B1[0:r, 0, n:n + 1], GL[0:r, m, n, :],
                                                       ALU.add, ALU.mult).then_inc(S["hg_ready"], 1)

                        def residual(i, m):
                            e.wait_ge(S["o_psum"], i + 1)
                            k = bass.ds(i * TPB, TPB)
                            e.tensor_tensor(flat(Y[:, k, :]), ps[:, OBANK + m, 0:SEQ], flat(Y[:, k, :]), ALU.add).then_inc(S["y_ready"], 1)

                        def stats(i, m):
                            wait_alone(e, S["y_ready"], i + 1)
                            for t in range(TPB):
                                k = bass.ds(i * TPB + t, 1)
                                e.bn_stats(flat(STAT[:, k, :]), flat(Y[:, k, :])).then_inc(S["stat"], 1)

                        def products(at):
                            at(2, residual)
                            at(0, gate)
                            if l == DEPTH - 1:
                                at(3, stats)
                        pipeline(e, products, back=3)

                    @block.tensor
                    def _(e):
                        wait_gelu(e)
                        e.wait_ge(S["zeroed"], 3)
                        for x in range(2):
                            for n, (o, m) in enumerate(HCH):
                                ins = e.matmul(ps[0:m, BBANK, x * NCH + n:x * NCH + n + 1], W1[:, x * HID + o:x * HID + o + m], lgb[:, 1:2],
                                               start=True, stop=True)
                        ins.then_inc(S["b1_psum"], 1)

                        def turn(i, m):
                            past(e, S["hT_ready"], 2 * (i - 1))
                            e.wait_ge(S["yg_ready"], i + 1)
                            for t in range(TPB):
                                ins = e.transpose(ps[:, TBANK + m, t * P:(t + 1) * P], yg[:, m, t, :], ident[:, :])
                            ins.then_inc(S["yT_psum"], 1)

                        def centre(i, m):
                            past(e, S["hc_ready"], i - 1)
                            e.wait_ge(S["hT_ready"], 2 * i + 2)
                            e.matmul(ps[:, CBANK + m, 0:SEQ], center[:, :], hT[:, m, :], start=True, stop=True).then_inc(S["hc_psum"], 1)

                        def variance(i, m):
                            past(e, S["ln_ready"], i - 1)
                            e.wait_ge(S["sq_ready"], i + 1)
                            e.matmul(ps[:, VBANK + m, 0:SEQ], mean[:, :], SQ[:, m, :], start=True, stop=True).then_inc(S["var_psum"], 1)

                        def norm(at):
                            at(0, turn)
                            at(3, variance)
                            at(1, centre)
                        pipeline(e, norm, back=4)
                        e.wait_ge(S["w1_scaled"], 1)
                        e.wait_ge(S["b1_ready"], NCH)
                        e.wait_ge(S["hn_ready"], BATCH)

                        def hidden(i, m):
                            for n, (o, r) in enumerate(HCH):
                                past(e, S["hg_ready"], (i - 1) * NCH + n + 1, alone=True)
                                e.matmul(ps[0:r, GBANK + n, 0:SEQ], W1G[:, HID + o:HID + o + r], row(i), start=True, stop=True).then_inc(S["g_psum"], 1)
                                e.matmul(ps[0:r, ABANK + n, 0:SEQ], W1G[:, o:o + r], row(i), start=True, stop=True).then_inc(S["a_psum"], 1)

                        def project(i, m):
                            past(e, S["y_ready"], i - 1)
                            e.wait_ge(S["hg_ready"], i * NCH + NCH)
                            for t in range(TPB):
                                for n in range(NCH):
                                    ins = e.matmul(ps[:, OBANK + m, t * P:(t + 1) * P], HG[:, m, n, t * P:(t + 1) * P], W2[:, n, :],
                                                   start=(n == 0), stop=(n == NCH - 1))
                            ins.then_inc(S["o_psum"], 1)

                        def products(at):
                            at(0, hidden)
                            at(1, project)
                        pipeline(e, products, back=2)

        def state_space():
            c = ExitStack()
            with c:
                def tb(name, shape, dt=F32):
                    return c.enter_context(nc.sbuf_tensor(name, shape, dt))
                U = tb("m_u", [P, CH, BATCH, SEQ])
                ZS = tb("m_z", [P, CH, BATCH, SEQ])
                DT = tb("m_dt", [P, CH, BATCH, SEQ])
                BC = tb("m_bc", [4 * NST, BATCH, SEQ], F32R)
                names = ("xn_ready xT_psum xT_ready in_psum xb_ready z_ready tap conv_ready u_ready dbl_psum dl_ready bc_ready "
                         "dt_psum dt_ready padded bc_low").split()
                S = {n: sem("m_" + n) for n in names}
                c1 = ExitStack()
                with c1:
                    def t1(name, shape):
                        return c1.enter_context(nc.sbuf_tensor(name, shape, F32))
                    xn, xT = t1("m_xn", [P, 2, TPB, P]), t1("m_xT", [P, 2, SEQ])
                    XB = t1("m_xb", [P, CH, SEQ + NCONV - 1])
                    CV = t1("m_cv", [P, CH, SEQ])
                    DL = t1("m_dl", [DTR, SEQ])
                    last = NCONV - 1
                    TBANK, IBANK, LBANK, BCBANK, DBANK = 0, 1, 5, 6, 7

                    def row(tile, ch, i):
                        return tile[:, ch, bass.ds(i, 1), :].rearrange("p b t -> p (b t)")

                    with nc.Block() as block:
                        @block.gpsimd
                        def _(e):
                            e.memset(XB[:, :, 0:last], 0.0).then_inc(S["padded"], 1)

                        @block.scalar
                        def _(e):
                            e.preload_act_table_set("silu_and_others")
                            e.wait_ge(space_in, SPACE_IN)
                            e.wait_ge(S["padded"], 1)

                            def stream(i, m):
                                past(e, S["xT_psum"], i - 1, alone=True)
                                for t in range(TPB):
                                    k = bass.ds(i * TPB + t, 1)
                                    e.activation(xn[:, m, t, :], flat(X[:, k, :]), ACT.Identity, scale=RSTD[:, k], bias=NMR[:, k])\
                                     .then_inc(S["xn_ready"], 1)

                            def inputs(i, m):
                                for ch in range(CH):
                                    past(e, S["conv_ready"], (i - 1) * CH + ch + 1)
                                    e.wait_ge(S["in_psum"], i * 2 * CH + ch + 1)
                                    e.activation(XB[:, ch, last:], ps[:, IBANK + ch, 0:SEQ], ACT.Copy).then_inc(S["xb_ready"], 1)

                            def gates(i, m):
                                for ch in range(CH):
                                    wait_alone(e, S["in_psum"], i * 2 * CH + CH + ch + 1)
                                    e.activation(row(ZS, ch, i), ps[:, IBANK + CH + ch, 0:SEQ], ACT.Silu).then_inc(S["z_ready"], 1)

                            def activated(i, m):
                                for ch in range(CH):
                                    wait_alone(e, S["conv_ready"], i * CH + ch + 1)
                                    e.activation(row(U, ch, i), CV[:, ch, :], ACT.Silu, bias=cb[:, ch:ch + 1]).then_inc(S["u_ready"], 1)

                            def low_rank(i, m):
                                past(e, S["dt_psum"], i)
                                wait_alone(e, S["dbl_psum"], i + 1)
                                e.activation(DL[:, :], ps[0:DTR, LBANK, 0:SEQ], ACT.Copy).then_inc(S["dl_ready"], 1)
                                e.activation(BC[:, bass.ds(i, 1), :].rearrange("p b t -> p (b t)"), ps[0:4 * NST, BCBANK, 0:SEQ], ACT.Copy)\
                                 .then_inc(S["bc_ready"], 1)

                            def steps_in(i, m):
                                wait_alone(e, S["dt_psum"], i + 1)
                                for ch in range(CH):
                                    e.activation(row(DT, ch, i), ps[:, DBANK, ch * SEQ:(ch + 1) * SEQ], ACT.Identity, bias=bdt[:, ch:ch + 1])\
                                     .then_inc(S["dt_ready"], 1)

                            def step(at):
                                at(0, inputs)
                                at(1, activated)
                                at(0, gates)
                                at(2, low_rank)
                                at(3, steps_in)
                                at(-3, stream)
                            pipeline(e, step, ahead=3, back=3)

                        @block.vector
                        def _(e):
                            e.wait_ge(S["padded"], 1)

                            def turned(i, m):
                                past(e, S["in_psum"], (i - 1) * 2 * CH)
                                e.wait_ge(S["xT_psum"], i + 1)
                                e.tensor_copy(xT[:, m, :], ps[:, TBANK, 0:SEQ]).then_inc(S["xT_ready"], 1)

                            def convolve(i, m):
                                def tap(ch, k):
                                    if k == last:
                                        past(e, S["u_ready"], (i - 1) * CH + ch + 1)
                                        e.wait_ge(S["xb_ready"], i * CH + ch + 1)
                                        e.tensor_scalar(CV[:, ch, :], XB[:, ch, k:k + SEQ], cw[:, ch, k:k + 1], None, ALU.mult)\
                                         .then_inc(S["tap"], 1)
                                    else:
                                        e.wait_ge(S["tap"], (i * last + last - 1 - k) * CH + ch + 1)
                                        e.scalar_tensor_tensor(CV[:, ch, :], XB[:, ch, k:k + SEQ], cw[:, ch, k:k + 1], CV[:, ch, :],
                                                               ALU.mult, ALU.add).then_inc(S["tap"] if k else S["conv_ready"], 1)
                                for k in reversed(range(NCONV)):
                                    for ch in range(CH):
                                        tap(ch, k)

                            def rest(i, m):
                                e.wait_ge(S["bc_ready"], i + 1)
                                low = BC[2 * NST:4 * NST, bass.ds(i, 1), :].rearrange("p b t -> p (b t)")
                                e.tensor_tensor(low, ps[2 * NST:4 * NST, BCBANK, 0:SEQ], low, ALU.subtract).then_inc(S["bc_low"], 1)

                            def step(at):
                                at(-1, turned)
                                at(0, convolve)
                                at(2, rest)
                            pipeline(e, step, ahead=3, back=3)

                        @block.tensor
                        def _(e):
                            e.wait_ge(space_in, SPACE_IN)

                            def turn(i, m):
                                past(e, S["xT_ready"], i)
                                e.wait_ge(S["xn_ready"], (i + 1) * TPB)
                                for t in range(TPB):
                                    ins = e.transpose(ps[:, TBANK, t * P:(t + 1) * P], xn[:, m, t, :], ident[:, :])
                                ins.then_inc(S["xT_psum"], 1)

                            def project(i, m):
                                e.wait_ge(S["xT_ready"], i + 1)
                                for n in range(2 * CH):
                                    ready, at = ("xb_ready", n) if n < CH else ("z_ready", n - CH)
                                    past(e, S[ready], (i - 1) * CH + at + 1)
                                    e.matmul(ps[:, IBANK + n, 0:SEQ], Win[:, n * P:(n + 1) * P], xT[:, m, :], start=True, stop=True)\
                                     .then_inc(S["in_psum"], 1)

                            def low_rank(i, m):
                                past(e, S["bc_low"], i, alone=True)
                                wait_alone(e, S["u_ready"], (i + 1) * CH)
                                for lo, r, bank in ((0, DTR, LBANK), (DTR, 4 * NST, BCBANK)):
                                    for ch in range(CH):
                                        ins = e.matmul(ps[0:r, bank, 0:SEQ], Wx[:, ch, lo:lo + r], row(U, ch, i), start=(ch == 0), stop=(ch == CH - 1))
                                ins.then_inc(S["dbl_psum"], 1)

                            def steps_in(i, m):
                                past(e, S["dt_ready"], i * CH)
                                e.wait_ge(S["dl_ready"], i + 1)
                                for ch in range(CH):
                                    ins = e.matmul(ps[:, DBANK, ch * SEQ:(ch + 1) * SEQ], Wdt[:, ch * P:(ch + 1) * P], DL[:, :], start=True, stop=True)
                                ins.then_inc(S["dt_psum"], 1)

                            def step(at):
                                at(0, project)
                                at(-2, turn)
                                at(2, low_rank)
                                at(3, steps_in)
                            pipeline(e, step, ahead=3, back=3)

                NQ, NH, NBUF = 4, 4, 2
                NPC, NSH = CH * NST // NQ, NST // NQ
                sel_in, sel = tb("m_sel_in", [4 * NST, 2 * NST]), tb("m_sel", [4 * NST, 2 * NST, P], F32R)
                BB = tb("m_bb", [P, NBUF, NQ, SEQ])
                DA = tb("m_da", [P, NBUF, NQ, SEQ])
                DU = tb("m_du", [P, 2, CH, SEQ])
                GT = tb("m_gt", [P, CH, SEQ])
                SP = tb("m_softplus", [P, CH, SEQ])
                HB = Y[:, :, :].rearrange("p t d -> p (t d)").rearrange("p (k n s) -> p k n s", n=NQ, s=SEQ)
                names2 = ("sel_in a_ready zeroed abs exp ln dt_ready sel_ready du_ready b_psum c_psum bb_ready da_ready dbx_ready h_ready "
                          "hc_ready hc_used skip_ready g_ready o_psum z_ready stat").split()
                R = {n: sem("s_" + n) for n in names2}
                BBANK, CBANK, ABANK = 0, 2, 6

                def run(e, step):
                    def steps(i, m):
                        for k in range(NPC):
                            def piece(ahead, f):
                                di, kk = divmod(k + ahead, NPC)
                                if not isinstance(i, int) or 0 <= i + di < BATCH:
                                    f(i + di, (m + di) % 2, kk)

                            def sequence(back, f):
                                if not isinstance(i, int) or 0 <= i - back < BATCH:
                                    f(i - back, (m - back) % 2)
                            step(k, piece, sequence)
                    for i in range(-2, 2):
                        steps(i, i % 2)
                    with e.Fori(1, BATCH // 2 - 1) as k:
                        for m in range(2):
                            steps(2 * k + m, m)
                    for i in range(BATCH - 2, BATCH + 2):
                        steps(i, i % 2)

                def rows(tile, ch, i):
                    return tile[:, ch, bass.ds(i, 1), :].rearrange("p a s -> p (a s)")

                with nc.Block() as block:
                    @block.sync
                    def _(e):
                        e.dma_start(sel_in[:, :], d["select"]).then_inc(R["sel_in"], 16)
                        e.wait_ge(R["sel_in"], 16)

                    @block.gpsimd
                    def _(e):
                        e.memset(DA[:, :, :, 0:1], 0.0).then_inc(R["zeroed"], 1)

                        def inputs(i, m, k):
                            q, ch = k // CH, k % CH
                            if q == 0:
                                e.wait_ge(R["du_ready"], i * CH + ch + 1)
                            e.wait_ge(R["bb_ready"], i * NSH + q + 1)
                            past(e, R["hc_used"], i * NPC + k - NH + 1)
                            e.tensor_tensor(HB[:, k % NH, :, :], BB[:, q % NBUF, :, :],
                                            DU[:, m, ch, :].unsqueeze(1).to_broadcast([P, NQ, SEQ]), ALU.mult).then_inc(R["dbx_ready"], 1)

                        def gate(i, m):
                            for ch in range(CH):
                                e.wait_ge(R["skip_ready"], i * CH + ch + 1)
                                e.tensor_tensor(GT[:, ch, :], GT[:, ch, :], rows(ZS, ch, i), ALU.mult).then_inc(R["g_ready"], 1)

                        def step(k, piece, sequence):
                            piece(0, inputs)
                            if k == 6:
                                sequence(1, gate)
                        run(e, step)

                    @block.scalar
                    def _(e):
                        e.preload_act_table_set("natural_log_exp_and_others")
                        e.activation(A[:, :, :], A[:, :, :], ACT.Exp).then_inc(R["a_ready"], 1)
                        e.wait_ge(R["a_ready"], 1)
                        e.activation(A[:, :, :], A[:, :, :], ACT.Copy, scale=-1.0).then_inc(R["a_ready"], 1)

                        e.wait_ge(R["a_ready"], 2)
                        e.wait_ge(R["zeroed"], 1)

                        def softplus(i, m):
                            past(e, R["dt_ready"], i, alone=True)
                            e.activation(SP[:, :, :], DT[:, :, bass.ds(i, 1), :].rearrange("p c a s -> p c (a s)"), ACT.Abs).then_inc(R["abs"], 1)
                            e.wait_ge(R["abs"], i + 1)
                            e.activation(SP[:, :, :], SP[:, :, :], ACT.Exp, scale=-1.0).then_inc(R["exp"], 1)
                            e.wait_ge(R["exp"], i + 1)
                            e.activation(SP[:, :, :], SP[:, :, :], ACT.Ln, bias=1.0).then_inc(R["ln"], 1)

                        def spread_copy(i, m, k):
                            q = k // CH
                            e.wait_ge(R["b_psum"], i * NSH + q + 1)
                            past(e, R["dbx_ready"], i * NPC + CH * (q - 1))
                            e.activation(BB[:, q % NBUF, :, :].rearrange("p n s -> p (n s)"),
                                         ps[:, BBANK:BBANK + 2, :].rearrange("p a n -> p (a n)"), ACT.Copy).then_inc(R["bb_ready"], 1)

                        def decays(i, m, k):
                            q, ch = k // CH, k % CH
                            if k == 0:
                                wait_alone(e, R["dt_ready"], i + 1)
                            past(e, R["h_ready"], i * NPC + k - NBUF + 1, alone=True)
                            for n in range(NQ):
                                e.activation(DA[:, k % NBUF, n, 1:SEQ], DT[:, ch, bass.ds(i, 1), 1:SEQ].rearrange("p a s -> p (a s)"), ACT.Exp,
                                             scale=A[:, ch, q * NQ + n:q * NQ + n + 1]).then_inc(R["da_ready"], 1)

                        def z_copy(i, m):
                            wait_alone(e, R["o_psum"], i + 1)
                            e.activation(flat(Z[:, bass.ds(i * TPB, TPB), :]), ps[:, ABANK + m, 0:SEQ], ACT.Copy).then_inc(R["z_ready"], 1)

                        def step(k, piece, sequence):
                            if k == 0:
                                sequence(2, z_copy)
                            piece(0, decays)
                            if k == 1:
                                sequence(-2, softplus)
                            if k % CH == 0:
                                piece(CH, spread_copy)
                        run(e, step)

                    @block.vector
                    def _(e):
                        e.wait_ge(R["sel_in"], 16)
                        e.tensor_copy(sel[:, :, :], sel_in[:, :].unsqueeze(2).to_broadcast([4 * NST, 2 * NST, P])).then_inc(R["sel_ready"], 1)

                        def steps_out(i, m):
                            v = DT[:, :, bass.ds(i, 1), :].rearrange("p c a s -> p c (a s)")
                            e.wait_ge(R["ln"], i + 1)
                            e.scalar_tensor_tensor(v, v, 0.0, SP[:, :, :], ALU.max, ALU.add).then_inc(R["dt_ready"], 1)

                        def dt_u(i, m):
                            past(e, R["dbx_ready"], (i - 1) * NPC)
                            e.wait_ge(R["dt_ready"], i + 1)
                            for ch in range(CH):
                                e.tensor_tensor(DU[:, m, ch, :], rows(DT, ch, i), rows(U, ch, i), ALU.mult).then_inc(R["du_ready"], 1)

                        def scan(i, m, k):
                            hb = HB[:, k % NH, :, :].rearrange("p n s -> p (n s)")
                            e.wait_ge(R["dbx_ready"], i * NPC + k + 1)
                            e.wait_ge(R["da_ready"], (i * NPC + k + 1) * NQ)
                            e.tensor_tensor_scan(hb, DA[:, k % NBUF, :, :].rearrange("p n s -> p (n s)"), hb, 0.0, ALU.mult, ALU.add)\
                             .then_inc(R["h_ready"], 1)

                        def outputs(i, m, k):
                            q = k // CH
                            hb, bank = HB[:, k % NH, :, :].rearrange("p n s -> p (n s)"), CBANK + 2 * (q % 2)
                            e.wait_ge(R["h_ready"], i * NPC + k + 1)
                            e.wait_ge(R["c_psum"], i * NSH + q + 1)
                            e.tensor_tensor(hb, ps[:, bank:bank + 2, :].rearrange("p a n -> p (a n)"), hb, ALU.mult).then_inc(R["hc_ready"], 1)

                        def skip(i, m):
                            e.wait_ge(R["hc_used"], (i + 1) * NPC)
                            past(e, R["o_psum"], i)
                            for ch in range(CH):
                                e.scalar_tensor_tensor(GT[:, ch, :], rows(U, ch, i), D[:, ch:ch + 1],
                                                       ps[:, ABANK + m, ch * SEQ:(ch + 1) * SEQ], ALU.mult, ALU.add).then_inc(R["skip_ready"], 1)

                        def stats(i, m):
                            wait_alone(e, R["z_ready"], i + 1)
                            for t in range(TPB):
                                k = bass.ds(i * TPB + t, 1)
                                e.bn_stats(flat(STAT[:, k, :]), flat(Z[:, k, :])).then_inc(R["stat"], 1)

                        def step(k, piece, sequence):
                            piece(0, scan)
                            piece(0, outputs)
                            if k == 1:
                                sequence(2, stats)
                            if k == 2:
                                sequence(1, skip)
                            if k == 3:
                                sequence(-1, dt_u)
                            if k == 4:
                                sequence(-2, steps_out)
                        run(e, step)

                    @block.tensor
                    def _(e):
                        e.wait_ge(R["sel_ready"], 1)

                        def spread(i, q, kind):
                            bank = CBANK + 2 * (q % 2) if kind else BBANK
                            bc = BC[:, bass.ds(i, 1), :].rearrange("p a s -> p (a s)")
                            for n in range(NQ):
                                at = n % 2 * SEQ
                                ins = e.matmul(ps[:, bank + n // 2, at:at + SEQ], sel[:, kind * NST + q * NQ + n, :], bc, start=True, stop=True)
                            return ins

                        def spread_b(i, m, k):
                            q = k // CH
                            past(e, R["bb_ready"], i * NSH + q, alone=True)
                            spread(i, q, 0).then_inc(R["b_psum"], 1)

                        def spread_c(i, m, k):
                            q = k // CH
                            past(e, R["hc_ready"], i * NPC + CH * (q - 1), alone=True)
                            spread(i, q, 1).then_inc(R["c_psum"], 1)

                        def total(i, m, k):
                            ch = k % CH
                            e.wait_ge(R["hc_ready"], i * NPC + k + 1)
                            if k == 0:
                                past(e, R["z_ready"], i - 1)
                            for n in range(NQ):
                                ins = e.matmul(ps[:, ABANK + m, ch * SEQ:(ch + 1) * SEQ], ident[:, :], HB[:, k % NH, n, :],
                                               start=(k == 0 and n == 0), stop=(k == NPC - 1 and n == NQ - 1))
                            ins.then_inc(R["hc_used"], 1)

                        def project(i, m):
                            e.wait_ge(R["g_ready"], i * CH + CH)
                            for t in range(TPB):
                                for ch in range(CH):
                                    ins = e.matmul(ps[:, ABANK + m, t * P:(t + 1) * P], GT[:, ch, t * P:(t + 1) * P], Wout[:, ch, :],
                                                   start=(ch == 0), stop=(ch == CH - 1))
                            ins.then_inc(R["o_psum"], 1)

                        def step(k, piece, sequence):
                            if k % CH == 0:
                                piece(2 * CH, spread_b)
                                piece(CH, spread_c)
                            piece(0, total)
                            if k == 5:
                                sequence(1, project)
                        run(e, step)

        def silu_ffn():
            c = ExitStack()
            with c:
                def tb(name, shape, dt=F32):
                    return c.enter_context(nc.sbuf_tensor(name, shape, dt))
                NCH = HID1 // P
                WI = tb("f_wi", [P, 3, HID1], I32)
                W = tb("f_w", [P, 3, HID1])
                xn, xT = tb("f_xn", [P, 2, TPB, P]), tb("f_xT", [P, 2, SEQ])
                SG, H = tb("f_sg", [P, 2, NCH, SEQ]), tb("f_h", [P, 2, NCH, SEQ])
                names = "w_in w_float w_ready xn_ready xT_psum xT_ready g_psum u_psum sg_ready h_ready o_psum z_ready stat".split()
                S = {n: sem("f_" + n) for n in names}
                GBANK, UBANK, TBANK, OBANK = 0, 3, 6, 7
                with nc.Block() as block:
                    @block.sync
                    def _(e):
                        e.dma_start(WI[:, 0, :], d["wg"]).then_inc(S["w_in"], 16)
                        e.dma_start(WI[:, 1, :], d["wu"]).then_inc(S["w_in"], 16)
                        e.dma_start(WI[:, 2, :].rearrange("p (c n) -> p c n", c=NCH), d["wd"].rearrange("(c p) n -> p c n", p=P))\
                         .then_inc(S["w_in"], 16)
                        e.wait_ge(S["w_in"], 48)

                    @block.scalar
                    def _(e):
                        e.preload_act_table_set("silu_and_others")

                        def stream(i, m):
                            past(e, S["xT_psum"], i - 1, alone=True)
                            for t in range(TPB):
                                k = bass.ds(i * TPB + t, 1)
                                e.activation(xn[:, m, t, :], flat(X[:, k, :]), ACT.Identity, scale=RSTD[:, k], bias=NMR[:, k])\
                                 .then_inc(S["xn_ready"], 1)

                        def silus(i, m):
                            past(e, S["h_ready"], (i - 1) * NCH)
                            for n in range(NCH):
                                e.wait_ge(S["g_psum"], i * NCH + n + 1)
                                e.activation(SG[:, m, n, :], ps[:, GBANK + n, 0:SEQ], ACT.Silu).then_inc(S["sg_ready"], 1)

                        def z_copy(i, m):
                            wait_alone(e, S["o_psum"], i + 1)
                            e.activation(flat(Z[:, bass.ds(i * TPB, TPB), :]), ps[:, OBANK, 0:SEQ], ACT.Copy).then_inc(S["z_ready"], 1)

                        def step(at):
                            at(-2, stream)
                            at(2, z_copy)
                            at(0, silus)
                        pipeline(e, step, ahead=2, back=3)

                    @block.vector
                    def _(e):
                        e.wait_ge(S["w_in"], 48)
                        wf = W[:, :, :].rearrange("p a n -> p (a n)")
                        e.tensor_copy(wf, WI[:, :, :].rearrange("p a n -> p (a n)")).then_inc(S["w_float"], 1)
                        e.wait_ge(S["w_float"], 1)
                        e.tensor_scalar(wf, wf, float(np.float32(1.0 / 127.0)), None, ALU.mult).then_inc(S["w_ready"], 1)

                        def turned(i, m):
                            past(e, S["u_psum"], (i - 1) * NCH)
                            e.wait_ge(S["xT_psum"], i + 1)
                            e.tensor_copy(xT[:, m, :], ps[:, TBANK, 0:SEQ]).then_inc(S["xT_ready"], 1)

                        def gate(i, m):
                            past(e, S["o_psum"], i - 1)
                            for n in range(NCH):
                                e.wait_ge(S["u_psum"], i * NCH + n + 1)
                                e.wait_ge(S["sg_ready"], i * NCH + n + 1)
                                e.tensor_tensor(H[:, m, n, :], ps[:, UBANK + n, 0:SEQ], SG[:, m, n, :], ALU.mult).then_inc(S["h_ready"], 1)

                        def stats(i, m):
                            wait_alone(e, S["z_ready"], i + 1)
                            for t in range(TPB):
                                k = bass.ds(i * TPB + t, 1)
                                e.bn_stats(flat(STAT[:, k, :]), flat(Z[:, k, :])).then_inc(S["stat"], 1)

                        def step(at):
                            at(-1, turned)
                            at(0, gate)
                            at(3, stats)
                        pipeline(e, step, ahead=2, back=3)

                    @block.tensor
                    def _(e):
                        e.wait_ge(S["w_ready"], 1)

                        def turn(i, m):
                            past(e, S["xT_ready"], i)
                            e.wait_ge(S["xn_ready"], (i + 1) * TPB)
                            for t in range(TPB):
                                ins = e.transpose(ps[:, TBANK, t * P:(t + 1) * P], xn[:, m, t, :], ident[:, :])
                            ins.then_inc(S["xT_psum"], 1)

                        def hidden(i, m):
                            e.wait_ge(S["xT_ready"], i + 1)
                            for n in range(NCH):
                                past(e, S["h_ready"], (i - 1) * NCH + n + 1)
                                e.matmul(ps[:, GBANK + n, 0:SEQ], W[:, 0, n * P:(n + 1) * P], xT[:, m, :], start=True, stop=True).then_inc(S["g_psum"], 1)
                                e.matmul(ps[:, UBANK + n, 0:SEQ], W[:, 1, n * P:(n + 1) * P], xT[:, m, :], start=True, stop=True).then_inc(S["u_psum"], 1)

                        def project(i, m):
                            past(e, S["z_ready"], i)
                            e.wait_ge(S["h_ready"], i * NCH + NCH)
                            for t in range(TPB):
                                for n in range(NCH):
                                    ins = e.matmul(ps[:, OBANK, t * P:(t + 1) * P], H[:, m, n, t * P:(t + 1) * P], W[:, 2, n * P:(n + 1) * P],
                                                   start=(n == 0), stop=(n == NCH - 1))
                            ins.then_inc(S["o_psum"], 1)

                        def step(at):
                            at(-1, turn)
                            at(0, hidden)
                            at(1, project)
                        pipeline(e, step, ahead=2, back=3)

        with stage():
            attention()
            seam("n0", Z, into_y=True)
        for l in range(DEPTH):
            with stage():
                window_attention(l)
                gelu_ffn(l)
        wide.close()
        with stage():
            seam("n1", Y)
        with stage():
            state_space()
            seam("n2", Z)
        with stage():
            silu_ffn()
            seam("n3", Z, final=True)


def kernel(**inputs):
    import numpy as _np
    import concourse.bacc as _bacc
    from concourse import mybir as _mybir
    from concourse.bass_utils import run_bass_kernel_spmd as _run

    v = {k: _np.asarray(a) for k, a in inputs.items()}
    swap = _np.arange(DIM) ^ 1
    feed = {
        "x": v["L0_attn_x"], "wq": v["L0_attn_Wq"].T, "wqr": v["L0_attn_Wq"][swap].T, "wk": v["L0_attn_Wk"].T,
        "wqkv": v["L0_ffn_wqkv"], "qs": v["L0_ffn_q_scale"], "ks": v["L0_ffn_k_scale"], "wo": v["L0_ffn_wo"],
        "lg": v["L0_ffn_ln_g"], "lb": v["L0_ffn_ln_b"], "w1": v["L0_ffn_w1"], "b1": v["L0_ffn_b1"],
        "w2b": _np.concatenate([v["L0_ffn_w2"], v["L0_ffn_b2"][:, None, :]], 1),
        "w_in": v["L1_attn_W_in"], "w_x": v["L1_attn_W_x"], "w_dt": v["L1_attn_W_dt"], "w_out": v["L1_attn_W_out"],
        "conv_w": v["L1_attn_conv_w"], "a_log": v["L1_attn_A_log"],
        "conv_b": v["L1_attn_conv_b"].reshape(CH, P).T, "b_dt": v["L1_attn_b_dt"].reshape(CH, P).T,
        "d_skip": v["L1_attn_D"].reshape(CH, P).T,
        "wg": v["L1_ffn_w_gate"].T, "wu": v["L1_ffn_w_up"].T, "wd": v["L1_ffn_w_down"].T,
        "wkr": v["L0_attn_Wk"][swap].T, "wv": v["L0_attn_Wv"].T, "wo0": v["L0_attn_Wo"].T,
        **shape_constants(),
    }
    nc = _bacc.Bacc("TRN2", target_bir_lowering=False, num_devices=1)
    arrays, aps = {}, {}
    for name, a in feed.items():
        a = _np.ascontiguousarray(a)
        arrays["in_" + name] = a
        aps[name] = nc.dram_tensor("in_" + name, a.shape, _mybir.dt.from_np(a.dtype), kind="ExternalInput").ap()
    y = nc.dram_tensor("out_x", (BATCH, SEQ, DIM), _mybir.dt.float32, kind="ExternalOutput").ap()
    build(nc, aps, y)
    r = _run(nc, [arrays], core_ids=[0])
    return r.results[0]["out_x"]
```
